# Optimizing a Trainium2 kernel written in Bass

```python
import numpy as np
import jax
import jax.numpy as jnp

def _softmax(x, axis=-1):
    return jax.nn.softmax(x, axis=axis)

def _gelu(x):
    return jax.nn.gelu(x, approximate=True)

def _silu(x):
    return jax.nn.silu(x)

def _sigmoid(x):
    return jax.nn.sigmoid(x)

def _layernorm(x, axis=-1, eps=1e-05):
    m = jnp.mean(x, axis=axis, keepdims=True)
    v = jnp.var(x, axis=axis, keepdims=True)
    return (x - m) / jnp.sqrt(v + eps)

def _scatter_add(tgt, idx, src, axis=0):
    return tgt.at[idx].add(src)

def _segment_sum(src, seg, n):
    return jax.ops.segment_sum(src, seg, n)
kernel_name = 'mk_gnn_preln_d4_gnn_r64_6c6e98'

def setup_inputs(seed: int=0):
    np.random.seed(seed)
    _w = jnp.asarray

    def _rec_inputs():
        import jax
        import jax.numpy as jnp
        _gk = jax.random.key(seed)
        x = -0.0005121 + 1.001 * jax.random.normal(jax.random.fold_in(_gk, 1), (100000, 32), jnp.float32)
        src = jax.random.randint(jax.random.fold_in(_gk, 2), (50000,), 0, 100000, jnp.int32)
        dst = jax.random.randint(jax.random.fold_in(_gk, 3), (50000,), 0, 100000, jnp.int32)
        _o = jnp.argsort(dst, stable=True)
        src = src[_o]
        dst = dst[_o]
        edge_attr_3 = jax.random.uniform(jax.random.fold_in(_gk, 11), (50000, 3), jnp.float32, 0.0, 1)
        edge_attr_8 = -0.00010739 + 0.99994 * jax.random.normal(jax.random.fold_in(_gk, 12), (50000, 8), jnp.float32)
        return (x, src, dst, edge_attr_3, edge_attr_8)
    x, src, dst, edge_attr_3, edge_attr_8 = _rec_inputs()

    def _L0_gnn_setup():
        import jax, jax.numpy as jnp
        import numpy as np
        N_NODES = 100000
        N_EDGES = 25000
        D = 32
        H = 2 * D
        EPS = 1e-07

        def _edge_softmax(logits, dst, num_nodes):
            m = jax.ops.segment_max(logits, dst, num_segments=num_nodes)
            e = jnp.exp(logits - m[dst])
            s = jax.ops.segment_sum(e, dst, num_segments=num_nodes)
            return e / s[dst]
        key = jax.random.key(seed)
        ks = jax.random.split(key, 6)
        x = jax.random.normal(ks[0], (N_NODES, D), dtype=jnp.float32)
        edge_index = jax.random.randint(ks[1], (2, N_EDGES), 0, N_NODES, dtype=jnp.int64)
        beta = jnp.ones((1,), dtype=jnp.float32)
        W1 = jax.random.normal(ks[2], (D, H), dtype=jnp.float32) * (1.0 / np.sqrt(D))
        b1 = jnp.zeros((H,), dtype=jnp.float32)
        W2 = jax.random.normal(ks[3], (H, D), dtype=jnp.float32) * (1.0 / np.sqrt(H))
        b2 = jnp.zeros((D,), dtype=jnp.float32)
        return {'x': x, 'edge_index': edge_index, 'beta': beta, 'W1': W1, 'b1': b1, 'W2': W2, 'b2': b2}
    _L0_gnn_all = _L0_gnn_setup()
    _L0_gnn_in = {k: v for k, v in _L0_gnn_all.items() if k in ('beta', 'W1', 'b1', 'W2', 'b2')}
    del _L0_gnn_all

    def _L1_gnn_setup():
        import jax, jax.numpy as jnp
        import numpy as np
        N_NODES = 50000
        N_EDGES = 12500
        C_IN = 32
        C_OUT = 32
        BN_EPS = 1e-05

        def batch_norm(h, gamma, beta):
            mean = jnp.mean(h, axis=0)
            var = jnp.mean((h - mean) ** 2, axis=0)
            return (h - mean) * jax.lax.rsqrt(var + BN_EPS) * gamma + beta
        key = jax.random.key(seed)
        ks = jax.random.split(key, 8)
        x = jax.random.normal(ks[0], (N_NODES, C_IN), dtype=jnp.float32)
        edge_index = jax.random.randint(ks[1], (2, N_EDGES), 0, N_NODES, dtype=jnp.int64)
        s1 = 1.0 / np.sqrt(2 * C_IN)
        s2 = 1.0 / np.sqrt(C_OUT)
        W1 = jax.random.uniform(ks[2], (2 * C_IN, C_OUT), jnp.float32, -s1, s1)
        b1 = jax.random.uniform(ks[3], (C_OUT,), jnp.float32, -s1, s1)
        W2 = jax.random.uniform(ks[4], (C_OUT, C_OUT), jnp.float32, -s2, s2)
        b2 = jax.random.uniform(ks[5], (C_OUT,), jnp.float32, -s2, s2)
        gamma1 = jnp.ones((C_OUT,), jnp.float32)
        beta1 = jnp.zeros((C_OUT,), jnp.float32)
        gamma2 = jnp.ones((C_OUT,), jnp.float32)
        beta2 = jnp.zeros((C_OUT,), jnp.float32)
        return {'x': x, 'W1': W1, 'b1': b1, 'gamma1': gamma1, 'beta1': beta1, 'W2': W2, 'b2': b2, 'gamma2': gamma2, 'beta2': beta2, 'edge_index': edge_index}
    _L1_gnn_all = _L1_gnn_setup()
    _L1_gnn_in = {k: v for k, v in _L1_gnn_all.items() if k in ('W1', 'b1', 'gamma1', 'beta1', 'W2', 'b2', 'gamma2', 'beta2')}
    del _L1_gnn_all

    def _L2_gnn_setup():
        import jax, jax.numpy as jnp
        import numpy as np
        DIM = 3
        K = 3
        S = 2 ** DIM
        KTOT = K ** DIM
        N_NODES = 100000
        N_EDGES = 25000
        C_IN = 32
        C_OUT = 32
        _BITS = np.array([[s >> d & 1 for d in range(DIM)] for s in range(S)], dtype=np.int32)
        _STRIDES = np.array([K ** d for d in range(DIM)], dtype=np.int32)

        def spline_basis(edge_attr):
            pos = edge_attr * (K - 1)
            lo = jnp.floor(pos)
            frac = pos - lo
            lo = lo.astype(jnp.int32)
            bits = jnp.asarray(_BITS)
            bits_f = bits.astype(edge_attr.dtype)
            basis = jnp.prod(bits_f[None] * frac[:, None, :] + (1.0 - bits_f[None]) * (1.0 - frac[:, None, :]), axis=-1)
            idx = jnp.clip(lo[:, None, :] + bits[None], 0, K - 1)
            wi = jnp.sum(idx * jnp.asarray(_STRIDES), axis=-1)
            return (basis, wi)

        def spline_conv(x, edge_index, basis, wi, weight, root, bias):
            n = x.shape[0]
            src, dst = (edge_index[0], edge_index[1])
            xW = jnp.einsum('ni,kio->nko', x, weight)
            msg = jnp.zeros((src.shape[0], weight.shape[2]), dtype=x.dtype)
            for s in range(S):
                msg = msg + basis[:, s, None] * xW[src, wi[:, s]]
            out = jax.ops.segment_sum(msg, dst, num_segments=n)
            deg = jax.ops.segment_sum(jnp.ones((dst.shape[0],), dtype=x.dtype), dst, num_segments=n)
            out = out / jnp.clip(deg, 1.0)[:, None]
            return out + x @ root + bias
        key = jax.random.key(seed)
        ks = jax.random.split(key, 10)
        x = jax.random.normal(ks[0], (N_NODES, C_IN), dtype=jnp.float32)
        edge_index = jax.random.randint(ks[1], (2, N_EDGES), 0, N_NODES, dtype=jnp.int32)
        edge_attr = jax.random.uniform(ks[2], (N_EDGES, DIM), dtype=jnp.float32)
        scale = 0.1
        w1 = jax.random.normal(ks[3], (KTOT, C_IN, C_OUT), dtype=jnp.float32) * scale
        root1 = jax.random.normal(ks[4], (C_IN, C_OUT), dtype=jnp.float32) * scale
        b1 = jnp.zeros((C_OUT,), dtype=jnp.float32)
        w2 = jax.random.normal(ks[5], (KTOT, C_OUT, C_OUT), dtype=jnp.float32) * scale
        root2 = jax.random.normal(ks[6], (C_OUT, C_OUT), dtype=jnp.float32) * scale
        b2 = jnp.zeros((C_OUT,), dtype=jnp.float32)
        return {'x': x, 'edge_index': edge_index, 'edge_attr': edge_attr, 'w1': w1, 'root1': root1, 'b1': b1, 'w2': w2, 'root2': root2, 'b2': b2}
    _L2_gnn_all = _L2_gnn_setup()
    _L2_gnn_in = {k: v for k, v in _L2_gnn_all.items() if k in ('w1', 'root1', 'b1', 'w2', 'root2', 'b2')}
    del _L2_gnn_all

    def _L3_gnn_setup():
        import jax, jax.numpy as jnp
        import numpy as np
        N_NODES = 100000
        N_EDGES = 25000
        NODE_DIM = 32
        EDGE_DIM = 8
        NUM_LAYERS = 3
        NEG_SLOPE = 0.01
        EPS = 0.0
        key = jax.random.key(seed)
        ks = jax.random.split(key, 7)
        x = jax.random.normal(ks[0], (N_NODES, NODE_DIM), dtype=jnp.float32)
        edge_attr = jax.random.normal(ks[1], (N_EDGES, EDGE_DIM), dtype=jnp.float32)
        W = jax.random.normal(ks[2], (NUM_LAYERS, NODE_DIM, NODE_DIM), dtype=jnp.float32) / np.sqrt(NODE_DIM)
        b = jax.random.normal(ks[3], (NUM_LAYERS, NODE_DIM), dtype=jnp.float32) * 0.01
        We = jax.random.normal(ks[4], (NUM_LAYERS, EDGE_DIM, NODE_DIM), dtype=jnp.float32) / np.sqrt(EDGE_DIM)
        be = jax.random.normal(ks[5], (NUM_LAYERS, NODE_DIM), dtype=jnp.float32) * 0.01
        edge_index = jax.random.randint(ks[6], (2, N_EDGES), 0, N_NODES, dtype=jnp.int64 if jax.config.jax_enable_x64 else jnp.int32)
        return {'x': x, 'edge_attr': edge_attr, 'W': W, 'b': b, 'We': We, 'be': be, 'edge_index': edge_index}
    _L3_gnn_all = _L3_gnn_setup()
    _L3_gnn_in = {k: v for k, v in _L3_gnn_all.items() if k in ('W', 'b', 'We', 'be')}
    del _L3_gnn_all
    return {'x': x, 'src': src, 'dst': dst, 'edge_attr_3': edge_attr_3, 'edge_attr_8': edge_attr_8, 'L0_gnn_beta': _L0_gnn_in['beta'], 'L0_gnn_W1': _L0_gnn_in['W1'], 'L0_gnn_b1': _L0_gnn_in['b1'], 'L0_gnn_W2': _L0_gnn_in['W2'], 'L0_gnn_b2': _L0_gnn_in['b2'], 'L1_gnn_W1': _L1_gnn_in['W1'], 'L1_gnn_b1': _L1_gnn_in['b1'], 'L1_gnn_gamma1': _L1_gnn_in['gamma1'], 'L1_gnn_beta1': _L1_gnn_in['beta1'], 'L1_gnn_W2': _L1_gnn_in['W2'], 'L1_gnn_b2': _L1_gnn_in['b2'], 'L1_gnn_gamma2': _L1_gnn_in['gamma2'], 'L1_gnn_beta2': _L1_gnn_in['beta2'], 'L2_gnn_w1': _L2_gnn_in['w1'], 'L2_gnn_root1': _L2_gnn_in['root1'], 'L2_gnn_b1': _L2_gnn_in['b1'], 'L2_gnn_w2': _L2_gnn_in['w2'], 'L2_gnn_root2': _L2_gnn_in['root2'], 'L2_gnn_b2': _L2_gnn_in['b2'], 'L3_gnn_W': _L3_gnn_in['W'], 'L3_gnn_b': _L3_gnn_in['b'], 'L3_gnn_We': _L3_gnn_in['We'], 'L3_gnn_be': _L3_gnn_in['be']}

def reference(x, src, dst, edge_attr_3, edge_attr_8, L0_gnn_beta, L0_gnn_W1, L0_gnn_b1, L0_gnn_W2, L0_gnn_b2, L1_gnn_W1, L1_gnn_b1, L1_gnn_gamma1, L1_gnn_beta1, L1_gnn_W2, L1_gnn_b2, L1_gnn_gamma2, L1_gnn_beta2, L2_gnn_w1, L2_gnn_root1, L2_gnn_b1, L2_gnn_w2, L2_gnn_root2, L2_gnn_b2, L3_gnn_W, L3_gnn_b, L3_gnn_We, L3_gnn_be):
    import jax
    import jax.numpy as jnp

    def _L0_gnn_ref(x, edge_index, beta, W1, b1, W2, b2):
        import jax, jax.numpy as jnp
        import numpy as np
        N_NODES = 100000
        N_EDGES = 25000
        D = 32
        H = 2 * D
        EPS = 1e-07

        def _edge_softmax(logits, dst, num_nodes):
            m = jax.ops.segment_max(logits, dst, num_segments=num_nodes)
            e = jnp.exp(logits - m[dst])
            s = jax.ops.segment_sum(e, dst, num_segments=num_nodes)
            return e / s[dst]
        n = x.shape[0]
        dst = edge_index[0]
        src = edge_index[1]
        edge_msg = jax.nn.relu(x[src]) + EPS
        alpha = _edge_softmax(beta * edge_msg, dst, n)
        h = jax.ops.segment_sum(edge_msg * alpha, dst, num_segments=n)
        h = jax.nn.relu(h @ W1 + b1) @ W2 + b2
        return h

    def _L1_gnn_ref(x, W1, b1, gamma1, beta1, W2, b2, gamma2, beta2, edge_index):
        import jax, jax.numpy as jnp
        import numpy as np
        N_NODES = 50000
        N_EDGES = 12500
        C_IN = 32
        C_OUT = 32
        BN_EPS = 1e-05

        def batch_norm(h, gamma, beta):
            mean = jnp.mean(h, axis=0)
            var = jnp.mean((h - mean) ** 2, axis=0)
            return (h - mean) * jax.lax.rsqrt(var + BN_EPS) * gamma + beta
        row, col = (edge_index[0], edge_index[1])
        ef = jnp.concatenate([x[row], x[col]], axis=-1)
        h = jax.nn.relu(batch_norm(ef @ W1 + b1, gamma1, beta1))
        h = jax.nn.relu(batch_norm(h @ W2 + b2, gamma2, beta2))
        out = jax.ops.segment_sum(h, row, num_segments=x.shape[0])
        return out

    def _L2_gnn_ref(x, edge_index, edge_attr, w1, root1, b1, w2, root2, b2):
        import jax, jax.numpy as jnp
        import numpy as np
        DIM = 3
        K = 3
        S = 2 ** DIM
        KTOT = K ** DIM
        N_NODES = 100000
        N_EDGES = 25000
        C_IN = 32
        C_OUT = 32
        _BITS = np.array([[s >> d & 1 for d in range(DIM)] for s in range(S)], dtype=np.int32)
        _STRIDES = np.array([K ** d for d in range(DIM)], dtype=np.int32)

        def spline_basis(edge_attr):
            pos = edge_attr * (K - 1)
            lo = jnp.floor(pos)
            frac = pos - lo
            lo = lo.astype(jnp.int32)
            bits = jnp.asarray(_BITS)
            bits_f = bits.astype(edge_attr.dtype)
            basis = jnp.prod(bits_f[None] * frac[:, None, :] + (1.0 - bits_f[None]) * (1.0 - frac[:, None, :]), axis=-1)
            idx = jnp.clip(lo[:, None, :] + bits[None], 0, K - 1)
            wi = jnp.sum(idx * jnp.asarray(_STRIDES), axis=-1)
            return (basis, wi)

        def spline_conv(x, edge_index, basis, wi, weight, root, bias):
            n = x.shape[0]
            src, dst = (edge_index[0], edge_index[1])
            xW = jnp.einsum('ni,kio->nko', x, weight)
            msg = jnp.zeros((src.shape[0], weight.shape[2]), dtype=x.dtype)
            for s in range(S):
                msg = msg + basis[:, s, None] * xW[src, wi[:, s]]
            out = jax.ops.segment_sum(msg, dst, num_segments=n)
            deg = jax.ops.segment_sum(jnp.ones((dst.shape[0],), dtype=x.dtype), dst, num_segments=n)
            out = out / jnp.clip(deg, 1.0)[:, None]
            return out + x @ root + bias
        basis, wi = spline_basis(edge_attr)
        h = jax.nn.elu(spline_conv(x, edge_index, basis, wi, w1, root1, b1))
        h = jax.nn.elu(spline_conv(h, edge_index, basis, wi, w2, root2, b2))
        return h

    def _L3_gnn_ref(x, edge_attr, W, b, We, be, edge_index):
        import jax, jax.numpy as jnp
        import numpy as np
        N_NODES = 100000
        N_EDGES = 25000
        NODE_DIM = 32
        EDGE_DIM = 8
        NUM_LAYERS = 3
        NEG_SLOPE = 0.01
        EPS = 0.0
        src = edge_index[0]
        dst = edge_index[1]
        n = x.shape[0]
        for l in range(NUM_LAYERS):
            e = edge_attr @ We[l] + be[l]
            msg = jax.nn.relu(x[src] + e)
            agg = jax.ops.segment_sum(msg, dst, num_segments=n)
            h = (1.0 + EPS) * x + agg
            x = jax.nn.leaky_relu(h @ W[l] + b[l], negative_slope=NEG_SLOPE)
        return x
    edge_index = jnp.stack([src, dst])
    h = jnp.maximum(_layernorm(x, axis=-1), 0.0)
    x = x + _L0_gnn_ref(h, edge_index, L0_gnn_beta, L0_gnn_W1, L0_gnn_b1, L0_gnn_W2, L0_gnn_b2)
    h = jnp.maximum(_layernorm(x, axis=-1), 0.0)
    x = x + _L1_gnn_ref(h, L1_gnn_W1, L1_gnn_b1, L1_gnn_gamma1, L1_gnn_beta1, L1_gnn_W2, L1_gnn_b2, L1_gnn_gamma2, L1_gnn_beta2, edge_index)
    h = jnp.maximum(_layernorm(x, axis=-1), 0.0)
    x = x + _L2_gnn_ref(h, edge_index, edge_attr_3, L2_gnn_w1, L2_gnn_root1, L2_gnn_b1, L2_gnn_w2, L2_gnn_root2, L2_gnn_b2)
    h = jnp.maximum(_layernorm(x, axis=-1), 0.0)
    x = x + _L3_gnn_ref(h, edge_attr_8, L3_gnn_W, L3_gnn_b, L3_gnn_We, L3_gnn_be, edge_index)
    return x

_drawn_inputs = setup_inputs


def setup_inputs(seed=0):
    import zlib

    import numpy as np

    out = dict(_drawn_inputs(seed))
    spreads = {'L0_gnn_b1': (0.0, 0.1),
     'L0_gnn_b2': (0.0, 0.1),
     'L1_gnn_gamma1': (1.0, 0.2),
     'L1_gnn_beta1': (0.0, 0.1),
     'L1_gnn_gamma2': (1.0, 0.2),
     'L1_gnn_beta2': (0.0, 0.1),
     'L2_gnn_b1': (0.0, 0.479),
     'L2_gnn_b2': (0.0, 0.1)}
    factors = {'L1_gnn_b1': 8.0, 'L1_gnn_b2': 8.0, 'L3_gnn_b': 8.0, 'L3_gnn_be': 8.0}
    for name, (base, spread) in spreads.items():
        noise = np.random.default_rng([zlib.crc32(name.encode()), seed]).standard_normal(out[name].shape)
        drawn = base * np.exp(spread * noise) if base else spread * noise
        out[name] = jnp.asarray(drawn.astype(out[name].dtype))
    for name, factor in factors.items():
        out[name] = (out[name] * factor).astype(out[name].dtype)
    return out
```

```python
from contextlib import ExitStack

import concourse.bass as bass
from concourse import mybir

F32 = mybir.dt.float32
F16 = mybir.dt.float16
I32 = mybir.dt.int32
ALU = mybir.AluOpType
ACT = mybir.ActivationFunctionType
AX = mybir.AxisListType

P = 128
D = 32
CH = 8
BIG = 1.0e30
FAR = 8388608.0


class Names:
    pass


class Link:

    def __init__(self, eng, sem):
        self.eng, self.sem, self.base, self.n = eng, sem, 0, 0

    def at(self, base):
        self.base, self.n = base, 0

    def inc(self, ins):
        self.n += 1
        ins.then_inc(self.sem, 1)

    def __call__(self, ins):
        self.inc(ins)
        self.eng.wait_ge(self.sem, self.base + self.n)


def hold(g, eng, sem, value):
    eng.wait_ge(sem, value)
    eng.sem_inc(g.hop, 1)


def over(ap, axis, n):
    ap = ap.unsqueeze(axis)
    shape = list(ap.shape)
    shape[axis] = n
    return ap.broadcast_to(shape)


def chunks(g, eng, body):
    body(0, 0, True)
    body(0, 1, True)
    with eng.Fori(1, g.NCH // 2) as k:
        body(k, 0, False)
        body(k, 1, False)
    body(g.NCH // 2, 0, False)


def ahead(g, load, store):
    load(0, 0, True)
    load(0, 1, True)
    last = g.NCH // 2
    with g.nc.sync.Fori(0, last - 1) as k:
        store(k, 0)
        load(k + 1, 0, False)
        store(k, 1)
        load(k + 1, 1, False)
    store(last - 1, 0)
    load(last, 0, False)
    store(last - 1, 1)
    store(last, 0)


def both(g, eng, sems, per):
    for b in range(2):
        eng.wait_ge(sems[b], per * ((g.NCH + 1 - b) // 2))


class Phase:

    def __init__(self, g, name):
        self.g, self.nc, self.name, self.ctx, self.sems = g, g.nc, name, ExitStack(), []

    def __enter__(self):
        self.ctx.__enter__()
        return self

    def __exit__(self, *a):
        done = self.ctx.__exit__(*a)
        if a[0] is None:
            self.nc.clear_and_free_semaphores(self.sems)
            self.nc.all_engine_barrier()
        return done

    def sb(self, n, s, d=F32):
        return self.ctx.enter_context(self.nc.sbuf_tensor(f"{self.name}_{n}", s, d))

    def sb2(self, n, s, d=F32):
        return [self.sb(f"{n}{i}", s, d) for i in range(2)]

    def ps(self, n, s=(P, 512), d=F32):
        return self.ctx.enter_context(self.nc.psum_tensor(f"{self.name}_{n}", list(s), d))

    def sem(self, n):
        self.sems.append(self.nc.alloc_semaphore(name=f"{self.name}_{n}"))
        return self.sems[-1]

    def sem2(self, n):
        return [self.sem(f"{n}{i}") for i in range(2)]

    def block(self):
        return self.ctx.enter_context(self.nc.Block())


def load_weights(g, a):
    with Phase(g, "prep") as ph:
        made, loaded, cleared = ph.sem("made"), ph.sem("loaded"), ph.sem("cleared")
        blank, mlp0, mlp1, filled = ph.sem("blank"), ph.sem("mlp0"), ph.sem("mlp1"), ph.sem("filled")
        psc = ph.ps("psc")
        rb1 = ph.sb("rb1", [2 * D, 1])
        rb1w = ph.sb("rb1w", [2 * D, P])
        w2c = ph.sb("w2c", [2 * D, D])
        block = ph.block()
        loads = []

        def diagonal(dst, src, rows, cols, times):
            for t in range(times):
                loads.append((dst[t * rows:(t + 1) * rows, t * cols:(t + 1) * cols], src))

        diagonal(g.w0a, a["L0_gnn_W1"], D, 2 * D, 4)
        diagonal(g.w0b, a["L0_gnn_W2"], 2 * D, D, 2)
        diagonal(g.w1s, a["L1_gnn_W1"][0:D, :], D, D, 4)
        diagonal(g.w1d, a["L1_gnn_W1"][D:2 * D, :], D, D, 4)
        diagonal(g.w2, a["L1_gnn_W2"], D, D, 4)
        diagonal(g.root[0], a["L2_gnn_root1"], D, D, 4)
        diagonal(g.root[1], a["L2_gnn_root2"], D, D, 4)
        for l in range(3):
            diagonal(g.w3[l], a["L3_gnn_W"][l], D, D, 4)
            diagonal(g.we[l], a["L3_gnn_We"][l], 8, D, 8)
        for n, ap in enumerate([a["L0_gnn_b2"], a["L1_gnn_b1"], a["L1_gnn_b2"], a["L2_gnn_b1"], a["L2_gnn_b2"],
                                *[a["L3_gnn_b"][l] for l in range(3)], *[a["L3_gnn_be"][l] for l in range(3)]]):
            loads.append((g.bias[:, n, :], ap.unsqueeze(0)))
        for n, ap in enumerate([a["L1_gnn_gamma1"], a["L1_gnn_beta1"], a["L1_gnn_gamma2"], a["L1_gnn_beta2"]]):
            loads.append((g.bn[:, n, :], over(ap, 0, P)))
        for t in range(2):
            loads.append((g.b0col[t * 2 * D:(t + 1) * 2 * D, :], a["L0_gnn_b1"].unsqueeze(1)))
        loads.append((g.beta[:, :], over(a["L0_gnn_beta"], 0, P)))
        loads.append((w2c[:, :], a["L0_gnn_W2"]))
        for c, w in enumerate((a["L2_gnn_w1"], a["L2_gnn_w2"])):
            wv = w.rearrange("(z j) i o -> z i j o", z=3)
            for z in range(3):
                loads.append((g.spline[c][z * D:(z + 1) * D, :, :], wv[z]))

        @block.sync
        def _(sp):
            sp.wait_ge(cleared, 1)
            for dst, src in loads:
                with g.nc.allow_non_contiguous_dma(reason="columns and small blocks of weights"):
                    sp.dma_start(dst, src).then_inc(loaded, 16)

        @block.gpsimd
        def _(pool):
            pool.iota(g.iota16[:, :], [[1, g.R1]], base=0, channel_multiplier=0,
                      allow_small_or_imprecise_dtypes=True).then_inc(made, 1)
            pool.memset(g.ident[:, :], 0.0).then_inc(blank, 1)
            pool.memset(g.before[:, :], 1.0).then_inc(blank, 1)
            pool.memset(g.notbefore[:, :], 1.0).then_inc(blank, 1)
            pool.wait_ge(blank, 3)
            pool.affine_select(out=g.ident[:, :], in_=g.ident[:, :], pattern=[[1, P]], compare_op=ALU.not_equal,
                               fill=1.0, base=0, channel_multiplier=-1).then_inc(made, 1)
            pool.affine_select(out=g.before[:, :], in_=g.before[:, :], pattern=[[1, P]], compare_op=ALU.is_gt,
                               fill=0.0, base=0, channel_multiplier=-1).then_inc(made, 1)
            pool.affine_select(out=g.notbefore[:, :], in_=g.notbefore[:, :], pattern=[[-1, P]],
                               compare_op=ALU.is_ge, fill=0.0, base=0, channel_multiplier=1).then_inc(made, 1)

        @block.vector
        def _(v):
            link = Link(v, filled)
            for t in (g.w0a, g.w0b, g.w1s, g.w1d, g.w2, *g.root, *g.w3, *g.we):
                link.inc(v.memset(t[:, :], 0.0))
            link.inc(v.memset(g.ones16[:, :], 1.0))
            link.inc(v.memset(g.ones[:, :], 1.0))
            link.inc(v.memset(g.eps[:, :], 1e-5))
            link(v.memset(g.zeros[:, :], 0.0))
            v.sem_inc(cleared, 1)
            v.wait_ge(loaded, 16 * len(loads))
            link(v.tensor_scalar(rb1[:, :], g.b0col[0:2 * D, :], 0.0, None, ALU.max))
            v.tensor_copy(rb1w[:, :], rb1[:, 0:1].broadcast_to([2 * D, P])).then_inc(mlp0, 1)
            v.wait_ge(mlp1, 1)
            link(v.tensor_copy(g.alone[:, :], psc[:, 0:D]))

        @block.tensor
        def _(pe):
            pe.wait_ge(mlp0, 1)
            pe.matmul(psc[:, 0:D], rb1w[:, :], w2c[:, :], start=True, stop=False)
            pe.matmul(psc[:, 0:D], g.ones[0:1, :], g.bias[:, 0, :], start=False, stop=True).then_inc(mlp1, 1)


def sort_edges(g, which, rows, C, mid, tab, fill):
    W, NCH, R0, R1 = g.W, g.NCH, g.R0, g.R1
    for dg, R, dest in ((0, R0, mid), (1, R1, tab)):
        with Phase(g, f"sort{which}{dg}") as ph:
            chain = ph.sem("chain")
            hot, counted, based, base = ph.sem("hot"), ph.sem("counted"), ph.sem("based"), ph.sem("base")
            hot2, ranked, picked, placed = ph.sem("hot2"), ph.sem("ranked"), ph.sem("picked"), ph.sem("placed")
            idx_ready, rows_ready, reloaded = ph.sem("idx"), ph.sem("rows"), ph.sem("reloaded")
            sent = ph.sem2("sent")
            key_i = ph.sb("key_i", [P, W], I32)
            dig_i = ph.sb("dig_i", [P, W], I32)
            digit = ph.sb("digit", [P, W])
            hist = ph.sb("hist", [P, R])
            excl = ph.sb("excl", [P, R + 1])
            onehot = ph.sb2("onehot", [P, R], F16)
            junk = ph.sb("junk", [P, R])
            rank8 = ph.sb2("rank", [P, CH])
            rank_i = ph.sb("rank_i", [P, 3, CH], I32)
            idxr = ph.sb2("idxr", [P, CH], I32)
            rowr = ph.sb2("rowr", [P, CH, C])
            psh, psr = ph.ps("psh")[:, 0:R], ph.ps("psr")[:, 0:R]
            extra = fill(ph, dg) if fill else None
            block = ph.block()

            @block.sync
            def _(sp):
                if extra:
                    extra.sync(sp)
                both(g, sp, sent, 16 * CH)
                t = dest if dg == 0 else dest[1:g.NP + 1, :]
                sp.dma_start(rows[:, :, :], t.rearrange("(p w) c -> p w c", w=W)).then_inc(reloaded, 16)
                sp.wait_ge(reloaded, 16)

            @block.gpsimd
            def _(pool):
                if extra:
                    extra.gpsimd(pool)

                def scatter(k, b, first):
                    pool.wait_ge(rows_ready, 2 * k + b + 1)
                    pool.wait_ge(idx_ready, 2 * k + b + 1)
                    pool.sem_inc(g.hop, 1)
                    for j in range(CH):
                        pool.indirect_dma_start(out=dest, out_offset=bass.IndirectOffsetOnAxis(ap=idxr[b][:, j:j + 1], axis=0),
                                                in_=rowr[b][:, j, :], in_offset=None).then_inc(sent[b], 16)
                chunks(g, pool, scatter)

            @block.scalar
            def _(act):
                def copy(k, b, first):
                    if not first:
                        hold(g, act, sent[b], 16 * CH * k)
                    act.copy(rowr[b][:, :, :], rows[:, bass.ts(2 * k + b, CH), :]).then_inc(rows_ready, 1)
                chunks(g, act, copy)

            @block.tensor
            def _(pe):
                def count(k, b, first):
                    for j in range(CH):
                        pe.wait_ge(hot, (2 * k + b) * CH + j + 1)
                        pe.matmul(psh, g.ones16[:, :], onehot[j % 2][:, :], start=first and b == 0 and j == 0, stop=False,
                                  skip_group_check=True).then_inc(counted, 1)
                chunks(g, pe, count)
                pe.wait_ge(based, 1)
                pe.matmul(psr, g.ident[:, :], excl[:, 0:R], start=True, stop=False, skip_group_check=True).then_inc(base, 1)

                def rank(k, b, first):
                    for j in range(CH):
                        c = (2 * k + b) * CH + j
                        pe.wait_ge(hot2, c + 1)
                        pe.matmul(psr, g.before[:, :], onehot[j % 2][:, :], start=False, stop=False,
                                  skip_group_check=True).then_inc(ranked, 1)
                        pe.wait_ge(picked, c + 1)
                        pe.matmul(psr, g.notbefore[:, :], onehot[j % 2][:, :], start=False, stop=False,
                                  skip_group_check=True).then_inc(placed, 1)
                chunks(g, pe, rank)

            @block.vector
            def _(v):
                link = Link(v, chain)
                link(v.tensor_copy(key_i[:, :], rows[:, :, 0]))
                if dg == 0:
                    link(v.tensor_scalar(dig_i[:, :], key_i[:, :], R0 - 1, None, ALU.bitwise_and))
                else:
                    link(v.tensor_scalar(dig_i[:, :], key_i[:, :], 8, None, ALU.arith_shift_right))
                link(v.tensor_copy(digit[:, :], dig_i[:, :]))

                def mark(k, b, first, j, used, out):
                    c = (2 * k + b) * CH + j
                    if not (first and b == 0 and j < 2):
                        v.wait_ge(used, c - 1)
                    v.tensor_scalar(onehot[j % 2][:, :], g.iota16[:, 0:R], digit[:, bass.ds(c, 1)], None,
                                    ALU.is_equal).then_inc(out, 1)

                def mark_chunk(k, b, first):
                    for j in range(CH):
                        mark(k, b, first, j, counted, hot)
                chunks(g, v, mark_chunk)
                v.wait_ge(counted, W)
                link(v.tensor_copy(hist[:, :], psh))
                link(v.memset(excl[:, 0:1], 0.0))
                v.tensor_tensor_scan(excl[:, 1:R + 1], g.zeros[:, 0:R], hist[:, :], 0.0, ALU.add, ALU.add).then_inc(based, 1)
                v.wait_ge(base, 1)

                def place(k, b, first):
                    c = 2 * k + b
                    mark(k, b, first, 0, placed, hot2)
                    for j in range(CH):
                        if j + 1 < CH:
                            mark(k, b, first, j + 1, placed, hot2)
                        v.wait_ge(ranked, c * CH + j + 1)
                        v.tensor_tensor_reduce(junk[:, :], psr, onehot[j % 2][:, :], 1.0, 0.0, ALU.mult, ALU.add,
                                               rank8[b][:, j:j + 1]).then_inc(picked, 1)
                    v.wait_ge(picked, (c + 1) * CH)
                    if not first:
                        v.wait_ge(sent[b], 16 * CH * k)
                    if dg == 0:
                        link.at(c * 3 + 5)
                        link(v.tensor_copy(rank_i[:, 0, :], rank8[b][:, :]))
                        link(v.tensor_scalar(rank_i[:, 1, :], rank_i[:, 0, :], P - 1, None, ALU.bitwise_and))
                        link(v.tensor_scalar(rank_i[:, 2, :], rank_i[:, 0, :], 7, None, ALU.arith_shift_right))
                        v.scalar_tensor_tensor(idxr[b][:, :], rank_i[:, 1, :], float(W), rank_i[:, 2, :], ALU.mult,
                                               ALU.add).then_inc(idx_ready, 1)
                    else:
                        v.tensor_scalar(idxr[b][:, :], rank8[b][:, :], 1.0, None, ALU.add).then_inc(idx_ready, 1)
                chunks(g, v, place)


def first_rows(g, a):
    W, FULL, REST, E = g.W, g.FULL, g.REST, g.E
    with Phase(g, "rows") as ph:
        padded, loaded, done = ph.sem("padded"), ph.sem("loaded"), ph.sem("done")
        guarded, stored = ph.sem("guarded"), ph.sem("stored")
        raw_i = ph.sb("raw_i", [P, 2, W], I32)
        raw3 = ph.sb("raw3", [P, W, 3])
        raw8 = ph.sb("raw8", [P, W, 8])
        guard = ph.sb("guard", [1, 2, g.CB])
        block = ph.block()

        @block.sync
        def _(sp):
            sp.wait_ge(padded, 3)
            for t, d in ((raw_i[:, 0, :], a["dst"]), (raw_i[:, 1, :], a["src"])):
                sp.dma_start(t[0:FULL], d[0:FULL * W].rearrange("(p w) -> p w", w=W)).then_inc(loaded, 16)
                sp.dma_start(t[FULL:FULL + 1, 0:REST], d[FULL * W:E].rearrange("(p w) -> p w", p=1)).then_inc(loaded, 16)
            for t, d in ((raw3, a["edge_attr_3"]), (raw8, a["edge_attr_8"])):
                sp.dma_start(t[0:FULL, :, :], d[0:FULL * W, :].rearrange("(p w) c -> p w c", w=W)).then_inc(loaded, 16)
                sp.dma_start(t[FULL:FULL + 1, 0:REST, :], d[FULL * W:E, :].rearrange("(p w) c -> p w c", p=1)).then_inc(loaded, 16)
            sp.wait_ge(guarded, 2)
            for tab, C in ((g.b_tab, g.CB), (g.a_tab, g.CA)):
                sp.dma_start(tab[0:1, :], guard[:, 0, 0:C]).then_inc(stored, 16)
                sp.dma_start(tab[g.NP + 1:g.NP + 2, :], guard[:, 1, 0:C]).then_inc(stored, 16)
            sp.wait_ge(stored, 16 * 4)

        @block.vector
        def _(v):
            v.memset(raw_i[:, :, :], g.PADKEY).then_inc(padded, 1)
            v.memset(raw3[:, :, :], 0.0).then_inc(padded, 1)
            v.memset(raw8[:, :, :], 0.0).then_inc(padded, 1)
            v.memset(guard[:, 0, :], -1.0).then_inc(guarded, 1)
            v.memset(guard[:, 1, :], -2.0).then_inc(guarded, 1)
            v.wait_ge(loaded, 16 * 8)
            v.tensor_copy(g.rows_b[:, :, 0], raw_i[:, 0, :]).then_inc(done, 1)
            v.tensor_copy(g.rows_b[:, :, 1], raw_i[:, 1, :]).then_inc(done, 1)
            v.tensor_copy(g.rows_a[:, :, 0], raw_i[:, 1, :]).then_inc(done, 1)
            v.tensor_copy(g.rows_a[:, :, 1], raw_i[:, 0, :]).then_inc(done, 1)

        @block.scalar
        def _(act):
            act.wait_ge(loaded, 16 * 8)
            act.copy(g.rows_b[:, :, 2:5], raw3[:, :, :]).then_inc(done, 1)
            act.copy(g.rows_b[:, :, 5:13], raw8[:, :, :]).then_inc(done, 1)


def node_table_filler(g, a):
    def fill(ph, dg):
        if dg:
            return None
        x2 = a["x"].rearrange("(p n) f -> p n f", p=g.NPART)
        t2 = g.nodes1.rearrange("(p n) f -> p n f", p=g.NPART)
        BN = 40
        steps = g.NPER // BN
        xin = ph.sb2("xin", [P, BN, D])
        xout = ph.sb2("xout", [P, BN, D + 2])
        got, made, wrote, none = ph.sem2("got"), ph.sem("made"), ph.sem2("wrote"), ph.sem("none")
        e = Names()

        def steps_of(eng, body):
            body(0, 0, True)
            body(0, 1, True)
            with eng.Fori(1, steps // 2) as k:
                body(k, 0, False)
                body(k, 1, False)

        def sync(sp):
            def load(k, b, first):
                if not first:
                    sp.wait_ge(made, 2 * k + b - 1)
                sp.dma_start(xin[b][0:g.NPART, :, :], x2[:, bass.ts(2 * k + b, BN), :]).then_inc(got[b], 16)

            def store(k, b):
                sp.wait_ge(made, 2 * k + b + 1)
                sp.dma_start(t2[:, bass.ts(2 * k + b, BN), :], xout[b][0:g.NPART, :, :]).then_inc(wrote[b], 16)
            load(0, 0, True)
            load(0, 1, True)
            with sp.Fori(0, steps // 2 - 1) as k:
                store(k, 0)
                load(k + 1, 0, False)
                store(k, 1)
                load(k + 1, 1, False)
            store(steps // 2 - 1, 0)
            store(steps // 2 - 1, 1)
            for b in range(2):
                sp.wait_ge(wrote[b], 16 * (steps // 2))

        def gpsimd(pool):
            pool.memset(xout[0][:, :, D:D + 2], float(g.NP)).then_inc(none, 1)
            pool.memset(xout[1][:, :, D:D + 2], float(g.NP)).then_inc(none, 1)
            pool.wait_ge(none, 2)

            def copy(k, b, first):
                pool.wait_ge(got[b], 16 * (k + 1))
                if not first:
                    pool.wait_ge(wrote[b], 16 * k)
                pool.sem_inc(g.hop, 1)
                pool.tensor_copy(xout[b][0:g.NPART, :, 0:D], xin[b][0:g.NPART, :, :]).then_inc(made, 1)
            steps_of(pool, copy)
        e.sync, e.gpsimd = sync, gpsimd
        return e
    return fill


def places(g, which, rows, tab, E_):
    W, N = g.W, g.N
    with Phase(g, f"place{which}") as ph:
        edged, chain, flagged = ph.sem("edged"), ph.sem("chain"), ph.sem("flagged")
        copied, sent, vals = ph.sem("copied"), ph.sem2("sent"), ph.sem("vals")
        before = ph.sb("prev", [P, 1])
        after = ph.sb("next", [P, 1])
        tmp = ph.sb("tmp", [P, W])
        place = ph.sb("placev", [P, W], F32)
        elem = ph.sb("elem", [P, W], I32)
        idxr = ph.sb2("idxr", [P, CH], I32)
        valr = ph.sb2("valr", [P, CH])
        iot = ph.sem("iota")
        block = ph.block()
        flat = g.nodes1.rearrange("n (f o) -> (n f) o", o=1)

        @block.sync
        def _(sp):
            with g.nc.allow_non_contiguous_dma(reason="one key a partition"):
                sp.dma_start(before[:, :], tab[0:g.NP, 0:1].rearrange("(p w) c -> p w c", w=W)[:, 0, :]).then_inc(edged, 16)
                sp.dma_start(after[:, :], tab[2:g.NP + 2, 0:1].rearrange("(p w) c -> p w c", w=W)[:, W - 1, :]).then_inc(edged, 16)

        @block.vector
        def _(v):
            link = Link(v, chain)
            key, other = rows[:, :, 0], rows[:, :, 1]
            link.inc(v.tensor_tensor(E_.same[:, 1:W], key[:, 1:W], key[:, 0:W - 1], ALU.is_equal))
            link.inc(v.tensor_tensor(E_.last[:, 0:W - 1], key[:, 1:W], key[:, 0:W - 1], ALU.not_equal))
            v.wait_ge(edged, 32)
            link.inc(v.tensor_tensor(E_.same[:, 0:1], key[:, 0:1], before[:, :], ALU.is_equal))
            link(v.tensor_tensor(E_.last[:, W - 1:W], key[:, W - 1:W], after[:, :], ALU.not_equal))
            link(v.tensor_tensor_scan(E_.pfx[:, :], E_.same[:, :], g.zerow[:, :], 1.0, ALU.mult, ALU.add))
            link(v.tensor_scalar(E_.other[:, :], other, float(N - 1), None, ALU.min))
            link(v.tensor_scalar(E_.own[:, :], key, float(N - 1), None, ALU.min))
            link(v.tensor_scalar(tmp[:, :], E_.last[:, :], -FAR, FAR, ALU.mult, ALU.add))
            link(v.tensor_tensor(E_.out[:, :], tmp[:, :], key, ALU.add))
            link(v.scalar_tensor_tensor(tmp[:, :], key, float(D + 2), tmp[:, :], ALU.mult, ALU.add))
            v.tensor_scalar(elem[:, :], tmp[:, :], float(D + E_.column), None, ALU.add).then_inc(flagged, 1)

        @block.gpsimd
        def _(pool):
            pool.iota(place[:, :], [[1, W]], base=0, channel_multiplier=W, allow_small_or_imprecise_dtypes=True).then_inc(iot, 1)
            pool.wait_ge(iot, 1)
            pool.wait_ge(flagged, 1)

            def scatter(k, b, first):
                c = 2 * k + b
                if not first:
                    hold(g, pool, sent[b], 16 * CH * k)
                pool.tensor_copy(idxr[b][:, :], elem[:, bass.ts(c, CH)]).then_inc(copied, 1)
                pool.tensor_copy(valr[b][:, :], place[:, bass.ts(c, CH)]).then_inc(copied, 1)
                pool.wait_ge(copied, 2 * c + 2)
                pool.sem_inc(g.hop, 1)
                for j in range(CH):
                    pool.indirect_dma_start(out=flat, out_offset=bass.IndirectOffsetOnAxis(ap=idxr[b][:, j:j + 1], axis=0),
                                            in_=valr[b][:, j:j + 1], in_offset=None, bounds_check=N * (D + 2) - 1,
                                            oob_is_err=False).then_inc(sent[b], 16)
            chunks(g, pool, scatter)
            both(g, pool, sent, 16 * CH)


def norm_dve(v, link, act_in, act_out, count, x, n, t, out):
    link(v.tensor_reduce(t.s[:, 0:n], x, AX.X, ALU.add))
    link(v.tensor_scalar(t.s[:, 0:n], t.s[:, 0:n], -1.0 / D, None, ALU.mult))
    link(v.tensor_tensor(t.xc[:, 0:n, :], x, over(t.s[:, 0:n], 2, D), ALU.add))
    link(v.tensor_tensor(t.sq[:, 0:n, :], t.xc[:, 0:n, :], t.xc[:, 0:n, :], ALU.mult))
    v.tensor_reduce(t.var[:, 0:n], t.sq[:, 0:n, :], AX.X, ALU.add).then_inc(act_in, 1)
    v.wait_ge(act_out, count)
    link(v.reciprocal(t.rs[:, 0:n], t.sd[:, 0:n]))
    return v.scalar_tensor_tensor(out, t.xc[:, 0:n, :], 0.0, over(t.rs[:, 0:n], 2, D), ALU.max, ALU.mult)


def norm_act(g, act, act_in, act_out, count, n, t):
    act.wait_ge(act_in, count)
    act.activation(t.sd[:, 0:n], t.var[:, 0:n], ACT.Sqrt, bias=g.eps[:, :], scale=1.0 / D).then_inc(act_out, 1)


def norm_tiles(ph, n):
    t = Names()
    t.s, t.var, t.sd, t.rs = (ph.sb(f"ln_{name}", [P, n]) for name in ("s", "var", "sd", "rs"))
    t.xc, t.sq = ph.sb("ln_xc", [P, n, D]), ph.sb("ln_sq", [P, n, D])
    return t


def carry_tiles(ph, F):
    c = Names()
    c.F = F
    c.edge, c.turned = ph.sb("edge", [P, 2, F]), ph.sb("turned", [F, 2, P])
    c.run, c.carry = ph.sb("run", [F, P + 1]), ph.sb("carry", [P, F])
    c.ask, c.told = ph.sem("ask"), ph.sem("told")
    c.ps = [ph.ps(f"carry{i}") for i in range(3)]
    return c


def carry_dve(v, link, c, base, col, mult, kind="sum", back=False):
    F = c.F
    at = 0
    for piece, m in zip(col, mult):
        w = piece.shape[-1]
        link.inc(v.tensor_copy(c.edge[:, 0, at:at + w], piece))
        link.inc(v.tensor_copy(c.edge[:, 1, at:at + w], m))
        at += w
    link.inc(v.memset(c.run[:, P:P + 1] if back else c.run[:, 0:1], 0.0))
    v.wait_ge(link.sem, link.base + link.n)
    v.sem_inc(c.ask, 1)
    v.wait_ge(c.told, base + 1)
    link(v.tensor_copy(c.turned[:, 0, :], c.ps[0][0:F, 0:P]))
    link(v.tensor_copy(c.turned[:, 1, :], c.ps[1][0:F, 0:P]))
    if kind == "max":
        link(v.tensor_scalar(c.turned[:, 1, :], c.turned[:, 1, :], -1.0, BIG, ALU.add, ALU.mult))
        v.tensor_tensor_scan(c.run[:, 1:P + 1], c.turned[:, 1, :], c.turned[:, 0, :], -BIG, ALU.add, ALU.max).then_inc(c.ask, 1)
    elif back:
        v.tensor_tensor_scan(c.run[:, 0:P][:, ::-1], c.turned[:, 1, ::-1], c.turned[:, 0, ::-1], 0.0, ALU.mult, ALU.add).then_inc(c.ask, 1)
    else:
        v.tensor_tensor_scan(c.run[:, 1:P + 1], c.turned[:, 1, :], c.turned[:, 0, :], 0.0, ALU.mult, ALU.add).then_inc(c.ask, 1)
    v.wait_ge(c.told, base + 2)
    link(v.tensor_copy(c.carry[:, :], c.ps[2][:, 0:F]))


def carry_pe(g, pe, c, base, back=False):
    F = c.F
    pe.wait_ge(c.ask, base + 1)
    pe.matmul(c.ps[0][0:F, 0:P], c.edge[:, 0, :], g.ident[:, :], start=True, stop=True)
    pe.matmul(c.ps[1][0:F, 0:P], c.edge[:, 1, :], g.ident[:, :], start=True, stop=True).then_inc(c.told, 1)
    pe.wait_ge(c.ask, base + 2)
    s = c.run[:, 1:P + 1] if back else c.run[:, 0:P]
    pe.matmul(c.ps[2][:, 0:F], s, g.ident[0:F, 0:F], start=True, stop=True).then_inc(c.told, 1)


def scan_sum(g, v, link, c, base, buf, A, n=D):
    W = g.W
    for f in range(n):
        link.inc(v.tensor_tensor_scan(buf[:, :, f], A.same[:, :], buf[:, :, f], 0.0, ALU.mult, ALU.add))
    v.wait_ge(link.sem, link.base + link.n)
    carry_dve(v, link, c, base, [buf[:, W - 1, :]], [A.pfx[:, W - 1:W].broadcast_to([P, n])])
    for f in range(n):
        link.inc(v.scalar_tensor_tensor(buf[:, :, f], A.pfx[:, :], c.carry[:, f:f + 1], buf[:, :, f], ALU.mult, ALU.add))
    v.wait_ge(link.sem, link.base + link.n)


def gather_chunks(g, pool, idx_all, idxr, copied, table, ring, got, free, base=0):
    def body(k, b, first):
        c = 2 * k + b
        if not first:
            free(pool, k, b)
            pool.sem_inc(g.hop, 1)
        pool.tensor_copy(idxr[b][:, :], idx_all[:, bass.ts(c, CH)]).then_inc(copied, 1)
        pool.wait_ge(copied, base + c + 1)
        pool.sem_inc(g.hop, 1)
        for j in range(CH):
            pool.indirect_dma_start(out=ring[b][:, j, :], out_offset=None, in_=table,
                                    in_offset=bass.IndirectOffsetOnAxis(ap=idxr[b][:, j:j + 1], axis=0)).then_inc(got[b], 16)
    chunks(g, pool, body)


def layer0_edges(g, A, H, QA):
    W = g.W
    F = 8
    with Phase(g, "l0") as ph:
        lk, act_in, act_out = ph.sem("lk"), ph.sem("ln_in"), ph.sem("ln_out")
        used, got, got2, kept, kept2 = ph.sem("used"), ph.sem2("got"), ph.sem2("gots"), ph.sem2("kept"), ph.sem2("kepts")
        copied, bulk_lk = ph.sem("copied"), ph.sem("messages")
        expo, exped = ph.sem("expo"), ph.sem("exped")
        t = norm_tiles(ph, CH)
        ring = ph.sb2("ring", [P, CH, D + 2])
        idxr = ph.sb2("idxr", [P, CH], I32)
        L, M, Dd, Nn, Pp = (ph.sb(n, [P, W, F]) for n in ("logit", "top", "decay", "num", "prod"))
        neg = ph.sb("neg", [P, W])
        pneg = ph.sb("pneg", [P, W])
        c = carry_tiles(ph, 2 * F)
        KG = 4
        block = ph.block()

        @block.gpsimd
        def _(pool):
            def free_dst(p_, k, b):
                p_.wait_ge(used, 2 * k + b - 1)
                p_.wait_ge(kept[b], 16 * k)
            gather_chunks(g, pool, A.other, idxr, copied, g.nodes1, ring, got, free_dst)
            pool.wait_ge(used, g.NCH)
            both(g, pool, kept, 16)

            def free_src(p_, k, b):
                p_.wait_ge(kept2[b], 16 * k)
            gather_chunks(g, pool, A.own, idxr, copied, g.nodes1, ring, got2, free_src, base=g.NCH)

        @block.sync
        def _(sp):
            def keep(g_, k_, lin):
                def body(k, b, first):
                    sp.wait_ge(g_[b], 16 * CH * (k + 1))
                    sp.dma_start(lin.rearrange("(p w) c -> p w c", w=W)[:, bass.ts(2 * k + b, CH), :], ring[b][:, :, :]).then_inc(k_[b], 16)
                chunks(g, sp, body)
                both(g, sp, k_, 16)
            keep(got, kept, g.xd_lin)
            keep(got2, kept2, g.xs_lin)

        @block.scalar
        def _(act):
            def root(k, b, first):
                norm_act(g, act, act_in, act_out, 2 * k + b + 1, CH, t)
            chunks(g, act, root)
            with act.Fori(0, D // F) as q:
                act.wait_ge(expo, 2 * q + 1)
                act.activation(L[:, :, :], L[:, :, :], ACT.Exp).then_inc(exped, 1)
                act.wait_ge(expo, 2 * q + 2)
                act.activation(Dd[:, :, :], Dd[:, :, :], ACT.Exp).then_inc(exped, 1)

        @block.tensor
        def _(pe):
            with pe.Fori(0, D // F) as q:
                carry_pe(g, pe, c, q * KG)
                carry_pe(g, pe, c, q * KG + 2)

        @block.vector
        def _(v):
            link = Link(v, lk)
            KL = 6

            def messages(k, b, first):
                cc = 2 * k + b
                link.at(cc * KL)
                v.wait_ge(got[b], 16 * CH * (k + 1))
                norm_dve(v, link, act_in, act_out, cc + 1, ring[b][:, :, 0:D], CH, t, t.sq[:, :, :]).then_inc(lk, 1)
                v.wait_ge(lk, cc * KL + KL)
                v.tensor_scalar(H[:, bass.ts(cc, CH), :], t.sq[:, :, :], 1e-7, None, ALU.add).then_inc(bulk_lk, 1)
                v.tensor_copy(QA[:, bass.ts(cc, CH)], ring[b][:, :, D]).then_inc(used, 1)
            chunks(g, v, messages)
            v.wait_ge(bulk_lk, g.NCH)
            base = g.NCH * KL
            link.at(base)
            link(v.tensor_scalar(neg[:, :], A.same[:, :], -1.0, BIG, ALU.add, ALU.mult))
            link(v.tensor_scalar(pneg[:, :], A.pfx[:, :], -1.0, BIG, ALU.add, ALU.mult))
            base += 2
            KK = 82
            with v.Fori(0, D // F) as q:
                link.at(base + q * KK)
                hs = H[:, :, bass.ds(q * F, F)]
                link(v.tensor_scalar(L[:, :, :], hs, g.beta[:, 0:1], None, ALU.mult))
                for f in range(F):
                    link.inc(v.tensor_tensor_scan(M[:, :, f], neg[:, :], L[:, :, f], -BIG, ALU.add, ALU.max))
                v.wait_ge(lk, link.base + link.n)
                e = [M[:, W - 1, :]] * 2
                carry_dve(v, link, c, q * KG, e, [A.pfx[:, W - 1:W].broadcast_to([P, F])] * 2, kind="max")
                for f in range(F):
                    link.inc(v.scalar_tensor_tensor(M[:, :, f], pneg[:, :], c.carry[:, f:f + 1], M[:, :, f], ALU.add, ALU.max))
                v.wait_ge(lk, link.base + link.n)
                link(v.tensor_tensor(L[:, :, :], L[:, :, :], M[:, :, :], ALU.subtract))
                v.sem_inc(expo, 1)
                link.inc(v.tensor_tensor(Dd[:, 1:W, :], M[:, 0:W - 1, :], M[:, 1:W, :], ALU.subtract))
                link(v.tensor_tensor(Dd[:, 0, :], c.carry[:, 0:F], M[:, 0, :], ALU.subtract))
                link(v.tensor_scalar(Dd[:, :, :], Dd[:, :, :], 0.0, None, ALU.min))
                v.sem_inc(expo, 1)
                v.wait_ge(exped, 2 * q + 2)
                link(v.tensor_tensor(Dd[:, :, :], Dd[:, :, :], over(A.same[:, :], 2, F), ALU.mult))
                for f in range(F):
                    link.inc(v.tensor_tensor_scan(Pp[:, :, f], Dd[:, :, f], g.zerow[:, :], 1.0, ALU.mult, ALU.add))
                    link.inc(v.tensor_tensor_scan(M[:, :, f], Dd[:, :, f], L[:, :, f], 0.0, ALU.mult, ALU.add))
                link(v.tensor_tensor(Nn[:, :, :], L[:, :, :], hs, ALU.mult))
                for f in range(F):
                    link.inc(v.tensor_tensor_scan(Nn[:, :, f], Dd[:, :, f], Nn[:, :, f], 0.0, ALU.mult, ALU.add))
                v.wait_ge(lk, link.base + link.n)
                carry_dve(v, link, c, q * KG + 2, [M[:, W - 1, :], Nn[:, W - 1, :]], [Pp[:, W - 1, :]] * 2)
                for f in range(F):
                    link.inc(v.scalar_tensor_tensor(M[:, :, f], Pp[:, :, f], c.carry[:, f:f + 1], M[:, :, f], ALU.mult, ALU.add))
                    link.inc(v.scalar_tensor_tensor(Nn[:, :, f], Pp[:, :, f], c.carry[:, F + f:F + f + 1], Nn[:, :, f], ALU.mult, ALU.add))
                v.wait_ge(lk, link.base + link.n)
                link(v.reciprocal(M[:, :, :], M[:, :, :]))
                link(v.tensor_tensor(H[:, :, bass.ds(q * F, F)], Nn[:, :, :], M[:, :, :], ALU.mult))
                assert link.n == KK, link.n


def fill_back(g, A, H):
    W = g.W
    with Phase(g, "fb") as ph:
        lk, stored, filled = ph.sem("lk"), ph.sem("stored"), ph.sem("filled")
        c = carry_tiles(ph, D)
        notlast = ph.sb("notlast", [P, W])
        sfx = ph.sb("sfx", [P, W])
        block = ph.block()

        @block.tensor
        def _(pe):
            carry_pe(g, pe, c, 0, back=True)

        @block.sync
        def _(sp):
            sp.wait_ge(filled, 1)
            sp.dma_start(g.agg_tab[0:g.NP, :].rearrange("(p w) c -> p w c", w=W), H[:, :, :]).then_inc(stored, 16)
            sp.dma_start(g.agg_tab[g.NP:g.NP + 1, :], g.zerow[0:1, 0:D]).then_inc(stored, 16)
            sp.wait_ge(stored, 32)

        @block.vector
        def _(v):
            link = Link(v, lk)
            link(v.tensor_scalar(notlast[:, :], A.last[:, :], -1.0, 1.0, ALU.mult, ALU.add))
            link.inc(v.tensor_tensor_scan(sfx[:, ::-1], notlast[:, ::-1], g.zerow[:, :], 1.0, ALU.mult, ALU.add))
            link(v.tensor_tensor(H[:, :, :], H[:, :, :], over(A.last[:, :], 2, D), ALU.mult))
            for f in range(D):
                link.inc(v.tensor_tensor_scan(H[:, ::-1, f], notlast[:, ::-1], H[:, ::-1, f], 0.0, ALU.mult, ALU.add))
            v.wait_ge(lk, link.n)
            carry_dve(v, link, c, 0, [H[:, 0, :]], [sfx[:, 0:1].broadcast_to([P, D])], back=True)
            for f in range(D):
                link.inc(v.scalar_tensor_tensor(H[:, :, f], sfx[:, :], c.carry[:, f:f + 1], H[:, :, f], ALU.mult, ALU.add))
            v.wait_ge(lk, link.n)
            v.sem_inc(filled, 1)


def layer01_edges(g, A, H, QA, Z, PB):
    W = g.W
    N2 = 2 * CH
    with Phase(g, "l01") as ph:
        lk, act_in, act_out = ph.sem("lk"), ph.sem("ln_in"), ph.sem("ln_out")
        got, used, xgot, copied = ph.sem2("got"), ph.sem("used"), ph.sem2("xgot"), ph.sem("copied")
        aready, tdone, adone, h1done, hready, odone = (ph.sem(n) for n in ("aready", "tdone", "adone", "h1done", "hready", "odone"))
        x1ready, nready, t2done, a2done, zdone, zkept, xkept = (ph.sem(n) for n in ("x1ready", "nready", "t2done", "a2done", "zdone", "zkept", "xkept"))
        xused = ph.sem("xused")
        t = norm_tiles(ph, N2)
        idxr = ph.sb2("idxr", [P, CH], I32)
        ring = ph.sb2("ring", [P, CH, D])
        xr = ph.sb2("xr", [P, N2, D + 2])
        agg = ph.sb("agg", [P, N2, D])
        aT = ph.sb("aT", [P, 512])
        hT = ph.sb2("hT", [P, 512])
        x1 = ph.sb("x1", [P, N2, D])
        h16 = ph.sb("h16", [P, N2, D])
        psA, psB, psC, psD, psE = (ph.ps(n) for n in ("psA", "psB", "psC", "psD", "psE"))
        block = ph.block()

        @block.gpsimd
        def _(pool):
            def free(p_, k, b):
                p_.wait_ge(used, 2 * k + b - 1)
            gather_chunks(g, pool, QA, idxr, copied, g.agg_tab, ring, got, free)

        @block.sync
        def _(sp):
            def load(k, b, first):
                if not first:
                    sp.wait_ge(xused, 2 * k + b - 1)
                for i, lin in enumerate((g.xs_lin, g.xd_lin)):
                    sp.dma_start(xr[b][:, i * CH:(i + 1) * CH, :],
                                 lin.rearrange("(p w) c -> p w c", w=W)[:, bass.ts(2 * k + b, CH), :]).then_inc(xgot[b], 16)

            def store(k, b):
                sp.wait_ge(x1ready, 2 * k + b + 1)
                sp.dma_start(g.x1_lin.rearrange("(p w) c -> p w c", w=W)[:, bass.ts(2 * k + b, CH), :], x1[:, 0:CH, :]).then_inc(xkept, 16)
            ahead(g, load, store)
            sp.wait_ge(xkept, 16 * g.NCH)

        @block.scalar
        def _(act):
            def body(k, b, first):
                c = 2 * k + b
                act.wait_ge(got[b], 16 * CH * (k + 1))
                if not (first and b == 0):
                    act.wait_ge(tdone, c)
                act.sem_inc(g.hop, 1)
                act.copy(agg[:, 0:CH, :], H[:, bass.ts(c, CH), :]).then_inc(aready, 1)
                act.copy(agg[:, CH:N2, :], ring[b][:, :, :]).then_inc(used, 1)
                act.wait_ge(tdone, c + 1)
                act.copy(aT[:, :], psA[:, :]).then_inc(adone, 1)
                act.wait_ge(h1done, c + 1)
                act.activation(hT[0][:, :], psB[:, :], ACT.Relu, bias=g.b0col[:, :]).then_inc(hready, 1)
                act.activation(hT[1][:, :], psC[:, :], ACT.Relu, bias=g.b0col[:, :]).then_inc(hready, 1)
                norm_act(g, act, act_in, act_out, c + 1, N2, t)
                act.wait_ge(t2done, c + 1)
                act.copy(aT[:, :], psA[:, :]).then_inc(a2done, 1)
                hold(g, act, zdone, c + 1)
                act.copy(Z[:, bass.ts(c, CH), :], psE[:, 0:256].rearrange("p (t f) -> p t f", f=D)).then_inc(zkept, 1)
            chunks(g, act, body)

        @block.tensor
        def _(pe):
            def body(k, b, first):
                c = 2 * k + b
                pe.wait_ge(aready, c + 1)
                pe.wait_ge(used, c + 1)
                for q in range(4):
                    ins = pe.transpose(psA[:, q * P:(q + 1) * P], agg[:, 4 * q:4 * q + 4, :].rearrange("p t f -> p (t f)"), g.ident[:, :])
                ins.then_inc(tdone, 1)
                pe.wait_ge(adone, c + 1)
                pe.matmul(psB[:, :], g.w0a[:, 0:P], aT[:, :], start=True, stop=True)
                pe.matmul(psC[:, :], g.w0a[:, P:2 * P], aT[:, :], start=True, stop=True).then_inc(h1done, 1)
                pe.wait_ge(hready, 2 * c + 2)
                pe.matmul(psD[:, :], g.ones[0:1, :], over(g.bias[:, 0, :], 1, N2), start=True, stop=False, skip_group_check=True)
                for q in range(4):
                    for i in range(2):
                        o = psD[:, q * P + i * 64:q * P + i * 64 + 64]
                        ins = pe.matmul(o, hT[i][:, q * P:(q + 1) * P], g.w0b[:, :], start=False, stop=False, skip_group_check=True)
                ins.then_inc(odone, 1)
                pe.wait_ge(nready, c + 1)
                for q in range(4):
                    ins = pe.transpose(psA[:, q * P:(q + 1) * P], h16[:, 4 * q:4 * q + 4, :].rearrange("p t f -> p (t f)"), g.ident[:, :])
                ins.then_inc(t2done, 1)
                pe.wait_ge(a2done, c + 1)
                if not (first and b == 0):
                    pe.wait_ge(zkept, c)
                pe.matmul(psE[:, 0:256], g.ones[0:1, :], over(g.bias[:, 1, :], 1, CH), start=True, stop=False, skip_group_check=True)
                for q in range(2):
                    o = psE[:, q * P:(q + 1) * P]
                    pe.matmul(o, aT[:, q * P:(q + 1) * P], g.w1s[:, :], start=False, stop=False, skip_group_check=True)
                    ins = pe.matmul(o, aT[:, (q + 2) * P:(q + 3) * P], g.w1d[:, :], start=False, stop=False, skip_group_check=True)
                ins.then_inc(zdone, 1)
            chunks(g, pe, body)

        @block.vector
        def _(v):
            link = Link(v, lk)
            KL = 6

            def body(k, b, first):
                c = 2 * k + b
                link.at(c * KL)
                v.wait_ge(xgot[b], 32 * (k + 1))
                v.wait_ge(odone, c + 1)
                if not (first and b == 0):
                    v.wait_ge(xkept, 16 * c)
                link(v.tensor_tensor(x1[:, :, :], xr[b][:, :, 0:D], psD[:, :].rearrange("p (t f) -> p t f", f=D), ALU.add))
                v.sem_inc(x1ready, 1)
                v.tensor_copy(PB[:, bass.ts(c, CH)], xr[b][:, 0:CH, D + 1]).then_inc(xused, 1)
                norm_dve(v, link, act_in, act_out, c + 1, x1[:, :, :], N2, t, h16[:, :, :]).then_inc(nready, 1)
                assert link.n == KL, link.n
            chunks(g, v, body)


def batch_norm(g, ph, Z, SQ, valid, gi, tag, then_chunks=None):
    E = float(g.E)
    W = g.W
    lk, summed, spread, sqin, sqout = (ph.sem(f"{tag}_{n}") for n in ("lk", "summed", "spread", "sqin", "sqout"))
    part = ph.sb(f"{tag}_part", [P, D])
    mean = ph.sb(f"{tag}_mean", [P, D])
    var = ph.sb(f"{tag}_var", [P, D])
    sd = ph.sb(f"{tag}_sd", [P, D])
    pst = ph.ps(f"{tag}_ps")
    parts = Names()

    def tensor(pe):
        for i in range(2):
            pe.wait_ge(summed, i + 1)
            pe.matmul(pst[:, 0:D], g.ones[:, :], part[:, :], start=True, stop=True).then_inc(spread, 1)

    def scalar(act):
        act.wait_ge(sqin, 1)
        act.activation(SQ[:, :, :], Z[:, :, :], ACT.Square).then_inc(sqout, 1)
        act.wait_ge(sqin, 2)
        act.activation(sd[:, :], var[:, :], ACT.Sqrt, bias=g.eps[:, :], scale=1.0 / E).then_inc(sqout, 1)

    def vector(v):
        link = Link(v, lk)
        vb = over(valid[:, :], 2, D)
        link(v.tensor_tensor(Z[:, :, :], Z[:, :, :], vb, ALU.mult))
        v.tensor_reduce(part[:, :], Z[:, :, :].rearrange("p w f -> p f w"), AX.X, ALU.add).then_inc(summed, 1)
        v.wait_ge(spread, 1)
        link(v.tensor_scalar(mean[:, :], pst[:, 0:D], -1.0 / E, None, ALU.mult))
        link(v.tensor_tensor(Z[:, :, :], Z[:, :, :], over(mean[:, :], 1, W), ALU.add))
        link(v.tensor_tensor(Z[:, :, :], Z[:, :, :], vb, ALU.mult))
        v.sem_inc(sqin, 1)
        v.wait_ge(sqout, 1)
        v.tensor_reduce(part[:, :], SQ[:, :, :].rearrange("p w f -> p f w"), AX.X, ALU.add).then_inc(summed, 1)
        v.wait_ge(spread, 2)
        link(v.tensor_copy(var[:, :], pst[:, 0:D]))
        v.sem_inc(sqin, 1)
        v.wait_ge(sqout, 2)
        link(v.reciprocal(sd[:, :], sd[:, :]))
        link(v.tensor_tensor(sd[:, :], sd[:, :], g.bn[:, gi, :], ALU.mult))
        link(v.tensor_tensor(Z[:, :, :], Z[:, :, :], over(sd[:, :], 1, W), ALU.mult))
        link(v.tensor_tensor(Z[:, :, :], Z[:, :, :], over(g.bn[:, gi + 1, :], 1, W), ALU.add))
    parts.tensor, parts.scalar, parts.vector = tensor, scalar, vector
    return parts


def layer1_rest(g, A, SQ, Z, PB):
    W, N = g.W, g.N
    with Phase(g, "l1") as ph:
        valid = ph.sb("valid", [P, W])
        vready, bn1, mid, bn2 = ph.sem("valid"), ph.sem("bn1"), ph.sem("mid"), ph.sem("bn2")
        zt = ph.sb("zt", [P, CH * D])
        aT = ph.sb("aT", [P, 256])
        tready, tdone, adone, zdone, zkept = (ph.sem(n) for n in ("tready", "tdone", "adone", "zdone", "zkept"))
        psA, psE = ph.ps("psA"), ph.ps("psE")
        b1 = batch_norm(g, ph, Z, SQ, valid, 0, "bn1")
        b2 = batch_norm(g, ph, Z, SQ, valid, 2, "bn2")
        BN = 20
        steps = g.NPER // BN
        xin = ph.sb2("xin", [P, BN, D + 2])
        xout = ph.sb2("xout", [P, BN, D + 1])
        tgot, tmade, twrote, tchain = ph.sem2("tgot"), ph.sem("tmade"), ph.sem2("twrote"), ph.sem("tchain")
        block = ph.block()
        n1 = g.nodes1.rearrange("(p n) f -> p n f", p=g.NPART)
        n2 = g.nodes2.rearrange("(p n) f -> p n f", p=g.NPART)

        @block.sync
        def _(sp):
            def load(k, b, first):
                if not first:
                    sp.wait_ge(tmade, 2 * k + b - 1)
                sp.dma_start(xin[b][0:g.NPART, :, :], n1[:, bass.ts(2 * k + b, BN), :]).then_inc(tgot[b], 16)

            def store(k, b):
                sp.wait_ge(tmade, 2 * k + b + 1)
                sp.dma_start(n2[:, bass.ts(2 * k + b, BN), :], xout[b][0:g.NPART, :, :]).then_inc(twrote[b], 16)
            load(0, 0, True)
            load(0, 1, True)
            with sp.Fori(0, steps // 2 - 1) as k:
                store(k, 0)
                load(k + 1, 0, False)
                store(k, 1)
                load(k + 1, 1, False)
            store(steps // 2 - 1, 0)
            store(steps // 2 - 1, 1)
            for b in range(2):
                sp.wait_ge(twrote[b], 16 * (steps // 2))

        @block.gpsimd
        def _(pool):
            pool.iota(valid[:, :], [[1, W]], base=0, channel_multiplier=W, allow_small_or_imprecise_dtypes=True).then_inc(vready, 1)
            q = g.NPART

            def copy(k, b, first):
                pool.wait_ge(tgot[b], 16 * (k + 1))
                if not first:
                    pool.wait_ge(twrote[b], 16 * k)
                pool.tensor_tensor(xout[b][0:q, :, 0:D], xin[b][0:q, :, 0:D], over(g.alone[0:q, :], 1, BN), ALU.add).then_inc(tchain, 1)
                pool.tensor_copy(xout[b][0:q, :, D], xin[b][0:q, :, D + 1]).then_inc(tchain, 1)
                pool.wait_ge(tchain, 2 * (2 * k + b) + 2)
                pool.sem_inc(tmade, 1)
            copy(0, 0, True)
            copy(0, 1, True)
            with pool.Fori(1, steps // 2) as k:
                copy(k, 0, False)
                copy(k, 1, False)

        @block.scalar
        def _(act):
            b1.scalar(act)
            act.wait_ge(bn1, 1)

            def body(k, b, first):
                c = 2 * k + b
                if not (first and b == 0):
                    act.wait_ge(zkept, c)
                act.sem_inc(g.hop, 1)
                act.copy(zt[:, :], Z[:, bass.ts(c, CH), :].rearrange("p t f -> p (t f)")).then_inc(tready, 1)
                act.wait_ge(tdone, c + 1)
                act.activation(aT[:, :], psA[:, 0:256], ACT.Relu).then_inc(adone, 1)
                hold(g, act, zdone, c + 1)
                act.copy(Z[:, bass.ts(c, CH), :], psE[:, 0:256].rearrange("p (t f) -> p t f", f=D)).then_inc(zkept, 1)
            chunks(g, act, body)
            b2.scalar(act)

        @block.tensor
        def _(pe):
            b1.tensor(pe)

            def body(k, b, first):
                c = 2 * k + b
                pe.wait_ge(tready, c + 1)
                for q in range(2):
                    ins = pe.transpose(psA[:, q * P:(q + 1) * P], zt[:, q * P:(q + 1) * P], g.ident[:, :])
                ins.then_inc(tdone, 1)
                pe.wait_ge(adone, c + 1)
                pe.matmul(psE[:, 0:256], g.ones[0:1, :], over(g.bias[:, 2, :], 1, CH), start=True, stop=False, skip_group_check=True)
                for q in range(2):
                    ins = pe.matmul(psE[:, q * P:(q + 1) * P], aT[:, q * P:(q + 1) * P], g.w2[:, :], start=False, stop=False, skip_group_check=True)
                ins.then_inc(zdone, 1)
            chunks(g, pe, body)
            b2.tensor(pe)

        @block.vector
        def _(v):
            v.wait_ge(vready, 1)
            link = Link(v, mid)
            link(v.tensor_scalar(valid[:, :], valid[:, :], float(g.E), None, ALU.is_lt))
            b1.vector(v)
            v.sem_inc(bn1, 1)
            v.wait_ge(zkept, g.NCH)
            b2.vector(v)
            v.tensor_scalar(Z[:, :, :], Z[:, :, :], 0.0, None, ALU.max).then_inc(bn2, 1)

    with Phase(g, "l1s") as ph:
        lk, made, sent = ph.sem("lk"), ph.sem("made"), ph.sem2("sent")
        xgot = ph.sem2("xgot")
        x1 = ph.sb2("x1", [P, CH, D])
        c = carry_tiles(ph, D)
        rowr = ph.sb2("rowr", [P, CH, D + 1])
        idxr = ph.sb2("idxr", [P, CH], I32)
        block = ph.block()

        @block.tensor
        def _(pe):
            carry_pe(g, pe, c, 0)

        @block.sync
        def _(sp):
            def load(k, b, first):
                if not first:
                    sp.wait_ge(made, 3 * (2 * k + b) - 3)
                sp.dma_start(x1[b][:, :, :], g.x1_lin.rearrange("(p w) c -> p w c", w=W)[:, bass.ts(2 * k + b, CH), :]).then_inc(xgot[b], 16)
            chunks(g, sp, load)

        @block.gpsimd
        def _(pool):
            def scatter(k, b, first):
                pool.wait_ge(made, 3 * (2 * k + b) + 3)
                pool.sem_inc(g.hop, 1)
                for j in range(CH):
                    pool.indirect_dma_start(out=g.nodes2, out_offset=bass.IndirectOffsetOnAxis(ap=idxr[b][:, j:j + 1], axis=0),
                                            in_=rowr[b][:, j, :], in_offset=None, bounds_check=N - 1,
                                            oob_is_err=False).then_inc(sent[b], 16)
            chunks(g, pool, scatter)
            both(g, pool, sent, 16 * CH)

        @block.vector
        def _(v):
            link = Link(v, lk)
            scan_sum(g, v, link, c, 0, Z, A)

            def body(k, b, first):
                cc = 2 * k + b
                if not first:
                    v.wait_ge(sent[b], 16 * CH * k)
                v.wait_ge(xgot[b], 16 * (k + 1))
                v.tensor_tensor(rowr[b][:, :, 0:D], x1[b][:, :, :], Z[:, bass.ts(cc, CH), :], ALU.add).then_inc(made, 1)
                v.tensor_copy(rowr[b][:, :, D], PB[:, bass.ts(cc, CH)]).then_inc(made, 1)
                v.tensor_copy(idxr[b][:, :], A.out[:, bass.ts(cc, CH)]).then_inc(made, 1)
            chunks(g, v, body)


def close_segments(g, B, M, table, ph_name, count=None, scale=None):
    W = g.W
    with Phase(g, ph_name) as ph:
        lk, stored, closed = ph.sem("lk"), ph.sem("stored"), ph.sem("closed")
        c = carry_tiles(ph, D)
        c1 = carry_tiles_one(ph) if count is not None else None
        block = ph.block()

        @block.tensor
        def _(pe):
            if count is not None:
                carry_pe(g, pe, c1, 0)
            carry_pe(g, pe, c, 0)

        @block.sync
        def _(sp):
            sp.wait_ge(closed, 1)
            sp.dma_start(table[0:g.NP, :].rearrange("(p w) c -> p w c", w=W), M[:, :, :]).then_inc(stored, 16)
            sp.dma_start(table[g.NP:g.NP + 1, :], g.zerow[0:1, 0:D]).then_inc(stored, 16)
            sp.wait_ge(stored, 32)

        @block.vector
        def _(v):
            link = Link(v, lk)
            if count is not None:
                link(v.memset(count[:, :, :], 1.0))
                scan_sum(g, v, link, c1, 0, count, B, 1)
                link(v.reciprocal(count[:, :, :], count[:, :, :]))
            scan_sum(g, v, link, c, 0, M, B)
            if scale is not None:
                link(v.tensor_tensor(M[:, :, :], M[:, :, :], over(scale[:, :, 0], 2, D), ALU.mult))
            v.sem_inc(closed, 1)


def carry_tiles_one(ph):
    c = Names()
    c.F = 1
    c.edge, c.turned = ph.sb("edge1", [P, 2, 1]), ph.sb("turned1", [1, 2, P])
    c.run, c.carry = ph.sb("run1", [1, P + 1]), ph.sb("single", [P, 1])
    c.ask, c.told = ph.sem("ask1"), ph.sem("told1")
    c.ps = [ph.ps(f"single{i}") for i in range(3)]
    return c


def spline_weights(g, WT):
    W = g.W
    with Phase(g, "basis") as ph:
        lk = ph.sem("lk")
        pos, r, gt, lo, fr, c0, c1, omf, t0, t1 = (ph.sb(n, [P, W, 3]) for n in ("pos", "r", "gt", "lo", "fr", "c0", "c1", "omf", "t0", "t1"))
        pi = ph.sb("pi", [P, W, 3], I32)
        block = ph.block()

        @block.vector
        def _(v):
            link = Link(v, lk)
            link(v.tensor_scalar(pos[:, :, :], g.rows_b[:, :, 2:5], 2.0, None, ALU.mult))
            link(v.tensor_copy(pi[:, :, :], pos[:, :, :]))
            link(v.tensor_copy(r[:, :, :], pi[:, :, :]))
            link(v.tensor_tensor(gt[:, :, :], r[:, :, :], pos[:, :, :], ALU.is_gt))
            link(v.tensor_tensor(lo[:, :, :], r[:, :, :], gt[:, :, :], ALU.subtract))
            link(v.tensor_tensor(fr[:, :, :], pos[:, :, :], lo[:, :, :], ALU.subtract))
            link(v.tensor_scalar(omf[:, :, :], fr[:, :, :], -1.0, 1.0, ALU.mult, ALU.add))
            link(v.tensor_scalar(c0[:, :, :], lo[:, :, :], 0.0, 2.0, ALU.max, ALU.min))
            link(v.tensor_scalar(c1[:, :, :], lo[:, :, :], 1.0, None, ALU.add))
            link(v.tensor_scalar(c1[:, :, :], c1[:, :, :], 0.0, 2.0, ALU.max, ALU.min))
            for k in range(3):
                link(v.scalar_tensor_tensor(t0[:, :, :], c0[:, :, :], float(k), omf[:, :, :], ALU.is_equal, ALU.mult))
                link(v.scalar_tensor_tensor(t1[:, :, :], c1[:, :, :], float(k), fr[:, :, :], ALU.is_equal, ALU.mult))
                link(v.tensor_tensor(WT[:, :, :].rearrange("p w (d k) -> p w d k", k=3)[:, :, :, k], t0[:, :, :], t1[:, :, :], ALU.add))


class Spline:

    def __init__(self, ph, g, WT, M):
        self.g, self.WT, self.M = g, WT, M
        self.w01 = ph.sb("w01", [P, CH, 3, 3])
        self.hz = ph.sb("hz", [P, CH, 3, D])
        self.hzT = ph.sb("hzT", [3 * D, CH * P])
        self.V = ph.sb("V", [P, 2, 9, D])
        self.msg = ph.sb("msg", [P, CH, D])
        self.psT = ph.ps("psT", (P, 1024))
        self.psU = [ph.ps(f"psU{i}", (P, 2, 512)) for i in range(2)]
        self.wide, self.turned, self.flat, self.multiplied, self.weighed = (ph.sem("spline_" + n) for n in ("wide", "turned", "flat", "multiplied", "weighed"))

    LINKS = 7

    def vector(self, v, link, c, h):
        WTc = self.WT[:, bass.ts(c, CH), :]
        v.tensor_tensor(self.hz[:, :, :, :], over(h, 2, 3), over(WTc[:, :, 6:9], 3, D), ALU.mult).then_inc(self.wide, 1)
        link(v.tensor_tensor(self.w01[:, :, :, :], over(WTc[:, :, 0:3], 2, 3), over(WTc[:, :, 3:6], 3, 3), ALU.mult))
        for i in range(4):
            v.wait_ge(self.multiplied, 4 * c + i + 1)
            link(v.tensor_tensor(self.V[:, :, :, :], self.psU[i % 2][:, :, 0:288].rearrange("p t (j o) -> p t j o", o=D),
                                 over(self.w01[:, 2 * i:2 * i + 2, :, :].rearrange("p t a b -> p t (a b)"), 3, D), ALU.mult))
            v.tensor_reduce(self.msg[:, 2 * i:2 * i + 2, :], self.V[:, :, :, :].rearrange("p t j o -> p t o j"), AX.X,
                            ALU.add).then_inc(self.weighed, 1)
            if i == 3:
                v.wait_ge(self.weighed, 4 * c + 4)
            elif i >= 0:
                v.wait_ge(self.weighed, 4 * c + i + 1)
        link(v.tensor_scalar(self.M[:, bass.ts(c, CH), :], self.msg[:, :, :], 1.0, None, ALU.mult))

    def tensor(self, pe, c, w):
        pe.wait_ge(self.wide, c + 1)
        for t in range(CH):
            ins = pe.transpose(self.psT[0:3 * D, t * P:(t + 1) * P], self.hz[:, t, :, :].rearrange("p k f -> p (k f)"), self.g.ident[:, :])
        ins.then_inc(self.turned, 1)
        pe.wait_ge(self.flat, c + 1)
        for i in range(4):
            if i >= 2:
                pe.wait_ge(self.weighed, 4 * c + i - 1)
            for t in range(2):
                ins = pe.matmul(self.psU[i % 2][:, t, 0:288], self.hzT[:, (2 * i + t) * P:(2 * i + t + 1) * P],
                                w[:, :, :].rearrange("p j o -> p (j o)"), start=True, stop=True)
            ins.then_inc(self.multiplied, 1)

    def scalar(self, act, c):
        act.wait_ge(self.turned, c + 1)
        act.copy(self.hzT[:, :], self.psT[0:3 * D, :]).then_inc(self.flat, 1)


def lin(g, t, c, n=D):
    return t.rearrange("(p w) c -> p w c", w=g.W)[:, bass.ts(c, CH), :]


def conv1_edges(g, B, WT, M, S, QB):
    N2 = 2 * CH
    with Phase(g, "c1") as ph:
        lk, act_in, act_out = ph.sem("lk"), ph.sem("ln_in"), ph.sem("ln_out")
        got, copied, nready, kept, skept = ph.sem2("got"), ph.sem("copied"), ph.sem("nready"), ph.sem2("kept"), ph.sem("skept")
        read = ph.sem("read")
        t = norm_tiles(ph, N2)
        ring = ph.sb2("ring", [P, N2, D + 1])
        idxr = ph.sb2("idxr", [P, N2], I32)
        h16 = ph.sb("h16", [P, N2, D])
        sp_ = Spline(ph, g, WT, M)
        block = ph.block()

        @block.gpsimd
        def _(pool):
            def body(k, b, first):
                c = 2 * k + b
                if not first:
                    pool.wait_ge(kept[b], 32 * k)
                    hold(g, pool, read, c - 1)
                pool.tensor_copy(idxr[b][:, 0:CH], B.other[:, bass.ts(c, CH)]).then_inc(copied, 1)
                pool.tensor_copy(idxr[b][:, CH:N2], B.own[:, bass.ts(c, CH)]).then_inc(copied, 1)
                pool.wait_ge(copied, 2 * c + 2)
                pool.sem_inc(g.hop, 1)
                for j in range(N2):
                    pool.indirect_dma_start(out=ring[b][:, j, :], out_offset=None, in_=g.nodes2,
                                            in_offset=bass.IndirectOffsetOnAxis(ap=idxr[b][:, j:j + 1], axis=0)).then_inc(got[b], 16)
            chunks(g, pool, body)

        @block.sync
        def _(sp):
            def body(k, b, first):
                c = 2 * k + b
                sp.wait_ge(got[b], 16 * N2 * (k + 1))
                sp.dma_start(lin(g, g.x2s_lin, c), ring[b][:, 0:CH, :]).then_inc(kept[b], 16)
                sp.dma_start(lin(g, g.x2d_lin, c), ring[b][:, CH:N2, :]).then_inc(kept[b], 16)
                sp.wait_ge(nready, c + 1)
                sp.dma_start(lin(g, g.dst_lin, c), h16[:, CH:N2, :]).then_inc(skept, 16)
            chunks(g, sp, body)
            both(g, sp, kept, 32)
            sp.wait_ge(skept, 16 * g.NCH)

        @block.scalar
        def _(act):
            def body(k, b, first):
                c = 2 * k + b
                norm_act(g, act, act_in, act_out, c + 1, N2, t)
                sp_.scalar(act, c)
            chunks(g, act, body)

        @block.tensor
        def _(pe):
            def body(k, b, first):
                sp_.tensor(pe, 2 * k + b, g.spline[0])
            chunks(g, pe, body)

        @block.vector
        def _(v):
            link = Link(v, lk)
            KL = 13

            def body(k, b, first):
                c = 2 * k + b
                link.at(c * KL)
                v.wait_ge(got[b], 16 * N2 * (k + 1))
                link(v.tensor_scalar(QB[:, bass.ts(c, CH)], ring[b][:, 0:CH, D], 1.0, None, ALU.mult))
                if not (first and b == 0):
                    v.wait_ge(skept, 16 * c)
                norm_dve(v, link, act_in, act_out, c + 1, ring[b][:, :, 0:D], N2, t, h16[:, :, :]).then_inc(nready, 1)
                v.wait_ge(nready, c + 1)
                v.sem_inc(read, 1)
                sp_.vector(v, link, c, h16[:, 0:CH, :])
                v.tensor_scalar(S[:, bass.ts(c, CH), :], h16[:, 0:CH, :], 1.0, None, ALU.mult).then_inc(lk, 1)
                link.n += 1
                assert link.n == KL, (ph.name, link.n)
                v.wait_ge(lk, (c + 1) * KL)
            chunks(g, v, body)


def next_edges(g, B, WT, M, S, QB, table, kind, l, ph_name):
    N2 = 2 * CH
    W = g.W
    with Phase(g, ph_name) as ph:
        s = lambda n: ph.sem(n)
        got, copied, used, lk = ph.sem2("got"), s("copied"), s("used"), s("lk")
        sgot, sread, skept, xkept = ph.sem2("sgot"), s("sread"), s("skept"), s("xkept")
        zin, turned, flat, done, act_e, act_eo = s("zin"), s("turned"), s("flat"), s("done"), s("act_e"), s("act_eo")
        new, mready = s("new"), s("mready")
        nx = 2 if kind == "conv3" else 0
        ring = ph.sb2("ring", [P, CH, D])
        idxr = ph.sb2("idxr", [P, CH], I32)
        din = ph.sb2("din", [P, CH, D])
        xin = ph.sb2("xin", [P, N2, D + 1]) if nx else None
        st = ph.sb("st", [P, N2, D])
        agg = ph.sb("agg", [P, N2, D])
        aT = ph.sb("aT", [P, 512])
        y = ph.sb("y", [P, N2, D])
        psA, psD = ph.ps("psA"), ph.ps("psD")
        bias = {"conv2": 3, "conv3": 4, "gin": 5 + l}[kind]
        weight = {"conv2": g.root[0], "conv3": g.root[1], "gin": g.w3[l]}[kind]
        el = {"conv3": 0, "gin": l + 1}.get(kind)
        e = ph.sb("e", [P, N2, D])
        if kind in ("conv2", "conv3"):
            m = ph.sb("m", [P, N2, D])
        if kind == "conv2":
            sp_ = Spline(ph, g, WT, M)
        else:
            ea, eT, psX, psE = ph.sb("ea", [P, CH * 8]), ph.sb("eT", [64, P]), ph.ps("psX"), ph.ps("psE")
            mm = ph.sb("mm", [P, CH, D])
            ea_in, ea_t, ea_f, ea_d = s("ea_in"), s("ea_t"), s("ea_f"), s("ea_d")
        if kind == "conv3":
            t = norm_tiles(ph, N2)
            act_in, act_out, x3r = s("ln_in"), s("ln_out"), s("x3r")
            x3 = ph.sb("x3", [P, N2, D])
        block = ph.block()

        @block.gpsimd
        def _(pool):
            def free(p_, k, b):
                p_.wait_ge(used, 2 * k + b - 1)
            gather_chunks(g, pool, QB, idxr, copied, table, ring, got, free)

        @block.sync
        def _(sp):
            def load(k, b, first):
                c = 2 * k + b
                if not first:
                    sp.wait_ge(sread, c - 1)
                sp.dma_start(din[b][:, :, :], lin(g, g.dst_lin, c)).then_inc(sgot[b], 16)
                if nx:
                    sp.dma_start(xin[b][:, 0:CH, :], lin(g, g.x2s_lin, c)).then_inc(sgot[b], 16)
                    sp.dma_start(xin[b][:, CH:N2, :], lin(g, g.x2d_lin, c)).then_inc(sgot[b], 16)

            def store(k, b):
                c = 2 * k + b
                sp.wait_ge(new, c + 1)
                sp.dma_start(lin(g, g.dst_lin, c), y[:, CH:N2, :]).then_inc(skept, 16)
                if kind == "conv3":
                    sp.dma_start(lin(g, g.x3_lin, c), x3[:, CH:N2, :]).then_inc(skept, 16)
            ahead(g, load, store)
            sp.wait_ge(skept, (32 if kind == "conv3" else 16) * g.NCH)

        @block.scalar
        def _(act):
            def body(k, b, first):
                c = 2 * k + b
                if kind != "conv2":
                    if not (first and b == 0):
                        act.wait_ge(ea_t, c)
                    act.sem_inc(g.hop, 1)
                    act.copy(ea[:, :].rearrange("p (t f) -> p t f", f=8), g.rows_b[:, bass.ts(c, CH), 5:13]).then_inc(ea_in, 1)
                    act.wait_ge(ea_t, c + 1)
                    act.copy(eT[:, :], psX[0:64, 0:P]).then_inc(ea_f, 1)
                act.wait_ge(turned, c + 1)
                act.copy(aT[:, :], psA[:, :]).then_inc(flat, 1)
                if kind == "gin":
                    act.wait_ge(done, c + 1)
                    act.copy(e[:, :, :], psD[:, :].rearrange("p (t f) -> p t f", f=D)).then_inc(act_eo, 1)
                else:
                    act.wait_ge(act_e, c + 1)
                    act.activation(e[:, :, :], m[:, :, :], ACT.Exp).then_inc(act_eo, 1)
                if kind == "conv3":
                    norm_act(g, act, act_in, act_out, c + 1, N2, t)
                if kind == "conv2":
                    sp_.scalar(act, c)
            chunks(g, act, body)

        @block.tensor
        def _(pe):
            def body(k, b, first):
                c = 2 * k + b
                if kind != "conv2":
                    hold(g, pe, ea_in, c + 1)
                    pe.transpose(psX[0:64, 0:P], ea[:, :], g.ident[:, :]).then_inc(ea_t, 1)
                pe.wait_ge(zin, c + 1)
                src = agg if kind == "gin" else st
                for q in range(4):
                    ins = pe.transpose(psA[:, q * P:(q + 1) * P], src[:, 4 * q:4 * q + 4, :].rearrange("p t f -> p (t f)"), g.ident[:, :])
                ins.then_inc(turned, 1)
                pe.wait_ge(flat, c + 1)
                pe.matmul(psD[:, :], g.ones[0:1, :], over(g.bias[:, bias, :], 1, N2), start=True, stop=False, skip_group_check=True)
                for q in range(4):
                    ins = pe.matmul(psD[:, q * P:(q + 1) * P], aT[:, q * P:(q + 1) * P], weight[:, :], start=False, stop=False, skip_group_check=True)
                ins.then_inc(done, 1)
                if kind == "conv2":
                    sp_.tensor(pe, c, g.spline[1])
                else:
                    pe.wait_ge(ea_f, c + 1)
                    if not (first and b == 0):
                        pe.wait_ge(mready, c)
                    pe.matmul(psE[:, 0:256], g.ones[0:1, :], over(g.bias[:, 8 + el, :], 1, CH), start=True, stop=False, skip_group_check=True)
                    pe.matmul(psE[:, 0:256], eT[:, :], g.we[el][:, :], start=False, stop=False, skip_group_check=True).then_inc(ea_d, 1)
            chunks(g, pe, body)

        @block.vector
        def _(v):
            link = Link(v, lk)
            KL = {"conv2": 13, "conv3": 13, "gin": 4}[kind]

            def body(k, b, first):
                c = 2 * k + b
                link.at(c * KL)
                v.wait_ge(got[b], 16 * CH * (k + 1))
                v.wait_ge(sgot[b], 16 * (1 + nx) * (k + 1))
                Sc, Mc = S[:, bass.ts(c, CH), :], M[:, bass.ts(c, CH), :]
                if kind == "gin":
                    link.inc(v.tensor_tensor(agg[:, 0:CH, :], Sc, ring[b][:, :, :], ALU.add))
                    link(v.tensor_tensor(agg[:, CH:N2, :], Mc, din[b][:, :, :], ALU.add))
                    v.sem_inc(zin, 1)
                    v.sem_inc(used, 1)
                    v.sem_inc(sread, 1)
                    v.wait_ge(act_eo, c + 1)
                    if not (first and b == 0):
                        v.wait_ge(skept, 16 * c)
                    v.scalar_tensor_tensor(y[:, :, :], psD[:, :].rearrange("p (t f) -> p t f", f=D), 0.01, e[:, :, :],
                                           ALU.mult, ALU.max).then_inc(new, 1)
                else:
                    link.inc(v.tensor_scalar(st[:, 0:CH, :], Sc, 1.0, None, ALU.mult))
                    link(v.tensor_scalar(st[:, CH:N2, :], din[b][:, :, :], 1.0, None, ALU.mult))
                    v.sem_inc(zin, 1)
                    v.wait_ge(done, c + 1)
                    pd = psD[:, :].rearrange("p (t f) -> p t f", f=D)
                    link.inc(v.tensor_tensor(agg[:, 0:CH, :], pd[:, 0:CH, :], ring[b][:, :, :], ALU.add))
                    link(v.tensor_tensor(agg[:, CH:N2, :], pd[:, CH:N2, :], Mc, ALU.add))
                    v.sem_inc(used, 1)
                    v.tensor_scalar(m[:, :, :], agg[:, :, :], 0.0, None, ALU.min).then_inc(act_e, 1)
                    v.wait_ge(act_eo, c + 1)
                    link(v.scalar_tensor_tensor(agg[:, :, :], agg[:, :, :], 0.0, e[:, :, :], ALU.max, ALU.add))
                if kind == "conv2":
                    v.sem_inc(sread, 1)
                    if not (first and b == 0):
                        v.wait_ge(skept, 16 * c)
                    link(v.tensor_scalar(y[:, :, :], agg[:, :, :], -1.0, None, ALU.add))
                    v.sem_inc(new, 1)
                    sp_.vector(v, link, c, y[:, 0:CH, :])
                    v.tensor_scalar(S[:, bass.ts(c, CH), :], y[:, 0:CH, :], 1.0, None, ALU.mult).then_inc(lk, 1)
                    link.n += 1
                elif kind == "conv3":
                    if not (first and b == 0):
                        v.wait_ge(skept, 32 * c)
                    link(v.scalar_tensor_tensor(x3[:, :, :], agg[:, :, :], -1.0, xin[b][:, :, 0:D], ALU.add, ALU.add))
                    v.sem_inc(sread, 1)
                    norm_dve(v, link, act_in, act_out, c + 1, x3[:, :, :], N2, t, y[:, :, :]).then_inc(new, 1)
                if kind != "conv2":
                    v.wait_ge(new, c + 1)
                    v.wait_ge(ea_d, c + 1)
                    v.tensor_tensor(mm[:, :, :], psE[:, 0:256].rearrange("p (t f) -> p t f", f=D), y[:, 0:CH, :], ALU.add).then_inc(mready, 1)
                    v.wait_ge(mready, c + 1)
                    v.tensor_scalar(Mc, mm[:, :, :], 0.0, None, ALU.max).then_inc(lk, 1)
                    link.n += 1
                    link(v.tensor_scalar(Sc, y[:, 0:CH, :], 1.0, None, ALU.mult))
                assert link.n == KL, (ph.name, link.n)
                v.wait_ge(lk, (c + 1) * KL)
            chunks(g, v, body)


def last_edges(g, B, M, out):
    N, W = g.N, g.W
    with Phase(g, "out") as ph:
        s = lambda n: ph.sem(n)
        got, lk, zin, turned, flat, done, relu, made = ph.sem2("got"), s("lk"), s("zin"), s("turned"), s("flat"), s("done"), s("relu"), s("made")
        sent, leaky = ph.sem2("sent"), s("leaky")
        r = ph.sb("r", [P, CH, D])
        din, xin = ph.sb2("din", [P, CH, D]), ph.sb2("xin", [P, CH, D])
        agg, aT, y = ph.sb("agg", [P, CH, D]), ph.sb("aT", [P, 256]), ph.sb("y", [P, CH, D])
        rowr, idxr = ph.sb2("rowr", [P, CH, D]), ph.sb2("idxr", [P, CH], I32)
        psA, psD = ph.ps("psA"), ph.ps("psD")
        block = ph.block()

        @block.sync
        def _(sp):
            def load(k, b, first):
                c = 2 * k + b
                if not first:
                    sp.wait_ge(made, 2 * (c - 1))
                sp.dma_start(din[b][:, :, :], lin(g, g.dst_lin, c)).then_inc(got[b], 16)
                sp.dma_start(xin[b][:, :, :], lin(g, g.x3_lin, c)).then_inc(got[b], 16)
            chunks(g, sp, load)

        @block.gpsimd
        def _(pool):
            def scatter(k, b, first):
                c = 2 * k + b
                pool.wait_ge(made, 2 * c + 2)
                pool.sem_inc(g.hop, 1)
                for j in range(CH):
                    pool.indirect_dma_start(out=out, out_offset=bass.IndirectOffsetOnAxis(ap=idxr[b][:, j:j + 1], axis=0),
                                            in_=rowr[b][:, j, :], in_offset=None, bounds_check=N - 1, oob_is_err=False).then_inc(sent[b], 16)
            chunks(g, pool, scatter)
            both(g, pool, sent, 16 * CH)

        @block.scalar
        def _(act):
            def body(k, b, first):
                c = 2 * k + b
                act.wait_ge(turned, c + 1)
                act.copy(aT[:, :], psA[:, 0:256]).then_inc(flat, 1)
                act.wait_ge(done, c + 1)
                if not (first and b == 0):
                    act.wait_ge(made, 2 * c)
                act.copy(r[:, :, :], psD[:, 0:256].rearrange("p (t f) -> p t f", f=D)).then_inc(relu, 1)
            chunks(g, act, body)

        @block.tensor
        def _(pe):
            def body(k, b, first):
                c = 2 * k + b
                pe.wait_ge(zin, c + 1)
                for q in range(2):
                    ins = pe.transpose(psA[:, q * P:(q + 1) * P], agg[:, 4 * q:4 * q + 4, :].rearrange("p t f -> p (t f)"), g.ident[:, :])
                ins.then_inc(turned, 1)
                pe.wait_ge(flat, c + 1)
                if not (first and b == 0):
                    pe.wait_ge(leaky, c)
                pe.matmul(psD[:, 0:256], g.ones[0:1, :], over(g.bias[:, 7, :], 1, CH), start=True, stop=False, skip_group_check=True)
                for q in range(2):
                    ins = pe.matmul(psD[:, q * P:(q + 1) * P], aT[:, q * P:(q + 1) * P], g.w3[2][:, :], start=False, stop=False, skip_group_check=True)
                ins.then_inc(done, 1)
            chunks(g, pe, body)

        @block.vector
        def _(v):
            def body(k, b, first):
                c = 2 * k + b
                v.wait_ge(got[b], 32 * (k + 1))
                if not (first and b == 0):
                    v.wait_ge(turned, c)
                v.tensor_tensor(agg[:, :, :], M[:, bass.ts(c, CH), :], din[b][:, :, :], ALU.add).then_inc(zin, 1)
                if not first:
                    v.wait_ge(sent[b], 16 * CH * k)
                v.tensor_scalar(idxr[b][:, :], B.out[:, bass.ts(c, CH)], 1.0, None, ALU.mult).then_inc(made, 1)
                v.wait_ge(relu, c + 1)
                v.scalar_tensor_tensor(y[:, :, :], psD[:, 0:256].rearrange("p (t f) -> p t f", f=D), 0.01, r[:, :, :],
                                       ALU.mult, ALU.max).then_inc(leaky, 1)
                v.wait_ge(leaky, c + 1)
                v.tensor_tensor(rowr[b][:, :, :], y[:, :, :], xin[b][:, :, :], ALU.add).then_inc(made, 1)
            chunks(g, v, body)


def all_nodes(g, out):
    BN = 2 * CH
    q = g.NPART
    steps = g.NPER // BN
    with Phase(g, "nodes") as ph:
        s = lambda n: ph.sem(n)
        got, read, sent, cleared = ph.sem2("got"), s("read"), ph.sem2("sent"), s("cleared")
        lk, act_in, act_out, zin, turned, flat, done, act_e, act_eo, relu = (s(n) for n in (
            "lk", "ln_in", "ln_out", "zin", "turned", "flat", "done", "act_e", "act_eo", "relu"))
        xin, o = ph.sb2("xin", [P, BN, D + 1]), ph.sb2("o", [P, BN, D])
        t = norm_tiles(ph, BN)
        st, agg, m, e, x3, aT = ph.sb("st", [P, BN, D]), ph.sb("agg", [P, BN, D]), ph.sb("m", [P, BN, D]), ph.sb("e", [P, BN, D]), ph.sb("x3", [P, BN, D]), ph.sb("aT", [P, 512])
        psA, psD = ph.ps("psA"), ph.ps("psD")
        block = ph.block()
        n2 = g.nodes2.rearrange("(p n) f -> p n f", p=q)
        od = out.rearrange("(p n) f -> p n f", p=q)
        pd = psD[:, :].rearrange("p (t f) -> p t f", f=D)
        outd = s("outd")

        def sweep(eng, body):
            body(0, 0, True)
            body(0, 1, True)
            with eng.Fori(1, steps // 2) as k:
                body(k, 0, False)
                body(k, 1, False)

        @block.sync
        def _(sp):
            sp.wait_ge(cleared, 2)

            def load(k, b, first):
                if not first:
                    sp.wait_ge(read, 2 * k + b - 1)
                sp.dma_start(xin[b][0:q, :, :], n2[:, bass.ts(2 * k + b, BN), :]).then_inc(got[b], 16)

            def store(k, b):
                sp.wait_ge(outd, 2 * k + b + 1)
                sp.dma_start(od[:, bass.ts(2 * k + b, BN), :], o[b][0:q, :, :]).then_inc(sent[b], 16)
            load(0, 0, True)
            load(0, 1, True)
            with sp.Fori(0, steps // 2 - 1) as k:
                store(k, 0)
                load(k + 1, 0, False)
                store(k, 1)
                load(k + 1, 1, False)
            store(steps // 2 - 1, 0)
            store(steps // 2 - 1, 1)
            for b in range(2):
                sp.wait_ge(sent[b], 16 * (steps // 2))

        @block.scalar
        def _(act):
            def body(k, b, first):
                c = 2 * k + b
                norm_act(g, act, act_in, act_out, 2 * c + 1, BN, t)
                for i in range(5):
                    act.wait_ge(turned, 5 * c + i + 1)
                    act.copy(aT[:, :], psA[:, :]).then_inc(flat, 1)
                    if i < 2:
                        act.wait_ge(act_e, 2 * c + i + 1)
                        act.activation(e[:, :, :], m[:, :, :], ACT.Exp).then_inc(act_eo, 1)
                        if i == 1:
                            norm_act(g, act, act_in, act_out, 2 * c + 2, BN, t)
                    else:
                        act.wait_ge(done, 5 * c + i + 1)
                        act.copy(e[:, :, :], pd).then_inc(relu, 1)
            sweep(act, body)

        @block.tensor
        def _(pe):
            def body(k, b, first):
                c = 2 * k + b
                for i in range(5):
                    pe.wait_ge(zin, 6 * c + i + 1)
                    for j in range(4):
                        ins = pe.transpose(psA[:, j * P:(j + 1) * P], st[:, 4 * j:4 * j + 4, :].rearrange("p t f -> p (t f)"), g.ident[:, :])
                    ins.then_inc(turned, 1)
                    pe.wait_ge(flat, 5 * c + i + 1)
                    pe.matmul(psD[:, :], g.ones[0:1, :], over(g.bias[:, 3 + i, :], 1, BN), start=True, stop=False, skip_group_check=True)
                    w = (*g.root, *g.w3)[i]
                    for j in range(4):
                        ins = pe.matmul(psD[:, j * P:(j + 1) * P], aT[:, j * P:(j + 1) * P], w[:, :], start=False, stop=False, skip_group_check=True)
                    ins.then_inc(done, 1)
            sweep(pe, body)

        @block.vector
        def _(v):
            link = Link(v, lk)
            KL = 13
            v.memset(xin[0][:, :, :], 0.0).then_inc(cleared, 1)
            v.memset(xin[1][:, :, :], 0.0).then_inc(cleared, 1)

            def elu(c, i):
                v.wait_ge(done, 5 * c + i + 1)
                v.tensor_scalar(m[:, :, :], pd, 0.0, None, ALU.min).then_inc(act_e, 1)
                v.wait_ge(act_eo, 2 * c + i + 1)
                link(v.scalar_tensor_tensor(agg[:, :, :], pd, 0.0, e[:, :, :], ALU.max, ALU.add))

            def body(k, b, first):
                c = 2 * k + b
                link.at(c * KL)
                v.wait_ge(got[b], 16 * (k + 1))
                norm_dve(v, link, act_in, act_out, 2 * c + 1, xin[b][:, :, 0:D], BN, t, st[:, :, :]).then_inc(zin, 1)
                elu(c, 0)
                v.tensor_scalar(st[:, :, :], agg[:, :, :], -1.0, None, ALU.add).then_inc(zin, 1)
                elu(c, 1)
                link(v.scalar_tensor_tensor(x3[:, :, :], agg[:, :, :], -1.0, xin[b][:, :, 0:D], ALU.add, ALU.add))
                v.sem_inc(read, 1)
                norm_dve(v, link, act_in, act_out, 2 * c + 2, x3[:, :, :], BN, t, st[:, :, :]).then_inc(zin, 1)
                for i in range(3):
                    v.wait_ge(relu, 3 * c + i + 1)
                    v.scalar_tensor_tensor(st[:, :, :], pd, 0.01, e[:, :, :], ALU.mult, ALU.max).then_inc(zin, 1)
                v.wait_ge(zin, 6 * c + 6)
                if not first:
                    v.wait_ge(sent[b], 16 * k)
                v.tensor_tensor(o[b][:, :, :], st[:, :, :], x3[:, :, :], ALU.add).then_inc(outd, 1)
                assert link.n == KL, (ph.name, link.n)
            sweep(v, body)


def build(nc, a, out):
    E, N = a["src"].shape[0], a["x"].shape[0]
    g = Names()
    g.nc, g.E, g.N = nc, E, N
    g.W = -(-E // (P * CH)) * CH
    g.NP = P * g.W
    g.NCH = g.W // CH
    g.FULL, g.REST = E // g.W, E % g.W
    g.R0 = 256
    g.R1 = (N >> 8) + 2
    g.PADKEY = (g.R1 - 1) << 8
    g.CB, g.CA = 13, 2
    g.NPART = 125
    g.NPER = N // g.NPART
    assert g.NCH % 2 == 1 and g.NPER * g.NPART == N
    with ExitStack() as ctx:
        sb = lambda n, s, d=F32, c=ctx: c.enter_context(nc.sbuf_tensor(n, s, d))
        dram = lambda n, s, d=F32: nc.dram_tensor(n, s, d, kind="Internal").ap()
        g.hop = ctx.enter_context(nc.semaphore("hop"))
        g.b_mid, g.b_tab = dram("b_mid", [g.NP, g.CB]), dram("b_tab", [g.NP + 2, g.CB])
        g.a_mid, g.a_tab = dram("a_mid", [g.NP, g.CA]), dram("a_tab", [g.NP + 2, g.CA])
        g.nodes1, g.nodes2 = dram("nodes1", [N, D + 2]), dram("nodes2", [N, D + 1])
        g.xd_lin, g.xs_lin = dram("xd_lin", [g.NP, D + 2]), dram("xs_lin", [g.NP, D + 2])
        g.x1_lin = dram("x1_lin", [g.NP, D])
        g.x2s_lin, g.x2d_lin = dram("x2s_lin", [g.NP, D + 1]), dram("x2d_lin", [g.NP, D + 1])
        g.dst_lin, g.x3_lin = dram("dst_lin", [g.NP, D]), dram("x3_lin", [g.NP, D])
        g.tabs = [dram(f"tab{i}", [g.NP + 1, D]) for i in range(2)]
        g.agg_tab = dram("agg_tab", [g.NP + 1, D])

        g.iota16 = sb("iota16", [P, g.R1], F16)
        g.ident = sb("ident", [P, P])
        g.before, g.notbefore, g.ones16 = (sb(n, [P, P], F16) for n in ("before", "notbefore", "ones16"))
        g.ones = sb("ones", [P, P])
        g.zeros = sb("zeros", [P, g.R1])
        g.zerow = g.zeros[:, 0:g.W]
        assert g.R1 >= g.W
        g.eps = sb("eps", [P, 1])
        g.beta = sb("beta", [P, 1])
        g.alone = sb("alone", [P, D])
        g.w0a, g.w0b = sb("w0a", [P, 2 * P]), sb("w0b", [P, 2 * D])
        g.w1s, g.w1d, g.w2 = (sb(n, [P, P]) for n in ("w1s", "w1d", "w2"))
        g.root = [sb(f"root{i}", [P, P]) for i in range(2)]
        g.w3 = [sb(f"w3_{i}", [P, P]) for i in range(3)]
        g.we = [sb(f"we{i}", [64, 256]) for i in range(3)]
        g.bias = sb("bias", [1, 11, D])
        g.bn = sb("bn", [P, 4, D])
        g.b0col = sb("b0col", [P, 1])
        g.spline = [sb(f"spline{i}", [3 * D, 9, D]) for i in range(2)]
        g.rows_b = sb("rows_b", [P, g.W, g.CB])

        def flags(n, column, c=ctx):
            f = Names()
            f.column = column
            f.same, f.last, f.pfx = (sb(f"{n}_{k}", [P, g.W], F32, c) for k in ("same", "last", "pfx"))
            f.other, f.own, f.out = (sb(f"{n}_{k}", [P, g.W], I32, c) for k in ("other", "own", "out"))
            return f
        B = flags("b", 1)
        with ExitStack() as c1:
            g.rows_a = sb("rows_a", [P, g.W, g.CA], F32, c1)
            A = flags("a", 0, c1)
            load_weights(g, a)
            first_rows(g, a)
            sort_edges(g, "b", g.rows_b, g.CB, g.b_mid, g.b_tab, node_table_filler(g, a))
            sort_edges(g, "a", g.rows_a, g.CA, g.a_mid, g.a_tab, None)
            places(g, "b", g.rows_b, g.b_tab, B)
            places(g, "a", g.rows_a, g.a_tab, A)
            QA = sb("QA", [P, g.W], I32, c1)
            PB = sb("PB", [P, g.W], F32, c1)
            H = sb("H", [P, g.W, D], F32, c1)
            layer0_edges(g, A, H, QA)
            fill_back(g, A, H)
            Z = sb("Z", [P, g.W, D], F32, c1)
            layer01_edges(g, A, H, QA, Z, PB)
            layer1_rest(g, A, H, Z, PB)
        all_nodes(g, out)
        WT = sb("WT", [P, g.W, 9])
        QB = sb("QB", [P, g.W], I32)
        spline_weights(g, WT)
        inv = sb("inv", [P, g.W, 1])
        M = sb("M", [P, g.W, D])
        S = sb("S", [P, g.W, D])
        conv1_edges(g, B, WT, M, S, QB)
        close_segments(g, B, M, g.tabs[0], "s1", count=inv, scale=inv)
        next_edges(g, B, WT, M, S, QB, g.tabs[0], "conv2", 0, "c2")
        close_segments(g, B, M, g.tabs[1], "s2", scale=inv)
        next_edges(g, B, WT, M, S, QB, g.tabs[1], "conv3", 0, "c3")
        close_segments(g, B, M, g.tabs[0], "s3")
        next_edges(g, B, WT, M, S, QB, g.tabs[0], "gin", 0, "g0")
        close_segments(g, B, M, g.tabs[1], "s4")
        next_edges(g, B, WT, M, S, QB, g.tabs[1], "gin", 1, "g1")
        close_segments(g, B, M, g.tabs[0], "s5")
        last_edges(g, B, M, out)


_INS = ['x', 'src', 'dst', 'edge_attr_3', 'edge_attr_8', 'L0_gnn_beta', 'L0_gnn_W1', 'L0_gnn_b1', 'L0_gnn_W2', 'L0_gnn_b2', 'L1_gnn_W1', 'L1_gnn_b1', 'L1_gnn_gamma1', 'L1_gnn_beta1', 'L1_gnn_W2', 'L1_gnn_b2', 'L1_gnn_gamma2', 'L1_gnn_beta2', 'L2_gnn_w1', 'L2_gnn_root1', 'L2_gnn_b1', 'L2_gnn_w2', 'L2_gnn_root2', 'L2_gnn_b2', 'L3_gnn_W', 'L3_gnn_b', 'L3_gnn_We', 'L3_gnn_be']
_OUTS = [((100000, 32), 'float32')]


def kernel(**inputs):
    import numpy as _np
    import concourse.bacc as _bacc
    from concourse import mybir as _mybir
    from concourse.bass_utils import run_bass_kernel_spmd as _run
    nc = _bacc.Bacc("TRN2", target_bir_lowering=False, num_devices=1)
    arrays, args = {}, {}
    for name in _INS:
        v = _np.ascontiguousarray(inputs[name])
        arrays[f"in_{name}_dram"] = v
        args[name] = nc.dram_tensor(f"in_{name}_dram", v.shape, _mybir.dt.from_np(v.dtype), kind="ExternalInput").ap()
    outs = []
    for i, (shape, dtype) in enumerate(_OUTS):
        dt = _mybir.dt.from_np(_np.dtype(dtype))
        outs.append(nc.dram_tensor(f"out_{i}_dram", shape, dt, kind="ExternalOutput").ap())
    build(nc, args, *outs)
    r = _run(nc, [arrays], core_ids=[0])
    return r.results[0]["out_0_dram"]
```

```python
from contextlib import ExitStack

import concourse.bass as bass
from concourse import mybir

F32 = mybir.dt.float32
F16 = mybir.dt.float16
I32 = mybir.dt.int32
ALU = mybir.AluOpType
ACT = mybir.ActivationFunctionType
AX = mybir.AxisListType

P = 128
D = 32
CH = 8
BIG = 1.0e30
FAR = 8388608.0


class Names:
    pass


class Link:

    def __init__(self, eng, sem):
        self.eng, self.sem, self.base, self.n = eng, sem, 0, 0

    def at(self, base):
        self.base, self.n = base, 0

    def inc(self, ins):
        self.n += 1
        ins.then_inc(self.sem, 1)

    def __call__(self, ins):
        self.inc(ins)
        self.eng.wait_ge(self.sem, self.base + self.n)


def hold(g, eng, sem, value):
    eng.wait_ge(sem, value)
    eng.sem_inc(g.hop, 1)


def over(ap, axis, n):
    ap = ap.unsqueeze(axis)
    shape = list(ap.shape)
    shape[axis] = n
    return ap.broadcast_to(shape)


def chunks(g, eng, body):
    body(0, 0, True)
    body(0, 1, True)
    with eng.Fori(1, g.NCH // 2) as k:
        body(k, 0, False)
        body(k, 1, False)
    body(g.NCH // 2, 0, False)


def ahead(g, load, store):
    load(0, 0, True)
    load(0, 1, True)
    last = g.NCH // 2
    with g.nc.sync.Fori(0, last - 1) as k:
        store(k, 0)
        load(k + 1, 0, False)
        store(k, 1)
        load(k + 1, 1, False)
    store(last - 1, 0)
    load(last, 0, False)
    store(last - 1, 1)
    store(last, 0)


def both(g, eng, sems, per):
    for b in range(2):
        eng.wait_ge(sems[b], per * ((g.NCH + 1 - b) // 2))


class Phase:

    def __init__(self, g, name):
        self.g, self.nc, self.name, self.ctx, self.sems = g, g.nc, name, ExitStack(), []

    def __enter__(self):
        self.ctx.__enter__()
        return self

    def __exit__(self, *a):
        done = self.ctx.__exit__(*a)
        if a[0] is None:
            self.nc.clear_and_free_semaphores(self.sems)
            self.nc.all_engine_barrier()
        return done

    def sb(self, n, s, d=F32):
        return self.ctx.enter_context(self.nc.sbuf_tensor(f"{self.name}_{n}", s, d))

    def sb2(self, n, s, d=F32):
        return [self.sb(f"{n}{i}", s, d) for i in range(2)]

    def ps(self, n, s=(P, 512), d=F32):
        return self.ctx.enter_context(self.nc.psum_tensor(f"{self.name}_{n}", list(s), d))

    def sem(self, n):
        self.sems.append(self.nc.alloc_semaphore(name=f"{self.name}_{n}"))
        return self.sems[-1]

    def sem2(self, n):
        return [self.sem(f"{n}{i}") for i in range(2)]

    def block(self):
        return self.ctx.enter_context(self.nc.Block())


def load_weights(g, a):
    with Phase(g, "prep") as ph:
        made, loaded, cleared = ph.sem("made"), ph.sem("loaded"), ph.sem("cleared")
        blank, mlp0, mlp1, filled = ph.sem("blank"), ph.sem("mlp0"), ph.sem("mlp1"), ph.sem("filled")
        psc = ph.ps("psc")
        rb1 = ph.sb("rb1", [2 * D, 1])
        rb1w = ph.sb("rb1w", [2 * D, P])
        w2c = ph.sb("w2c", [2 * D, D])
        block = ph.block()
        loads = []

        def diagonal(dst, src, rows, cols, times):
            for t in range(times):
                loads.append((dst[t * rows:(t + 1) * rows, t * cols:(t + 1) * cols], src))

        diagonal(g.w0a, a["L0_gnn_W1"], D, 2 * D, 4)
        diagonal(g.w0b, a["L0_gnn_W2"], 2 * D, D, 2)
        diagonal(g.w1s, a["L1_gnn_W1"][0:D, :], D, D, 4)
        diagonal(g.w1d, a["L1_gnn_W1"][D:2 * D, :], D, D, 4)
        diagonal(g.w2, a["L1_gnn_W2"], D, D, 4)
        diagonal(g.root[0], a["L2_gnn_root1"], D, D, 4)
        diagonal(g.root[1], a["L2_gnn_root2"], D, D, 4)
        for l in range(3):
            diagonal(g.w3[l], a["L3_gnn_W"][l], D, D, 4)
            diagonal(g.we[l], a["L3_gnn_We"][l], 8, D, 8)
        for n, ap in enumerate([a["L0_gnn_b2"], a["L1_gnn_b1"], a["L1_gnn_b2"], a["L2_gnn_b1"], a["L2_gnn_b2"],
                                *[a["L3_gnn_b"][l] for l in range(3)], *[a["L3_gnn_be"][l] for l in range(3)]]):
            loads.append((g.bias[:, n, :], ap.unsqueeze(0)))
        for n, ap in enumerate([a["L1_gnn_gamma1"], a["L1_gnn_beta1"], a["L1_gnn_gamma2"], a["L1_gnn_beta2"]]):
            loads.append((g.bn[:, n, :], over(ap, 0, P)))
        for t in range(2):
            loads.append((g.b0col[t * 2 * D:(t + 1) * 2 * D, :], a["L0_gnn_b1"].unsqueeze(1)))
        for n, ap in enumerate([a["L2_gnn_b1"], a["L2_gnn_b2"], *[a["L3_gnn_b"][l] for l in range(3)]]):
            for t in range(4):
                loads.append((g.bcols[t * D:(t + 1) * D, n:n + 1], ap.unsqueeze(1)))
        loads.append((g.beta[:, :], over(a["L0_gnn_beta"], 0, P)))
        loads.append((w2c[:, :], a["L0_gnn_W2"]))
        for c, w in enumerate((a["L2_gnn_w1"], a["L2_gnn_w2"])):
            wv = w.rearrange("(z j) i o -> z i j o", z=3)
            for z in range(3):
                loads.append((g.spline[c][z * D:(z + 1) * D, :, :], wv[z]))

        @block.sync
        def _(sp):
            sp.wait_ge(cleared, 1)
            for dst, src in loads:
                with g.nc.allow_non_contiguous_dma(reason="columns and small blocks of weights"):
                    sp.dma_start(dst, src).then_inc(loaded, 16)

        @block.gpsimd
        def _(pool):
            pool.iota(g.iota16[:, :], [[1, g.R1]], base=0, channel_multiplier=0,
                      allow_small_or_imprecise_dtypes=True).then_inc(made, 1)
            pool.memset(g.ident[:, :], 0.0).then_inc(blank, 1)
            pool.memset(g.before[:, :], 1.0).then_inc(blank, 1)
            pool.memset(g.notbefore[:, :], 1.0).then_inc(blank, 1)
            pool.wait_ge(blank, 3)
            pool.affine_select(out=g.ident[:, :], in_=g.ident[:, :], pattern=[[1, P]], compare_op=ALU.not_equal,
                               fill=1.0, base=0, channel_multiplier=-1).then_inc(made, 1)
            pool.affine_select(out=g.before[:, :], in_=g.before[:, :], pattern=[[1, P]], compare_op=ALU.is_gt,
                               fill=0.0, base=0, channel_multiplier=-1).then_inc(made, 1)
            pool.affine_select(out=g.notbefore[:, :], in_=g.notbefore[:, :], pattern=[[-1, P]],
                               compare_op=ALU.is_ge, fill=0.0, base=0, channel_multiplier=1).then_inc(made, 1)

        @block.vector
        def _(v):
            link = Link(v, filled)
            for t in (g.w0a, g.w0b, g.w1s, g.w1d, g.w2, *g.root, *g.w3, *g.we):
                link.inc(v.memset(t[:, :], 0.0))
            link.inc(v.memset(g.ones16[:, :], 1.0))
            link(v.memset(g.mean[:, :], 0.0))
            for t in range(4):
                link(v.memset(g.mean[t * D:(t + 1) * D, t * D:(t + 1) * D], 1.0 / D))
            v.wait_ge(made, 2)
            link(v.tensor_tensor(g.center[:, :], g.ident[:, :], g.mean[:, :], ALU.subtract))
            link.inc(v.memset(g.ones[:, :], 1.0))
            link.inc(v.memset(g.eps[:, :], 1e-5))
            link(v.memset(g.zeros[:, :], 0.0))
            v.sem_inc(cleared, 1)
            v.wait_ge(loaded, 16 * len(loads))
            link(v.tensor_scalar(rb1[:, :], g.b0col[0:2 * D, :], 0.0, None, ALU.max))
            v.tensor_copy(rb1w[:, :], rb1[:, 0:1].broadcast_to([2 * D, P])).then_inc(mlp0, 1)
            v.wait_ge(mlp1, 1)
            link(v.tensor_copy(g.alone[:, :], psc[:, 0:D]))

        @block.tensor
        def _(pe):
            pe.wait_ge(mlp0, 1)
            pe.matmul(psc[:, 0:D], rb1w[:, :], w2c[:, :], start=True, stop=False)
            pe.matmul(psc[:, 0:D], g.ones[0:1, :], g.bias[:, 0, :], start=False, stop=True).then_inc(mlp1, 1)


def digits_of(g, ph, v, link, rows, dg, name):
    W = g.W
    key_i, dig_i, digit = ph.sb(f"{name}_key", [P, W], I32), ph.sb(f"{name}_bits", [P, W], I32), ph.sb(name, [P, W + 2])

    def make():
        link(v.memset(digit[:, W:W + 2], 0.0))
        link(v.tensor_copy(key_i[:, :], rows[:, :, 0]))
        if dg == 0:
            link(v.tensor_scalar(dig_i[:, :], key_i[:, :], g.R0 - 1, None, ALU.bitwise_and))
        else:
            link(v.tensor_scalar(dig_i[:, :], key_i[:, :], 8, None, ALU.arith_shift_right))
        link(v.tensor_copy(digit[:, 0:W], dig_i[:, :]))
    return digit, make


def starts(g, v, link, hist, counts, R):
    link(v.tensor_copy(hist[:, 0:R], counts[:, 0:R]))
    link(v.memset(g.starts[:, 0:1], 0.0))
    link(v.tensor_tensor_scan(g.starts[:, 1:R + 1], g.zeros[:, 0:R], hist[:, 0:R], 0.0, ALU.add, ALU.add))


def first_count(g, rows, fill):
    R = g.R0
    with Phase(g, "count") as ph:
        chain, hot, counted = ph.sem("chain"), ph.sem("hot"), ph.sem("counted")
        hist = ph.sb("hist", [P, R])
        onehot = ph.sb2("onehot", [P, R], F16)
        counts = ph.ps("counts")
        extra = fill(ph)
        block = ph.block()

        @block.sync
        def _(sp):
            extra.sync(sp)

        @block.gpsimd
        def _(pool):
            extra.gpsimd(pool)

        @block.tensor
        def _(pe):
            def count(k, b, first):
                for j in range(CH):
                    pe.wait_ge(hot, (2 * k + b) * CH + j + 1)
                    pe.matmul(counts[:, 0:R], g.ones16[:, :], onehot[j % 2][:, :], start=first and b == 0 and j == 0, stop=False,
                              skip_group_check=True).then_inc(counted, 1)
            chunks(g, pe, count)

        @block.vector
        def _(v):
            link = Link(v, chain)
            digit, make = digits_of(g, ph, v, link, rows, 0, "digit")
            make()

            def mark(k, b, first):
                for j in range(CH):
                    c = (2 * k + b) * CH + j
                    if not (first and b == 0 and j < 2):
                        v.wait_ge(counted, c - 1)
                    v.tensor_scalar(onehot[j % 2][:, :], g.iota16[:, 0:R], digit[:, bass.ds(c, 1)], None,
                                    ALU.is_equal).then_inc(hot, 1)
            chunks(g, v, mark)
            v.wait_ge(counted, g.W)
            starts(g, v, link, hist, counts, R)


def sort_pass(g, name, rows, C, dg, dest, next_rows, next_dg):
    W, R = g.W, (g.R0, g.R1)[dg]
    RN = (g.R0, g.R1)[next_dg] if next_rows is not None else 0
    with Phase(g, name) as ph:
        chain, based = ph.sem("chain"), ph.sem("base")
        hot, ranked, picked, placed = ph.sem("hot"), ph.sem("ranked"), ph.sem("picked"), ph.sem("placed")
        next_hot, next_counted = ph.sem("next_hot"), ph.sem("next_counted")
        idx_ready, rows_ready, reloaded = ph.sem("idx"), ph.sem("rows"), ph.sem("reloaded")
        sent = ph.sem2("sent")
        hist = ph.sb("hist", [P, g.R1])
        onehot = [ph.sb(f"onehot{i}", [P, R], F16) for i in range(4)]
        next_onehot = ph.sb2("next_onehot", [P, g.R1], F16)
        junk = ph.sb2("junk", [P, R])
        rank8 = ph.sb2("rank", [P, CH])
        rank_i = ph.sb("rank_i", [P, 3, CH], I32)
        idxr = ph.sb2("idxr", [P, CH], I32)
        rowr = ph.sb2("rowr", [P, CH, C])
        place = [ph.ps(f"place{i}")[:, 0:R] for i in range(2)]
        counts = ph.ps("counts")
        block = ph.block()

        @block.sync
        def _(sp):
            both(g, sp, sent, 16 * CH)
            t = dest if dg == 0 else dest[1:g.NP + 1, :]
            sp.dma_start(rows[:, :, :], t.rearrange("(p w) c -> p w c", w=W)).then_inc(reloaded, 16)
            sp.wait_ge(reloaded, 16)

        @block.gpsimd
        def _(pool):
            def scatter(k, b, first):
                pool.wait_ge(rows_ready, 2 * k + b + 1)
                pool.wait_ge(idx_ready, 2 * k + b + 1)
                pool.sem_inc(g.hop, 1)
                for j in range(CH):
                    pool.indirect_dma_start(out=dest, out_offset=bass.IndirectOffsetOnAxis(ap=idxr[b][:, j:j + 1], axis=0),
                                            in_=rowr[b][:, j, :], in_offset=None).then_inc(sent[b], 16)
            chunks(g, pool, scatter)

        @block.scalar
        def _(act):
            def copy(k, b, first):
                if not first:
                    hold(g, act, sent[b], 16 * CH * k)
                act.copy(rowr[b][:, :, :], rows[:, bass.ts(2 * k + b, CH), :]).then_inc(rows_ready, 1)
            chunks(g, act, copy)

        @block.tensor
        def _(pe):
            for i in range(2):
                ins = pe.matmul(place[i], g.ident[:, :], g.starts[:, 0:R], start=True, stop=False, skip_group_check=True)
            ins.then_inc(based, 1)

            def rank(k, b, first):
                for j in range(CH):
                    c = (2 * k + b) * CH + j
                    start = first and b == 0 and j == 0
                    pe.wait_ge(hot, c + 1)
                    pe.matmul(place[j % 2], g.before[:, :], onehot[j % 4][:, :], start=False, stop=False,
                              skip_group_check=True).then_inc(ranked, 1)
                    if not start:
                        pe.wait_ge(picked, c)
                        pe.matmul(place[(j + 1) % 2], g.notbefore[:, :], onehot[(j + 3) % 4][:, :], start=False, stop=False,
                                  skip_group_check=True).then_inc(placed, 1)
                    pe.matmul(place[(j + 1) % 2], g.ones16[:, :], onehot[j % 4][:, :], start=False, stop=False,
                              skip_group_check=True)
                    if RN:
                        pe.wait_ge(next_hot, c + 1)
                        pe.matmul(counts[:, 0:RN], g.ones16[:, :], next_onehot[j % 2][:, 0:RN], start=start, stop=False,
                                  skip_group_check=True).then_inc(next_counted, 1)
            chunks(g, pe, rank)

        @block.vector
        def _(v):
            link = Link(v, chain)
            digit, make = digits_of(g, ph, v, link, rows, dg, "digit")
            make()
            if RN:
                next_digit, make_next = digits_of(g, ph, v, link, next_rows, next_dg, "next_digit")
                make_next()
            after = link.n

            def mark(i, c):
                v.tensor_scalar(onehot[i % 4][:, :], g.iota16[:, 0:R], digit[:, bass.ds(c, 1)], None,
                                ALU.is_equal).then_inc(hot, 1)
            mark(0, 0)
            mark(1, 1)
            v.wait_ge(based, 1)

            def place_chunk(k, b, first):
                t = 2 * k + b
                for j in range(CH):
                    c = t * CH + j
                    if not (first and b == 0 and j < 2):
                        v.wait_ge(placed, c - 1)
                    mark(j + 2, c + 2)
                    if RN:
                        if not (first and b == 0 and j < 2):
                            v.wait_ge(next_counted, c - 1)
                        v.tensor_scalar(next_onehot[j % 2][:, 0:RN], g.iota16[:, 0:RN], next_digit[:, bass.ds(c, 1)], None,
                                        ALU.is_equal).then_inc(next_hot, 1)
                    v.wait_ge(ranked, c + 1)
                    v.tensor_tensor_reduce(junk[j % 2][:, :], place[j % 2], onehot[j % 4][:, :], 1.0, 0.0, ALU.mult, ALU.add,
                                           rank8[b][:, j:j + 1]).then_inc(picked, 1)
                v.wait_ge(picked, (t + 1) * CH)
                if not first:
                    v.wait_ge(sent[b], 16 * CH * k)
                if dg == 0:
                    link.at(t * 3 + after)
                    link(v.tensor_copy(rank_i[:, 0, :], rank8[b][:, :]))
                    link(v.tensor_scalar(rank_i[:, 1, :], rank_i[:, 0, :], P - 1, None, ALU.bitwise_and))
                    link(v.tensor_scalar(rank_i[:, 2, :], rank_i[:, 0, :], 7, None, ALU.arith_shift_right))
                    v.scalar_tensor_tensor(idxr[b][:, :], rank_i[:, 1, :], float(W), rank_i[:, 2, :], ALU.mult,
                                           ALU.add).then_inc(idx_ready, 1)
                else:
                    v.tensor_scalar(idxr[b][:, :], rank8[b][:, :], 1.0, None, ALU.add).then_inc(idx_ready, 1)
            chunks(g, v, place_chunk)
            if RN:
                v.wait_ge(next_counted, W)
                link.at((g.NCH * 3 if dg == 0 else 0) + after)
                starts(g, v, link, hist, counts, RN)


def first_rows(g, a):
    W, FULL, REST, E = g.W, g.FULL, g.REST, g.E
    with Phase(g, "rows") as ph:
        padded, loaded, done = ph.sem("padded"), ph.sem("loaded"), ph.sem("done")
        guarded, stored = ph.sem("guarded"), ph.sem("stored")
        raw_i = ph.sb("raw_i", [P, 2, W], I32)
        raw3 = ph.sb("raw3", [P, W, 3])
        raw8 = ph.sb("raw8", [P, W, 8])
        guard = ph.sb("guard", [1, 2, g.CB])
        block = ph.block()

        @block.sync
        def _(sp):
            sp.wait_ge(padded, 3)
            for t, d in ((raw_i[:, 0, :], a["dst"]), (raw_i[:, 1, :], a["src"])):
                sp.dma_start(t[0:FULL], d[0:FULL * W].rearrange("(p w) -> p w", w=W)).then_inc(loaded, 16)
                sp.dma_start(t[FULL:FULL + 1, 0:REST], d[FULL * W:E].rearrange("(p w) -> p w", p=1)).then_inc(loaded, 16)
            for t, d in ((raw3, a["edge_attr_3"]), (raw8, a["edge_attr_8"])):
                sp.dma_start(t[0:FULL, :, :], d[0:FULL * W, :].rearrange("(p w) c -> p w c", w=W)).then_inc(loaded, 16)
                sp.dma_start(t[FULL:FULL + 1, 0:REST, :], d[FULL * W:E, :].rearrange("(p w) c -> p w c", p=1)).then_inc(loaded, 16)
            sp.wait_ge(guarded, 2)
            for tab, C in ((g.b_tab, g.CB), (g.a_tab, g.CA)):
                sp.dma_start(tab[0:1, :], guard[:, 0, 0:C]).then_inc(stored, 16)
                sp.dma_start(tab[g.NP + 1:g.NP + 2, :], guard[:, 1, 0:C]).then_inc(stored, 16)
            sp.wait_ge(stored, 16 * 4)

        @block.vector
        def _(v):
            v.memset(raw_i[:, :, :], g.PADKEY).then_inc(padded, 1)
            v.memset(raw3[:, :, :], 0.0).then_inc(padded, 1)
            v.memset(raw8[:, :, :], 0.0).then_inc(padded, 1)
            v.memset(guard[:, 0, :], -1.0).then_inc(guarded, 1)
            v.memset(guard[:, 1, :], -2.0).then_inc(guarded, 1)
            v.wait_ge(loaded, 16 * 8)
            v.tensor_copy(g.rows_b[:, :, 0], raw_i[:, 0, :]).then_inc(done, 1)
            v.tensor_copy(g.rows_b[:, :, 1], raw_i[:, 1, :]).then_inc(done, 1)
            v.tensor_copy(g.rows_a[:, :, 0], raw_i[:, 1, :]).then_inc(done, 1)
            v.tensor_copy(g.rows_a[:, :, 1], raw_i[:, 0, :]).then_inc(done, 1)

        @block.scalar
        def _(act):
            act.wait_ge(loaded, 16 * 8)
            act.copy(g.rows_b[:, :, 2:5], raw3[:, :, :]).then_inc(done, 1)
            act.copy(g.rows_b[:, :, 5:13], raw8[:, :, :]).then_inc(done, 1)


def node_table_filler(g, a):
    def fill(ph):
        x2 = a["x"].rearrange("(p n) f -> p n f", p=g.NPART)
        t2 = g.nodes1.rearrange("(p n) f -> p n f", p=g.NPART)
        BN = 40
        steps = g.NPER // BN
        xin = ph.sb2("xin", [P, BN, D])
        xout = ph.sb2("xout", [P, BN, D + 2])
        got, made, wrote, none = ph.sem2("got"), ph.sem("made"), ph.sem2("wrote"), ph.sem("none")
        e = Names()

        def steps_of(eng, body):
            body(0, 0, True)
            body(0, 1, True)
            with eng.Fori(1, steps // 2) as k:
                body(k, 0, False)
                body(k, 1, False)

        def sync(sp):
            def load(k, b, first):
                if not first:
                    sp.wait_ge(made, 2 * k + b - 1)
                sp.dma_start(xin[b][0:g.NPART, :, :], x2[:, bass.ts(2 * k + b, BN), :]).then_inc(got[b], 16)

            def store(k, b):
                sp.wait_ge(made, 2 * k + b + 1)
                sp.dma_start(t2[:, bass.ts(2 * k + b, BN), :], xout[b][0:g.NPART, :, :]).then_inc(wrote[b], 16)
            load(0, 0, True)
            load(0, 1, True)
            with sp.Fori(0, steps // 2 - 1) as k:
                store(k, 0)
                load(k + 1, 0, False)
                store(k, 1)
                load(k + 1, 1, False)
            store(steps // 2 - 1, 0)
            store(steps // 2 - 1, 1)
            for b in range(2):
                sp.wait_ge(wrote[b], 16 * (steps // 2))

        def gpsimd(pool):
            pool.memset(xout[0][:, :, D:D + 2], float(g.NP)).then_inc(none, 1)
            pool.memset(xout[1][:, :, D:D + 2], float(g.NP)).then_inc(none, 1)
            pool.wait_ge(none, 2)

            def copy(k, b, first):
                pool.wait_ge(got[b], 16 * (k + 1))
                if not first:
                    pool.wait_ge(wrote[b], 16 * k)
                pool.sem_inc(g.hop, 1)
                pool.tensor_copy(xout[b][0:g.NPART, :, 0:D], xin[b][0:g.NPART, :, :]).then_inc(made, 1)
            steps_of(pool, copy)
        e.sync, e.gpsimd = sync, gpsimd
        return e
    return fill


def places(g, which, rows, tab, E_):
    W, N = g.W, g.N
    with Phase(g, f"place{which}") as ph:
        edged, chain, flagged = ph.sem("edged"), ph.sem("chain"), ph.sem("flagged")
        copied, sent, vals = ph.sem("copied"), ph.sem2("sent"), ph.sem("vals")
        before = ph.sb("prev", [P, 1])
        after = ph.sb("next", [P, 1])
        tmp = ph.sb("tmp", [P, W])
        place = ph.sb("placev", [P, W], F32)
        elem = ph.sb("elem", [P, W], I32)
        idxr = ph.sb2("idxr", [P, CH], I32)
        valr = ph.sb2("valr", [P, CH])
        iot = ph.sem("iota")
        block = ph.block()
        flat = g.nodes1.rearrange("n (f o) -> (n f) o", o=1)

        @block.sync
        def _(sp):
            with g.nc.allow_non_contiguous_dma(reason="one key a partition"):
                sp.dma_start(before[:, :], tab[0:g.NP, 0:1].rearrange("(p w) c -> p w c", w=W)[:, 0, :]).then_inc(edged, 16)
                sp.dma_start(after[:, :], tab[2:g.NP + 2, 0:1].rearrange("(p w) c -> p w c", w=W)[:, W - 1, :]).then_inc(edged, 16)

        @block.vector
        def _(v):
            link = Link(v, chain)
            key, other = rows[:, :, 0], rows[:, :, 1]
            link.inc(v.tensor_tensor(E_.same[:, 1:W], key[:, 1:W], key[:, 0:W - 1], ALU.is_equal))
            link.inc(v.tensor_tensor(E_.last[:, 0:W - 1], key[:, 1:W], key[:, 0:W - 1], ALU.not_equal))
            v.wait_ge(edged, 32)
            link.inc(v.tensor_tensor(E_.same[:, 0:1], key[:, 0:1], before[:, :], ALU.is_equal))
            link(v.tensor_tensor(E_.last[:, W - 1:W], key[:, W - 1:W], after[:, :], ALU.not_equal))
            link(v.tensor_tensor_scan(E_.pfx[:, :], E_.same[:, :], g.zerow[:, :], 1.0, ALU.mult, ALU.add))
            link(v.tensor_scalar(E_.other[:, :], other, float(N - 1), None, ALU.min))
            link(v.tensor_scalar(E_.own[:, :], key, float(N - 1), None, ALU.min))
            link(v.tensor_scalar(tmp[:, :], E_.last[:, :], -FAR, FAR, ALU.mult, ALU.add))
            link(v.tensor_tensor(E_.out[:, :], tmp[:, :], key, ALU.add))
            link(v.scalar_tensor_tensor(tmp[:, :], key, float(D + 2), tmp[:, :], ALU.mult, ALU.add))
            v.tensor_scalar(elem[:, :], tmp[:, :], float(D + E_.column), None, ALU.add).then_inc(flagged, 1)

        @block.gpsimd
        def _(pool):
            pool.iota(place[:, :], [[1, W]], base=0, channel_multiplier=W, allow_small_or_imprecise_dtypes=True).then_inc(iot, 1)
            pool.wait_ge(iot, 1)
            pool.wait_ge(flagged, 1)

            def scatter(k, b, first):
                c = 2 * k + b
                if not first:
                    hold(g, pool, sent[b], 16 * CH * k)
                pool.tensor_copy(idxr[b][:, :], elem[:, bass.ts(c, CH)]).then_inc(copied, 1)
                pool.tensor_copy(valr[b][:, :], place[:, bass.ts(c, CH)]).then_inc(copied, 1)
                pool.wait_ge(copied, 2 * c + 2)
                pool.sem_inc(g.hop, 1)
                for j in range(CH):
                    pool.indirect_dma_start(out=flat, out_offset=bass.IndirectOffsetOnAxis(ap=idxr[b][:, j:j + 1], axis=0),
                                            in_=valr[b][:, j:j + 1], in_offset=None, bounds_check=N * (D + 2) - 1,
                                            oob_is_err=False).then_inc(sent[b], 16)
            chunks(g, pool, scatter)
            both(g, pool, sent, 16 * CH)


def norm_dve(v, link, act_in, act_out, count, x, n, t, out):
    link(v.tensor_reduce(t.s[:, 0:n], x, AX.X, ALU.add))
    link(v.tensor_scalar(t.s[:, 0:n], t.s[:, 0:n], -1.0 / D, None, ALU.mult))
    link(v.tensor_tensor(t.xc[:, 0:n, :], x, over(t.s[:, 0:n], 2, D), ALU.add))
    link(v.tensor_tensor(t.sq[:, 0:n, :], t.xc[:, 0:n, :], t.xc[:, 0:n, :], ALU.mult))
    v.tensor_reduce(t.var[:, 0:n], t.sq[:, 0:n, :], AX.X, ALU.add).then_inc(act_in, 1)
    v.wait_ge(act_out, count)
    link(v.reciprocal(t.rs[:, 0:n], t.sd[:, 0:n]))
    return v.scalar_tensor_tensor(out, t.xc[:, 0:n, :], 0.0, over(t.rs[:, 0:n], 2, D), ALU.max, ALU.mult)


def norm_act(g, act, act_in, act_out, count, n, t):
    act.wait_ge(act_in, count)
    act.activation(t.sd[:, 0:n], t.var[:, 0:n], ACT.Sqrt, bias=g.eps[:, :], scale=1.0 / D).then_inc(act_out, 1)


def norm_tiles(ph, n):
    t = Names()
    t.s, t.var, t.sd, t.rs = (ph.sb(f"ln_{name}", [P, n]) for name in ("s", "var", "sd", "rs"))
    t.xc, t.sq = ph.sb("ln_xc", [P, n, D]), ph.sb("ln_sq", [P, n, D])
    return t


def carry_tiles(ph, F):
    c = Names()
    c.F = F
    c.edge, c.turned = ph.sb("edge", [P, 2, F]), ph.sb("turned", [F, 2, P])
    c.run, c.carry = ph.sb("run", [F, P + 1]), ph.sb("carry", [P, F])
    c.ask, c.told = ph.sem("ask"), ph.sem("told")
    c.ps = [ph.ps(f"carry{i}") for i in range(3)]
    return c


def carry_dve(v, link, c, base, col, mult, kind="sum", back=False):
    F = c.F
    at = 0
    for piece, m in zip(col, mult):
        w = piece.shape[-1]
        link.inc(v.tensor_copy(c.edge[:, 0, at:at + w], piece))
        link.inc(v.tensor_copy(c.edge[:, 1, at:at + w], m))
        at += w
    link.inc(v.memset(c.run[:, P:P + 1] if back else c.run[:, 0:1], 0.0))
    v.wait_ge(link.sem, link.base + link.n)
    v.sem_inc(c.ask, 1)
    v.wait_ge(c.told, base + 1)
    link(v.tensor_copy(c.turned[:, 0, :], c.ps[0][0:F, 0:P]))
    link(v.tensor_copy(c.turned[:, 1, :], c.ps[1][0:F, 0:P]))
    if kind == "max":
        link(v.tensor_scalar(c.turned[:, 1, :], c.turned[:, 1, :], -1.0, BIG, ALU.add, ALU.mult))
        v.tensor_tensor_scan(c.run[:, 1:P + 1], c.turned[:, 1, :], c.turned[:, 0, :], -BIG, ALU.add, ALU.max).then_inc(c.ask, 1)
    elif back:
        v.tensor_tensor_scan(c.run[:, 0:P][:, ::-1], c.turned[:, 1, ::-1], c.turned[:, 0, ::-1], 0.0, ALU.mult, ALU.add).then_inc(c.ask, 1)
    else:
        v.tensor_tensor_scan(c.run[:, 1:P + 1], c.turned[:, 1, :], c.turned[:, 0, :], 0.0, ALU.mult, ALU.add).then_inc(c.ask, 1)
    v.wait_ge(c.told, base + 2)
    link(v.tensor_copy(c.carry[:, :], c.ps[2][:, 0:F]))


def carry_pe(g, pe, c, base, back=False):
    F = c.F
    pe.wait_ge(c.ask, base + 1)
    pe.matmul(c.ps[0][0:F, 0:P], c.edge[:, 0, :], g.ident[:, :], start=True, stop=True)
    pe.matmul(c.ps[1][0:F, 0:P], c.edge[:, 1, :], g.ident[:, :], start=True, stop=True).then_inc(c.told, 1)
    pe.wait_ge(c.ask, base + 2)
    s = c.run[:, 1:P + 1] if back else c.run[:, 0:P]
    pe.matmul(c.ps[2][:, 0:F], s, g.ident[0:F, 0:F], start=True, stop=True).then_inc(c.told, 1)


def scan_sum(g, v, link, c, base, buf, A, n=D):
    W = g.W
    for f in range(n):
        link.inc(v.tensor_tensor_scan(buf[:, :, f], A.same[:, :], buf[:, :, f], 0.0, ALU.mult, ALU.add))
    v.wait_ge(link.sem, link.base + link.n)
    carry_dve(v, link, c, base, [buf[:, W - 1, :]], [A.pfx[:, W - 1:W].broadcast_to([P, n])])
    for f in range(n):
        link.inc(v.scalar_tensor_tensor(buf[:, :, f], A.pfx[:, :], c.carry[:, f:f + 1], buf[:, :, f], ALU.mult, ALU.add))
    v.wait_ge(link.sem, link.base + link.n)


def gather_chunks(g, pool, idx_all, idxr, copied, table, ring, got, free, base=0):
    def body(k, b, first):
        c = 2 * k + b
        if not first:
            free(pool, k, b)
            pool.sem_inc(g.hop, 1)
        pool.tensor_copy(idxr[b][:, :], idx_all[:, bass.ts(c, CH)]).then_inc(copied, 1)
        pool.wait_ge(copied, base + c + 1)
        pool.sem_inc(g.hop, 1)
        for j in range(CH):
            pool.indirect_dma_start(out=ring[b][:, j, :], out_offset=None, in_=table,
                                    in_offset=bass.IndirectOffsetOnAxis(ap=idxr[b][:, j:j + 1], axis=0)).then_inc(got[b], 16)
    chunks(g, pool, body)


def layer0_edges(g, A, H, QA):
    W = g.W
    F = 8
    with Phase(g, "l0") as ph:
        lk, act_in, act_out = ph.sem("lk"), ph.sem("ln_in"), ph.sem("ln_out")
        used, got, got2, kept, kept2 = ph.sem("used"), ph.sem2("got"), ph.sem2("gots"), ph.sem2("kept"), ph.sem2("kepts")
        copied, bulk_lk = ph.sem("copied"), ph.sem("messages")
        expo, exped = ph.sem("expo"), ph.sem("exped")
        t = norm_tiles(ph, CH)
        ring = ph.sb2("ring", [P, CH, D + 2])
        idxr = ph.sb2("idxr", [P, CH], I32)
        L, M, Dd, Nn, Pp = (ph.sb(n, [P, W, F]) for n in ("logit", "top", "decay", "num", "prod"))
        neg = ph.sb("neg", [P, W])
        pneg = ph.sb("pneg", [P, W])
        c = carry_tiles(ph, 2 * F)
        KG = 4
        block = ph.block()

        @block.gpsimd
        def _(pool):
            def free_dst(p_, k, b):
                p_.wait_ge(used, 2 * k + b - 1)
                p_.wait_ge(kept[b], 16 * k)
            gather_chunks(g, pool, A.other, idxr, copied, g.nodes1, ring, got, free_dst)
            pool.wait_ge(used, g.NCH)
            both(g, pool, kept, 16)

            def free_src(p_, k, b):
                p_.wait_ge(kept2[b], 16 * k)
            gather_chunks(g, pool, A.own, idxr, copied, g.nodes1, ring, got2, free_src, base=g.NCH)

        @block.sync
        def _(sp):
            def keep(g_, k_, lin):
                def body(k, b, first):
                    sp.wait_ge(g_[b], 16 * CH * (k + 1))
                    sp.dma_start(lin.rearrange("(p w) c -> p w c", w=W)[:, bass.ts(2 * k + b, CH), :], ring[b][:, :, :]).then_inc(k_[b], 16)
                chunks(g, sp, body)
                both(g, sp, k_, 16)
            keep(got, kept, g.xd_lin)
            keep(got2, kept2, g.xs_lin)

        @block.scalar
        def _(act):
            def root(k, b, first):
                norm_act(g, act, act_in, act_out, 2 * k + b + 1, CH, t)
            chunks(g, act, root)
            with act.Fori(0, D // F) as q:
                act.wait_ge(expo, 2 * q + 1)
                act.activation(L[:, :, :], L[:, :, :], ACT.Exp).then_inc(exped, 1)
                act.wait_ge(expo, 2 * q + 2)
                act.activation(Dd[:, :, :], Dd[:, :, :], ACT.Exp).then_inc(exped, 1)

        @block.tensor
        def _(pe):
            with pe.Fori(0, D // F) as q:
                carry_pe(g, pe, c, q * KG)
                carry_pe(g, pe, c, q * KG + 2)

        @block.vector
        def _(v):
            link = Link(v, lk)
            KL = 6

            def messages(k, b, first):
                cc = 2 * k + b
                link.at(cc * KL)
                v.wait_ge(got[b], 16 * CH * (k + 1))
                norm_dve(v, link, act_in, act_out, cc + 1, ring[b][:, :, 0:D], CH, t, t.sq[:, :, :]).then_inc(lk, 1)
                v.wait_ge(lk, cc * KL + KL)
                v.tensor_scalar(H[:, bass.ts(cc, CH), :], t.sq[:, :, :], 1e-7, None, ALU.add).then_inc(bulk_lk, 1)
                v.tensor_copy(QA[:, bass.ts(cc, CH)], ring[b][:, :, D]).then_inc(used, 1)
            chunks(g, v, messages)
            v.wait_ge(bulk_lk, g.NCH)
            base = g.NCH * KL
            link.at(base)
            link(v.tensor_scalar(neg[:, :], A.same[:, :], -1.0, BIG, ALU.add, ALU.mult))
            link(v.tensor_scalar(pneg[:, :], A.pfx[:, :], -1.0, BIG, ALU.add, ALU.mult))
            base += 2
            KK = 82
            with v.Fori(0, D // F) as q:
                link.at(base + q * KK)
                hs = H[:, :, bass.ds(q * F, F)]
                link(v.tensor_scalar(L[:, :, :], hs, g.beta[:, 0:1], None, ALU.mult))
                for f in range(F):
                    link.inc(v.tensor_tensor_scan(M[:, :, f], neg[:, :], L[:, :, f], -BIG, ALU.add, ALU.max))
                v.wait_ge(lk, link.base + link.n)
                e = [M[:, W - 1, :]] * 2
                carry_dve(v, link, c, q * KG, e, [A.pfx[:, W - 1:W].broadcast_to([P, F])] * 2, kind="max")
                for f in range(F):
                    link.inc(v.scalar_tensor_tensor(M[:, :, f], pneg[:, :], c.carry[:, f:f + 1], M[:, :, f], ALU.add, ALU.max))
                v.wait_ge(lk, link.base + link.n)
                link(v.tensor_tensor(L[:, :, :], L[:, :, :], M[:, :, :], ALU.subtract))
                v.sem_inc(expo, 1)
                link.inc(v.tensor_tensor(Dd[:, 1:W, :], M[:, 0:W - 1, :], M[:, 1:W, :], ALU.subtract))
                link(v.tensor_tensor(Dd[:, 0, :], c.carry[:, 0:F], M[:, 0, :], ALU.subtract))
                link(v.tensor_scalar(Dd[:, :, :], Dd[:, :, :], 0.0, None, ALU.min))
                v.sem_inc(expo, 1)
                v.wait_ge(exped, 2 * q + 2)
                link(v.tensor_tensor(Dd[:, :, :], Dd[:, :, :], over(A.same[:, :], 2, F), ALU.mult))
                for f in range(F):
                    link.inc(v.tensor_tensor_scan(Pp[:, :, f], Dd[:, :, f], g.zerow[:, :], 1.0, ALU.mult, ALU.add))
                    link.inc(v.tensor_tensor_scan(M[:, :, f], Dd[:, :, f], L[:, :, f], 0.0, ALU.mult, ALU.add))
                link(v.tensor_tensor(Nn[:, :, :], L[:, :, :], hs, ALU.mult))
                for f in range(F):
                    link.inc(v.tensor_tensor_scan(Nn[:, :, f], Dd[:, :, f], Nn[:, :, f], 0.0, ALU.mult, ALU.add))
                v.wait_ge(lk, link.base + link.n)
                carry_dve(v, link, c, q * KG + 2, [M[:, W - 1, :], Nn[:, W - 1, :]], [Pp[:, W - 1, :]] * 2)
                for f in range(F):
                    link.inc(v.scalar_tensor_tensor(M[:, :, f], Pp[:, :, f], c.carry[:, f:f + 1], M[:, :, f], ALU.mult, ALU.add))
                    link.inc(v.scalar_tensor_tensor(Nn[:, :, f], Pp[:, :, f], c.carry[:, F + f:F + f + 1], Nn[:, :, f], ALU.mult, ALU.add))
                v.wait_ge(lk, link.base + link.n)
                link(v.reciprocal(M[:, :, :], M[:, :, :]))
                link(v.tensor_tensor(H[:, :, bass.ds(q * F, F)], Nn[:, :, :], M[:, :, :], ALU.mult))
                assert link.n == KK, link.n


def fill_back(g, A, H):
    W = g.W
    with Phase(g, "fb") as ph:
        lk, stored, filled = ph.sem("lk"), ph.sem("stored"), ph.sem("filled")
        c = carry_tiles(ph, D)
        notlast = ph.sb("notlast", [P, W])
        sfx = ph.sb("sfx", [P, W])
        block = ph.block()

        @block.tensor
        def _(pe):
            carry_pe(g, pe, c, 0, back=True)

        @block.sync
        def _(sp):
            sp.wait_ge(filled, 1)
            sp.dma_start(g.agg_tab[0:g.NP, :].rearrange("(p w) c -> p w c", w=W), H[:, :, :]).then_inc(stored, 16)
            sp.dma_start(g.agg_tab[g.NP:g.NP + 1, :], g.zerow[0:1, 0:D]).then_inc(stored, 16)
            sp.wait_ge(stored, 32)

        @block.vector
        def _(v):
            link = Link(v, lk)
            link(v.tensor_scalar(notlast[:, :], A.last[:, :], -1.0, 1.0, ALU.mult, ALU.add))
            link.inc(v.tensor_tensor_scan(sfx[:, ::-1], notlast[:, ::-1], g.zerow[:, :], 1.0, ALU.mult, ALU.add))
            link(v.tensor_tensor(H[:, :, :], H[:, :, :], over(A.last[:, :], 2, D), ALU.mult))
            for f in range(D):
                link.inc(v.tensor_tensor_scan(H[:, ::-1, f], notlast[:, ::-1], H[:, ::-1, f], 0.0, ALU.mult, ALU.add))
            v.wait_ge(lk, link.n)
            carry_dve(v, link, c, 0, [H[:, 0, :]], [sfx[:, 0:1].broadcast_to([P, D])], back=True)
            for f in range(D):
                link.inc(v.scalar_tensor_tensor(H[:, :, f], sfx[:, :], c.carry[:, f:f + 1], H[:, :, f], ALU.mult, ALU.add))
            v.wait_ge(lk, link.n)
            v.sem_inc(filled, 1)


def layer01_edges(g, A, H, QA, Z, PB):
    W = g.W
    N2 = 2 * CH
    with Phase(g, "l01") as ph:
        lk, act_in, act_out = ph.sem("lk"), ph.sem("ln_in"), ph.sem("ln_out")
        got, used, xgot, copied = ph.sem2("got"), ph.sem("used"), ph.sem2("xgot"), ph.sem("copied")
        aready, tdone, adone, h1done, hready, odone = (ph.sem(n) for n in ("aready", "tdone", "adone", "h1done", "hready", "odone"))
        x1ready, nready, t2done, a2done, zdone, zkept, xkept = (ph.sem(n) for n in ("x1ready", "nready", "t2done", "a2done", "zdone", "zkept", "xkept"))
        xused = ph.sem("xused")
        t = norm_tiles(ph, N2)
        idxr = ph.sb2("idxr", [P, CH], I32)
        ring = ph.sb2("ring", [P, CH, D])
        xr = ph.sb2("xr", [P, N2, D + 2])
        agg = ph.sb("agg", [P, N2, D])
        aT = ph.sb("aT", [P, 512])
        hT = ph.sb2("hT", [P, 512])
        x1 = ph.sb("x1", [P, N2, D])
        h16 = ph.sb("h16", [P, N2, D])
        psA, psB, psC, psD, psE = (ph.ps(n) for n in ("psA", "psB", "psC", "psD", "psE"))
        block = ph.block()

        @block.gpsimd
        def _(pool):
            def free(p_, k, b):
                p_.wait_ge(used, 2 * k + b - 1)
            gather_chunks(g, pool, QA, idxr, copied, g.agg_tab, ring, got, free)

        @block.sync
        def _(sp):
            def load(k, b, first):
                if not first:
                    sp.wait_ge(xused, 2 * k + b - 1)
                for i, lin in enumerate((g.xs_lin, g.xd_lin)):
                    sp.dma_start(xr[b][:, i * CH:(i + 1) * CH, :],
                                 lin.rearrange("(p w) c -> p w c", w=W)[:, bass.ts(2 * k + b, CH), :]).then_inc(xgot[b], 16)

            def store(k, b):
                sp.wait_ge(x1ready, 2 * k + b + 1)
                sp.dma_start(g.x1_lin.rearrange("(p w) c -> p w c", w=W)[:, bass.ts(2 * k + b, CH), :], x1[:, 0:CH, :]).then_inc(xkept, 16)
            ahead(g, load, store)
            sp.wait_ge(xkept, 16 * g.NCH)

        @block.scalar
        def _(act):
            def body(k, b, first):
                c = 2 * k + b
                act.wait_ge(got[b], 16 * CH * (k + 1))
                if not (first and b == 0):
                    act.wait_ge(tdone, c)
                act.sem_inc(g.hop, 1)
                act.copy(agg[:, 0:CH, :], H[:, bass.ts(c, CH), :]).then_inc(aready, 1)
                act.copy(agg[:, CH:N2, :], ring[b][:, :, :]).then_inc(used, 1)
                act.wait_ge(tdone, c + 1)
                act.copy(aT[:, :], psA[:, :]).then_inc(adone, 1)
                act.wait_ge(h1done, c + 1)
                act.activation(hT[0][:, :], psB[:, :], ACT.Relu, bias=g.b0col[:, :]).then_inc(hready, 1)
                act.activation(hT[1][:, :], psC[:, :], ACT.Relu, bias=g.b0col[:, :]).then_inc(hready, 1)
                norm_act(g, act, act_in, act_out, c + 1, N2, t)
                act.wait_ge(t2done, c + 1)
                act.copy(aT[:, :], psA[:, :]).then_inc(a2done, 1)
                hold(g, act, zdone, c + 1)
                act.copy(Z[:, bass.ts(c, CH), :], psE[:, 0:256].rearrange("p (t f) -> p t f", f=D)).then_inc(zkept, 1)
            chunks(g, act, body)

        @block.tensor
        def _(pe):
            def body(k, b, first):
                c = 2 * k + b
                pe.wait_ge(aready, c + 1)
                pe.wait_ge(used, c + 1)
                for q in range(4):
                    ins = pe.transpose(psA[:, q * P:(q + 1) * P], agg[:, 4 * q:4 * q + 4, :].rearrange("p t f -> p (t f)"), g.ident[:, :])
                ins.then_inc(tdone, 1)
                pe.wait_ge(adone, c + 1)
                pe.matmul(psB[:, :], g.w0a[:, 0:P], aT[:, :], start=True, stop=True)
                pe.matmul(psC[:, :], g.w0a[:, P:2 * P], aT[:, :], start=True, stop=True).then_inc(h1done, 1)
                pe.wait_ge(hready, 2 * c + 2)
                pe.matmul(psD[:, :], g.ones[0:1, :], over(g.bias[:, 0, :], 1, N2), start=True, stop=False, skip_group_check=True)
                for q in range(4):
                    for i in range(2):
                        o = psD[:, q * P + i * 64:q * P + i * 64 + 64]
                        ins = pe.matmul(o, hT[i][:, q * P:(q + 1) * P], g.w0b[:, :], start=False, stop=False, skip_group_check=True)
                ins.then_inc(odone, 1)
                pe.wait_ge(nready, c + 1)
                for q in range(4):
                    ins = pe.transpose(psA[:, q * P:(q + 1) * P], h16[:, 4 * q:4 * q + 4, :].rearrange("p t f -> p (t f)"), g.ident[:, :])
                ins.then_inc(t2done, 1)
                pe.wait_ge(a2done, c + 1)
                if not (first and b == 0):
                    pe.wait_ge(zkept, c)
                pe.matmul(psE[:, 0:256], g.ones[0:1, :], over(g.bias[:, 1, :], 1, CH), start=True, stop=False, skip_group_check=True)
                for q in range(2):
                    o = psE[:, q * P:(q + 1) * P]
                    pe.matmul(o, aT[:, q * P:(q + 1) * P], g.w1s[:, :], start=False, stop=False, skip_group_check=True)
                    ins = pe.matmul(o, aT[:, (q + 2) * P:(q + 3) * P], g.w1d[:, :], start=False, stop=False, skip_group_check=True)
                ins.then_inc(zdone, 1)
            chunks(g, pe, body)

        @block.vector
        def _(v):
            link = Link(v, lk)
            KL = 6

            def body(k, b, first):
                c = 2 * k + b
                link.at(c * KL)
                v.wait_ge(xgot[b], 32 * (k + 1))
                v.wait_ge(odone, c + 1)
                if not (first and b == 0):
                    v.wait_ge(xkept, 16 * c)
                link(v.tensor_tensor(x1[:, :, :], xr[b][:, :, 0:D], psD[:, :].rearrange("p (t f) -> p t f", f=D), ALU.add))
                v.sem_inc(x1ready, 1)
                v.tensor_copy(PB[:, bass.ts(c, CH)], xr[b][:, 0:CH, D + 1]).then_inc(xused, 1)
                norm_dve(v, link, act_in, act_out, c + 1, x1[:, :, :], N2, t, h16[:, :, :]).then_inc(nready, 1)
                assert link.n == KL, link.n
            chunks(g, v, body)


def batch_norm(g, ph, Z, SQ, valid, gi, tag, then_chunks=None):
    E = float(g.E)
    W = g.W
    lk, summed, spread, sqin, sqout = (ph.sem(f"{tag}_{n}") for n in ("lk", "summed", "spread", "sqin", "sqout"))
    part = ph.sb(f"{tag}_part", [P, D])
    mean = ph.sb(f"{tag}_mean", [P, D])
    var = ph.sb(f"{tag}_var", [P, D])
    sd = ph.sb(f"{tag}_sd", [P, D])
    pst = ph.ps(f"{tag}_ps")
    parts = Names()

    def tensor(pe):
        for i in range(2):
            pe.wait_ge(summed, i + 1)
            pe.matmul(pst[:, 0:D], g.ones[:, :], part[:, :], start=True, stop=True).then_inc(spread, 1)

    def scalar(act):
        act.wait_ge(sqin, 1)
        act.activation(SQ[:, :, :], Z[:, :, :], ACT.Square).then_inc(sqout, 1)
        act.wait_ge(sqin, 2)
        act.activation(sd[:, :], var[:, :], ACT.Sqrt, bias=g.eps[:, :], scale=1.0 / E).then_inc(sqout, 1)

    def vector(v):
        link = Link(v, lk)
        vb = over(valid[:, :], 2, D)
        link(v.tensor_tensor(Z[:, :, :], Z[:, :, :], vb, ALU.mult))
        v.tensor_reduce(part[:, :], Z[:, :, :].rearrange("p w f -> p f w"), AX.X, ALU.add).then_inc(summed, 1)
        v.wait_ge(spread, 1)
        link(v.tensor_scalar(mean[:, :], pst[:, 0:D], -1.0 / E, None, ALU.mult))
        link(v.tensor_tensor(Z[:, :, :], Z[:, :, :], over(mean[:, :], 1, W), ALU.add))
        link(v.tensor_tensor(Z[:, :, :], Z[:, :, :], vb, ALU.mult))
        v.sem_inc(sqin, 1)
        v.wait_ge(sqout, 1)
        v.tensor_reduce(part[:, :], SQ[:, :, :].rearrange("p w f -> p f w"), AX.X, ALU.add).then_inc(summed, 1)
        v.wait_ge(spread, 2)
        link(v.tensor_copy(var[:, :], pst[:, 0:D]))
        v.sem_inc(sqin, 1)
        v.wait_ge(sqout, 2)
        link(v.reciprocal(sd[:, :], sd[:, :]))
        link(v.tensor_tensor(sd[:, :], sd[:, :], g.bn[:, gi, :], ALU.mult))
        link(v.tensor_tensor(Z[:, :, :], Z[:, :, :], over(sd[:, :], 1, W), ALU.mult))
        link(v.tensor_tensor(Z[:, :, :], Z[:, :, :], over(g.bn[:, gi + 1, :], 1, W), ALU.add))
    parts.tensor, parts.scalar, parts.vector = tensor, scalar, vector
    return parts


def layer1_rest(g, A, SQ, Z, PB):
    W, N = g.W, g.N
    with Phase(g, "l1") as ph:
        valid = ph.sb("valid", [P, W])
        vready, bn1, mid, bn2 = ph.sem("valid"), ph.sem("bn1"), ph.sem("mid"), ph.sem("bn2")
        zt = ph.sb("zt", [P, CH * D])
        aT = ph.sb("aT", [P, 256])
        tready, tdone, adone, zdone, zkept = (ph.sem(n) for n in ("tready", "tdone", "adone", "zdone", "zkept"))
        psA, psE = ph.ps("psA"), ph.ps("psE")
        b1 = batch_norm(g, ph, Z, SQ, valid, 0, "bn1")
        b2 = batch_norm(g, ph, Z, SQ, valid, 2, "bn2")
        BN = 20
        steps = g.NPER // BN
        xin = ph.sb2("xin", [P, BN, D + 2])
        xout = ph.sb2("xout", [P, BN, D + 1])
        tgot, tmade, twrote, tchain = ph.sem2("tgot"), ph.sem("tmade"), ph.sem2("twrote"), ph.sem("tchain")
        block = ph.block()
        n1 = g.nodes1.rearrange("(p n) f -> p n f", p=g.NPART)
        n2 = g.nodes2.rearrange("(p n) f -> p n f", p=g.NPART)

        @block.sync
        def _(sp):
            def load(k, b, first):
                if not first:
                    sp.wait_ge(tmade, 2 * k + b - 1)
                sp.dma_start(xin[b][0:g.NPART, :, :], n1[:, bass.ts(2 * k + b, BN), :]).then_inc(tgot[b], 16)

            def store(k, b):
                sp.wait_ge(tmade, 2 * k + b + 1)
                sp.dma_start(n2[:, bass.ts(2 * k + b, BN), :], xout[b][0:g.NPART, :, :]).then_inc(twrote[b], 16)
            load(0, 0, True)
            load(0, 1, True)
            with sp.Fori(0, steps // 2 - 1) as k:
                store(k, 0)
                load(k + 1, 0, False)
                store(k, 1)
                load(k + 1, 1, False)
            store(steps // 2 - 1, 0)
            store(steps // 2 - 1, 1)
            for b in range(2):
                sp.wait_ge(twrote[b], 16 * (steps // 2))

        @block.gpsimd
        def _(pool):
            pool.iota(valid[:, :], [[1, W]], base=0, channel_multiplier=W, allow_small_or_imprecise_dtypes=True).then_inc(vready, 1)
            q = g.NPART

            def copy(k, b, first):
                pool.wait_ge(tgot[b], 16 * (k + 1))
                if not first:
                    pool.wait_ge(twrote[b], 16 * k)
                pool.tensor_tensor(xout[b][0:q, :, 0:D], xin[b][0:q, :, 0:D], over(g.alone[0:q, :], 1, BN), ALU.add).then_inc(tchain, 1)
                pool.tensor_copy(xout[b][0:q, :, D], xin[b][0:q, :, D + 1]).then_inc(tchain, 1)
                pool.wait_ge(tchain, 2 * (2 * k + b) + 2)
                pool.sem_inc(tmade, 1)
            copy(0, 0, True)
            copy(0, 1, True)
            with pool.Fori(1, steps // 2) as k:
                copy(k, 0, False)
                copy(k, 1, False)

        @block.scalar
        def _(act):
            b1.scalar(act)
            act.wait_ge(bn1, 1)

            def body(k, b, first):
                c = 2 * k + b
                if not (first and b == 0):
                    act.wait_ge(zkept, c)
                act.sem_inc(g.hop, 1)
                act.copy(zt[:, :], Z[:, bass.ts(c, CH), :].rearrange("p t f -> p (t f)")).then_inc(tready, 1)
                act.wait_ge(tdone, c + 1)
                act.activation(aT[:, :], psA[:, 0:256], ACT.Relu).then_inc(adone, 1)
                hold(g, act, zdone, c + 1)
                act.copy(Z[:, bass.ts(c, CH), :], psE[:, 0:256].rearrange("p (t f) -> p t f", f=D)).then_inc(zkept, 1)
            chunks(g, act, body)
            b2.scalar(act)

        @block.tensor
        def _(pe):
            b1.tensor(pe)

            def body(k, b, first):
                c = 2 * k + b
                pe.wait_ge(tready, c + 1)
                for q in range(2):
                    ins = pe.transpose(psA[:, q * P:(q + 1) * P], zt[:, q * P:(q + 1) * P], g.ident[:, :])
                ins.then_inc(tdone, 1)
                pe.wait_ge(adone, c + 1)
                pe.matmul(psE[:, 0:256], g.ones[0:1, :], over(g.bias[:, 2, :], 1, CH), start=True, stop=False, skip_group_check=True)
                for q in range(2):
                    ins = pe.matmul(psE[:, q * P:(q + 1) * P], aT[:, q * P:(q + 1) * P], g.w2[:, :], start=False, stop=False, skip_group_check=True)
                ins.then_inc(zdone, 1)
            chunks(g, pe, body)
            b2.tensor(pe)

        @block.vector
        def _(v):
            v.wait_ge(vready, 1)
            link = Link(v, mid)
            link(v.tensor_scalar(valid[:, :], valid[:, :], float(g.E), None, ALU.is_lt))
            b1.vector(v)
            v.sem_inc(bn1, 1)
            v.wait_ge(zkept, g.NCH)
            b2.vector(v)
            v.tensor_scalar(Z[:, :, :], Z[:, :, :], 0.0, None, ALU.max).then_inc(bn2, 1)

    with Phase(g, "l1s") as ph:
        lk, made, sent = ph.sem("lk"), ph.sem("made"), ph.sem2("sent")
        xgot = ph.sem2("xgot")
        x1 = ph.sb2("x1", [P, CH, D])
        c = carry_tiles(ph, D)
        rowr = ph.sb2("rowr", [P, CH, D + 1])
        idxr = ph.sb2("idxr", [P, CH], I32)
        block = ph.block()

        @block.tensor
        def _(pe):
            carry_pe(g, pe, c, 0)

        @block.sync
        def _(sp):
            def load(k, b, first):
                if not first:
                    sp.wait_ge(made, 3 * (2 * k + b) - 3)
                sp.dma_start(x1[b][:, :, :], g.x1_lin.rearrange("(p w) c -> p w c", w=W)[:, bass.ts(2 * k + b, CH), :]).then_inc(xgot[b], 16)
            chunks(g, sp, load)

        @block.gpsimd
        def _(pool):
            def scatter(k, b, first):
                pool.wait_ge(made, 3 * (2 * k + b) + 3)
                pool.sem_inc(g.hop, 1)
                for j in range(CH):
                    pool.indirect_dma_start(out=g.nodes2, out_offset=bass.IndirectOffsetOnAxis(ap=idxr[b][:, j:j + 1], axis=0),
                                            in_=rowr[b][:, j, :], in_offset=None, bounds_check=N - 1,
                                            oob_is_err=False).then_inc(sent[b], 16)
            chunks(g, pool, scatter)
            both(g, pool, sent, 16 * CH)

        @block.vector
        def _(v):
            link = Link(v, lk)
            scan_sum(g, v, link, c, 0, Z, A)

            def body(k, b, first):
                cc = 2 * k + b
                if not first:
                    v.wait_ge(sent[b], 16 * CH * k)
                v.wait_ge(xgot[b], 16 * (k + 1))
                v.tensor_tensor(rowr[b][:, :, 0:D], x1[b][:, :, :], Z[:, bass.ts(cc, CH), :], ALU.add).then_inc(made, 1)
                v.tensor_copy(rowr[b][:, :, D], PB[:, bass.ts(cc, CH)]).then_inc(made, 1)
                v.tensor_copy(idxr[b][:, :], A.out[:, bass.ts(cc, CH)]).then_inc(made, 1)
            chunks(g, v, body)


def close_segments(g, B, M, table, ph_name, count=None, scale=None):
    W = g.W
    with Phase(g, ph_name) as ph:
        lk, stored, closed = ph.sem("lk"), ph.sem("stored"), ph.sem("closed")
        c = carry_tiles(ph, D)
        c1 = carry_tiles_one(ph) if count is not None else None
        block = ph.block()

        @block.tensor
        def _(pe):
            if count is not None:
                carry_pe(g, pe, c1, 0)
            carry_pe(g, pe, c, 0)

        @block.sync
        def _(sp):
            sp.wait_ge(closed, 1)
            sp.dma_start(table[0:g.NP, :].rearrange("(p w) c -> p w c", w=W), M[:, :, :]).then_inc(stored, 16)
            sp.dma_start(table[g.NP:g.NP + 1, :], g.zerow[0:1, 0:D]).then_inc(stored, 16)
            sp.wait_ge(stored, 32)

        @block.vector
        def _(v):
            link = Link(v, lk)
            if count is not None:
                link(v.memset(count[:, :, :], 1.0))
                scan_sum(g, v, link, c1, 0, count, B, 1)
                link(v.reciprocal(count[:, :, :], count[:, :, :]))
            scan_sum(g, v, link, c, 0, M, B)
            if scale is not None:
                link(v.tensor_tensor(M[:, :, :], M[:, :, :], over(scale[:, :, 0], 2, D), ALU.mult))
            v.sem_inc(closed, 1)


def carry_tiles_one(ph):
    c = Names()
    c.F = 1
    c.edge, c.turned = ph.sb("edge1", [P, 2, 1]), ph.sb("turned1", [1, 2, P])
    c.run, c.carry = ph.sb("run1", [1, P + 1]), ph.sb("single", [P, 1])
    c.ask, c.told = ph.sem("ask1"), ph.sem("told1")
    c.ps = [ph.ps(f"single{i}") for i in range(3)]
    return c


def spline_weights(g, WT):
    W = g.W
    with Phase(g, "basis") as ph:
        lk = ph.sem("lk")
        pos, r, gt, lo, fr, c0, c1, omf, t0, t1 = (ph.sb(n, [P, W, 3]) for n in ("pos", "r", "gt", "lo", "fr", "c0", "c1", "omf", "t0", "t1"))
        pi = ph.sb("pi", [P, W, 3], I32)
        block = ph.block()

        @block.vector
        def _(v):
            link = Link(v, lk)
            link(v.tensor_scalar(pos[:, :, :], g.rows_b[:, :, 2:5], 2.0, None, ALU.mult))
            link(v.tensor_copy(pi[:, :, :], pos[:, :, :]))
            link(v.tensor_copy(r[:, :, :], pi[:, :, :]))
            link(v.tensor_tensor(gt[:, :, :], r[:, :, :], pos[:, :, :], ALU.is_gt))
            link(v.tensor_tensor(lo[:, :, :], r[:, :, :], gt[:, :, :], ALU.subtract))
            link(v.tensor_tensor(fr[:, :, :], pos[:, :, :], lo[:, :, :], ALU.subtract))
            link(v.tensor_scalar(omf[:, :, :], fr[:, :, :], -1.0, 1.0, ALU.mult, ALU.add))
            link(v.tensor_scalar(c0[:, :, :], lo[:, :, :], 0.0, 2.0, ALU.max, ALU.min))
            link(v.tensor_scalar(c1[:, :, :], lo[:, :, :], 1.0, None, ALU.add))
            link(v.tensor_scalar(c1[:, :, :], c1[:, :, :], 0.0, 2.0, ALU.max, ALU.min))
            for k in range(3):
                link(v.scalar_tensor_tensor(t0[:, :, :], c0[:, :, :], float(k), omf[:, :, :], ALU.is_equal, ALU.mult))
                link(v.scalar_tensor_tensor(t1[:, :, :], c1[:, :, :], float(k), fr[:, :, :], ALU.is_equal, ALU.mult))
                link(v.tensor_tensor(WT[:, :, :].rearrange("p w (d k) -> p w d k", k=3)[:, :, :, k], t0[:, :, :], t1[:, :, :], ALU.add))


class Spline:

    def __init__(self, ph, g, WT, M):
        self.g, self.WT, self.M = g, WT, M
        self.w01 = ph.sb("w01", [P, CH, 3, 3])
        self.hz = ph.sb("hz", [P, CH, 3, D])
        self.hzT = ph.sb("hzT", [3 * D, CH * P])
        self.V = ph.sb("V", [P, 2, 9, D])
        self.msg = ph.sb("msg", [P, CH, D])
        self.psT = ph.ps("psT", (P, 1024))
        self.psU = [ph.ps(f"psU{i}", (P, 2, 512)) for i in range(2)]
        self.wide, self.turned, self.flat, self.multiplied, self.weighed = (ph.sem("spline_" + n) for n in ("wide", "turned", "flat", "multiplied", "weighed"))

    LINKS = 7

    def vector(self, v, link, c, h):
        WTc = self.WT[:, bass.ts(c, CH), :]
        v.tensor_tensor(self.hz[:, :, :, :], over(h, 2, 3), over(WTc[:, :, 6:9], 3, D), ALU.mult).then_inc(self.wide, 1)
        link(v.tensor_tensor(self.w01[:, :, :, :], over(WTc[:, :, 0:3], 2, 3), over(WTc[:, :, 3:6], 3, 3), ALU.mult))
        for i in range(4):
            v.wait_ge(self.multiplied, 4 * c + i + 1)
            link(v.tensor_tensor(self.V[:, :, :, :], self.psU[i % 2][:, :, 0:288].rearrange("p t (j o) -> p t j o", o=D),
                                 over(self.w01[:, 2 * i:2 * i + 2, :, :].rearrange("p t a b -> p t (a b)"), 3, D), ALU.mult))
            v.tensor_reduce(self.msg[:, 2 * i:2 * i + 2, :], self.V[:, :, :, :].rearrange("p t j o -> p t o j"), AX.X,
                            ALU.add).then_inc(self.weighed, 1)
            if i == 3:
                v.wait_ge(self.weighed, 4 * c + 4)
            elif i >= 0:
                v.wait_ge(self.weighed, 4 * c + i + 1)
        link(v.tensor_scalar(self.M[:, bass.ts(c, CH), :], self.msg[:, :, :], 1.0, None, ALU.mult))

    def tensor(self, pe, c, w):
        pe.wait_ge(self.wide, c + 1)
        for t in range(CH):
            ins = pe.transpose(self.psT[0:3 * D, t * P:(t + 1) * P], self.hz[:, t, :, :].rearrange("p k f -> p (k f)"), self.g.ident[:, :])
        ins.then_inc(self.turned, 1)
        pe.wait_ge(self.flat, c + 1)
        for i in range(4):
            if i >= 2:
                pe.wait_ge(self.weighed, 4 * c + i - 1)
            for t in range(2):
                ins = pe.matmul(self.psU[i % 2][:, t, 0:288], self.hzT[:, (2 * i + t) * P:(2 * i + t + 1) * P],
                                w[:, :, :].rearrange("p j o -> p (j o)"), start=True, stop=True)
            ins.then_inc(self.multiplied, 1)

    def scalar(self, act, c):
        act.wait_ge(self.turned, c + 1)
        act.copy(self.hzT[:, :], self.psT[0:3 * D, :]).then_inc(self.flat, 1)


def lin(g, t, c, n=D):
    return t.rearrange("(p w) c -> p w c", w=g.W)[:, bass.ts(c, CH), :]


def conv1_edges(g, B, WT, M, S, QB):
    N2 = 2 * CH
    with Phase(g, "c1") as ph:
        lk, act_in, act_out = ph.sem("lk"), ph.sem("ln_in"), ph.sem("ln_out")
        got, copied, nready, kept, skept = ph.sem2("got"), ph.sem("copied"), ph.sem("nready"), ph.sem2("kept"), ph.sem("skept")
        read = ph.sem("read")
        t = norm_tiles(ph, N2)
        ring = ph.sb2("ring", [P, N2, D + 1])
        idxr = ph.sb2("idxr", [P, N2], I32)
        h16 = ph.sb("h16", [P, N2, D])
        sp_ = Spline(ph, g, WT, M)
        block = ph.block()

        @block.gpsimd
        def _(pool):
            def body(k, b, first):
                c = 2 * k + b
                if not first:
                    pool.wait_ge(kept[b], 32 * k)
                    hold(g, pool, read, c - 1)
                pool.tensor_copy(idxr[b][:, 0:CH], B.other[:, bass.ts(c, CH)]).then_inc(copied, 1)
                pool.tensor_copy(idxr[b][:, CH:N2], B.own[:, bass.ts(c, CH)]).then_inc(copied, 1)
                pool.wait_ge(copied, 2 * c + 2)
                pool.sem_inc(g.hop, 1)
                for j in range(N2):
                    pool.indirect_dma_start(out=ring[b][:, j, :], out_offset=None, in_=g.nodes2,
                                            in_offset=bass.IndirectOffsetOnAxis(ap=idxr[b][:, j:j + 1], axis=0)).then_inc(got[b], 16)
            chunks(g, pool, body)

        @block.sync
        def _(sp):
            def body(k, b, first):
                c = 2 * k + b
                sp.wait_ge(got[b], 16 * N2 * (k + 1))
                sp.dma_start(lin(g, g.x2s_lin, c), ring[b][:, 0:CH, :]).then_inc(kept[b], 16)
                sp.dma_start(lin(g, g.x2d_lin, c), ring[b][:, CH:N2, :]).then_inc(kept[b], 16)
                sp.wait_ge(nready, c + 1)
                sp.dma_start(lin(g, g.dst_lin, c), h16[:, CH:N2, :]).then_inc(skept, 16)
            chunks(g, sp, body)
            both(g, sp, kept, 32)
            sp.wait_ge(skept, 16 * g.NCH)

        @block.scalar
        def _(act):
            def body(k, b, first):
                c = 2 * k + b
                norm_act(g, act, act_in, act_out, c + 1, N2, t)
                sp_.scalar(act, c)
            chunks(g, act, body)

        @block.tensor
        def _(pe):
            def body(k, b, first):
                sp_.tensor(pe, 2 * k + b, g.spline[0])
            chunks(g, pe, body)

        @block.vector
        def _(v):
            link = Link(v, lk)
            KL = 13

            def body(k, b, first):
                c = 2 * k + b
                link.at(c * KL)
                v.wait_ge(got[b], 16 * N2 * (k + 1))
                link(v.tensor_scalar(QB[:, bass.ts(c, CH)], ring[b][:, 0:CH, D], 1.0, None, ALU.mult))
                if not (first and b == 0):
                    v.wait_ge(skept, 16 * c)
                norm_dve(v, link, act_in, act_out, c + 1, ring[b][:, :, 0:D], N2, t, h16[:, :, :]).then_inc(nready, 1)
                v.wait_ge(nready, c + 1)
                v.sem_inc(read, 1)
                sp_.vector(v, link, c, h16[:, 0:CH, :])
                v.tensor_scalar(S[:, bass.ts(c, CH), :], h16[:, 0:CH, :], 1.0, None, ALU.mult).then_inc(lk, 1)
                link.n += 1
                assert link.n == KL, (ph.name, link.n)
                v.wait_ge(lk, (c + 1) * KL)
            chunks(g, v, body)


def next_edges(g, B, WT, M, S, QB, table, kind, l, ph_name):
    N2 = 2 * CH
    W = g.W
    with Phase(g, ph_name) as ph:
        s = lambda n: ph.sem(n)
        got, copied, used, lk = ph.sem2("got"), s("copied"), s("used"), s("lk")
        sgot, sread, skept, xkept = ph.sem2("sgot"), s("sread"), s("skept"), s("xkept")
        zin, turned, flat, done, act_e, act_eo = s("zin"), s("turned"), s("flat"), s("done"), s("act_e"), s("act_eo")
        new, mready = s("new"), s("mready")
        nx = 2 if kind == "conv3" else 0
        ring = ph.sb2("ring", [P, CH, D])
        idxr = ph.sb2("idxr", [P, CH], I32)
        din = ph.sb2("din", [P, CH, D])
        xin = ph.sb2("xin", [P, N2, D + 1]) if nx else None
        st = ph.sb("st", [P, N2, D])
        agg = ph.sb("agg", [P, N2, D])
        aT = ph.sb("aT", [P, 512])
        y = ph.sb("y", [P, N2, D])
        psA, psD = ph.ps("psA"), ph.ps("psD")
        bias = {"conv2": 3, "conv3": 4, "gin": 5 + l}[kind]
        weight = {"conv2": g.root[0], "conv3": g.root[1], "gin": g.w3[l]}[kind]
        el = {"conv3": 0, "gin": l + 1}.get(kind)
        e = ph.sb("e", [P, N2, D])
        if kind in ("conv2", "conv3"):
            m = ph.sb("m", [P, N2, D])
        if kind == "conv2":
            sp_ = Spline(ph, g, WT, M)
        else:
            ea, eT, psX, psE = ph.sb("ea", [P, CH * 8]), ph.sb("eT", [64, P]), ph.ps("psX"), ph.ps("psE")
            mm = ph.sb("mm", [P, CH, D])
            ea_in, ea_t, ea_f, ea_d = s("ea_in"), s("ea_t"), s("ea_f"), s("ea_d")
        if kind == "conv3":
            t = norm_tiles(ph, N2)
            act_in, act_out, x3r = s("ln_in"), s("ln_out"), s("x3r")
            x3 = ph.sb("x3", [P, N2, D])
        block = ph.block()

        @block.gpsimd
        def _(pool):
            def free(p_, k, b):
                p_.wait_ge(used, 2 * k + b - 1)
            gather_chunks(g, pool, QB, idxr, copied, table, ring, got, free)

        @block.sync
        def _(sp):
            def load(k, b, first):
                c = 2 * k + b
                if not first:
                    sp.wait_ge(sread, c - 1)
                sp.dma_start(din[b][:, :, :], lin(g, g.dst_lin, c)).then_inc(sgot[b], 16)
                if nx:
                    sp.dma_start(xin[b][:, 0:CH, :], lin(g, g.x2s_lin, c)).then_inc(sgot[b], 16)
                    sp.dma_start(xin[b][:, CH:N2, :], lin(g, g.x2d_lin, c)).then_inc(sgot[b], 16)

            def store(k, b):
                c = 2 * k + b
                sp.wait_ge(new, c + 1)
                sp.dma_start(lin(g, g.dst_lin, c), y[:, CH:N2, :]).then_inc(skept, 16)
                if kind == "conv3":
                    sp.dma_start(lin(g, g.x3_lin, c), x3[:, CH:N2, :]).then_inc(skept, 16)
            ahead(g, load, store)
            sp.wait_ge(skept, (32 if kind == "conv3" else 16) * g.NCH)

        @block.scalar
        def _(act):
            def body(k, b, first):
                c = 2 * k + b
                if kind != "conv2":
                    if not (first and b == 0):
                        act.wait_ge(ea_t, c)
                    act.sem_inc(g.hop, 1)
                    act.copy(ea[:, :].rearrange("p (t f) -> p t f", f=8), g.rows_b[:, bass.ts(c, CH), 5:13]).then_inc(ea_in, 1)
                    act.wait_ge(ea_t, c + 1)
                    act.copy(eT[:, :], psX[0:64, 0:P]).then_inc(ea_f, 1)
                act.wait_ge(turned, c + 1)
                act.copy(aT[:, :], psA[:, :]).then_inc(flat, 1)
                if kind == "gin":
                    act.wait_ge(done, c + 1)
                    act.copy(e[:, :, :], psD[:, :].rearrange("p (t f) -> p t f", f=D)).then_inc(act_eo, 1)
                else:
                    act.wait_ge(act_e, c + 1)
                    act.activation(e[:, :, :], m[:, :, :], ACT.Exp).then_inc(act_eo, 1)
                if kind == "conv3":
                    norm_act(g, act, act_in, act_out, c + 1, N2, t)
                if kind == "conv2":
                    sp_.scalar(act, c)
            chunks(g, act, body)

        @block.tensor
        def _(pe):
            def body(k, b, first):
                c = 2 * k + b
                if kind != "conv2":
                    hold(g, pe, ea_in, c + 1)
                    pe.transpose(psX[0:64, 0:P], ea[:, :], g.ident[:, :]).then_inc(ea_t, 1)
                pe.wait_ge(zin, c + 1)
                src = agg if kind == "gin" else st
                for q in range(4):
                    ins = pe.transpose(psA[:, q * P:(q + 1) * P], src[:, 4 * q:4 * q + 4, :].rearrange("p t f -> p (t f)"), g.ident[:, :])
                ins.then_inc(turned, 1)
                pe.wait_ge(flat, c + 1)
                pe.matmul(psD[:, :], g.ones[0:1, :], over(g.bias[:, bias, :], 1, N2), start=True, stop=False, skip_group_check=True)
                for q in range(4):
                    ins = pe.matmul(psD[:, q * P:(q + 1) * P], aT[:, q * P:(q + 1) * P], weight[:, :], start=False, stop=False, skip_group_check=True)
                ins.then_inc(done, 1)
                if kind == "conv2":
                    sp_.tensor(pe, c, g.spline[1])
                else:
                    pe.wait_ge(ea_f, c + 1)
                    if not (first and b == 0):
                        pe.wait_ge(mready, c)
                    pe.matmul(psE[:, 0:256], g.ones[0:1, :], over(g.bias[:, 8 + el, :], 1, CH), start=True, stop=False, skip_group_check=True)
                    pe.matmul(psE[:, 0:256], eT[:, :], g.we[el][:, :], start=False, stop=False, skip_group_check=True).then_inc(ea_d, 1)
            chunks(g, pe, body)

        @block.vector
        def _(v):
            link = Link(v, lk)
            KL = {"conv2": 13, "conv3": 13, "gin": 4}[kind]

            def body(k, b, first):
                c = 2 * k + b
                link.at(c * KL)
                v.wait_ge(got[b], 16 * CH * (k + 1))
                v.wait_ge(sgot[b], 16 * (1 + nx) * (k + 1))
                Sc, Mc = S[:, bass.ts(c, CH), :], M[:, bass.ts(c, CH), :]
                if kind == "gin":
                    link.inc(v.tensor_tensor(agg[:, 0:CH, :], Sc, ring[b][:, :, :], ALU.add))
                    link(v.tensor_tensor(agg[:, CH:N2, :], Mc, din[b][:, :, :], ALU.add))
                    v.sem_inc(zin, 1)
                    v.sem_inc(used, 1)
                    v.sem_inc(sread, 1)
                    v.wait_ge(act_eo, c + 1)
                    if not (first and b == 0):
                        v.wait_ge(skept, 16 * c)
                    v.scalar_tensor_tensor(y[:, :, :], psD[:, :].rearrange("p (t f) -> p t f", f=D), 0.01, e[:, :, :],
                                           ALU.mult, ALU.max).then_inc(new, 1)
                else:
                    link.inc(v.tensor_scalar(st[:, 0:CH, :], Sc, 1.0, None, ALU.mult))
                    link(v.tensor_scalar(st[:, CH:N2, :], din[b][:, :, :], 1.0, None, ALU.mult))
                    v.sem_inc(zin, 1)
                    v.wait_ge(done, c + 1)
                    pd = psD[:, :].rearrange("p (t f) -> p t f", f=D)
                    link.inc(v.tensor_tensor(agg[:, 0:CH, :], pd[:, 0:CH, :], ring[b][:, :, :], ALU.add))
                    link(v.tensor_tensor(agg[:, CH:N2, :], pd[:, CH:N2, :], Mc, ALU.add))
                    v.sem_inc(used, 1)
                    v.tensor_scalar(m[:, :, :], agg[:, :, :], 0.0, None, ALU.min).then_inc(act_e, 1)
                    v.wait_ge(act_eo, c + 1)
                    link(v.scalar_tensor_tensor(agg[:, :, :], agg[:, :, :], 0.0, e[:, :, :], ALU.max, ALU.add))
                if kind == "conv2":
                    v.sem_inc(sread, 1)
                    if not (first and b == 0):
                        v.wait_ge(skept, 16 * c)
                    link(v.tensor_scalar(y[:, :, :], agg[:, :, :], -1.0, None, ALU.add))
                    v.sem_inc(new, 1)
                    sp_.vector(v, link, c, y[:, 0:CH, :])
                    v.tensor_scalar(S[:, bass.ts(c, CH), :], y[:, 0:CH, :], 1.0, None, ALU.mult).then_inc(lk, 1)
                    link.n += 1
                elif kind == "conv3":
                    if not (first and b == 0):
                        v.wait_ge(skept, 32 * c)
                    link(v.scalar_tensor_tensor(x3[:, :, :], agg[:, :, :], -1.0, xin[b][:, :, 0:D], ALU.add, ALU.add))
                    v.sem_inc(sread, 1)
                    norm_dve(v, link, act_in, act_out, c + 1, x3[:, :, :], N2, t, y[:, :, :]).then_inc(new, 1)
                if kind != "conv2":
                    v.wait_ge(new, c + 1)
                    v.wait_ge(ea_d, c + 1)
                    v.tensor_tensor(mm[:, :, :], psE[:, 0:256].rearrange("p (t f) -> p t f", f=D), y[:, 0:CH, :], ALU.add).then_inc(mready, 1)
                    v.wait_ge(mready, c + 1)
                    v.tensor_scalar(Mc, mm[:, :, :], 0.0, None, ALU.max).then_inc(lk, 1)
                    link.n += 1
                    link(v.tensor_scalar(Sc, y[:, 0:CH, :], 1.0, None, ALU.mult))
                assert link.n == KL, (ph.name, link.n)
                v.wait_ge(lk, (c + 1) * KL)
            chunks(g, v, body)


def last_edges(g, B, M, out):
    N, W = g.N, g.W
    with Phase(g, "out") as ph:
        s = lambda n: ph.sem(n)
        got, lk, zin, turned, flat, done, relu, made = ph.sem2("got"), s("lk"), s("zin"), s("turned"), s("flat"), s("done"), s("relu"), s("made")
        sent, leaky = ph.sem2("sent"), s("leaky")
        r = ph.sb("r", [P, CH, D])
        din, xin = ph.sb2("din", [P, CH, D]), ph.sb2("xin", [P, CH, D])
        agg, aT, y = ph.sb("agg", [P, CH, D]), ph.sb("aT", [P, 256]), ph.sb("y", [P, CH, D])
        rowr, idxr = ph.sb2("rowr", [P, CH, D]), ph.sb2("idxr", [P, CH], I32)
        psA, psD = ph.ps("psA"), ph.ps("psD")
        block = ph.block()

        @block.sync
        def _(sp):
            def load(k, b, first):
                c = 2 * k + b
                if not first:
                    sp.wait_ge(made, 2 * (c - 1))
                sp.dma_start(din[b][:, :, :], lin(g, g.dst_lin, c)).then_inc(got[b], 16)
                sp.dma_start(xin[b][:, :, :], lin(g, g.x3_lin, c)).then_inc(got[b], 16)
            chunks(g, sp, load)

        @block.gpsimd
        def _(pool):
            def scatter(k, b, first):
                c = 2 * k + b
                pool.wait_ge(made, 2 * c + 2)
                pool.sem_inc(g.hop, 1)
                for j in range(CH):
                    pool.indirect_dma_start(out=out, out_offset=bass.IndirectOffsetOnAxis(ap=idxr[b][:, j:j + 1], axis=0),
                                            in_=rowr[b][:, j, :], in_offset=None, bounds_check=N - 1, oob_is_err=False).then_inc(sent[b], 16)
            chunks(g, pool, scatter)
            both(g, pool, sent, 16 * CH)

        @block.scalar
        def _(act):
            def body(k, b, first):
                c = 2 * k + b
                act.wait_ge(turned, c + 1)
                act.copy(aT[:, :], psA[:, 0:256]).then_inc(flat, 1)
                act.wait_ge(done, c + 1)
                if not (first and b == 0):
                    act.wait_ge(made, 2 * c)
                act.copy(r[:, :, :], psD[:, 0:256].rearrange("p (t f) -> p t f", f=D)).then_inc(relu, 1)
            chunks(g, act, body)

        @block.tensor
        def _(pe):
            def body(k, b, first):
                c = 2 * k + b
                pe.wait_ge(zin, c + 1)
                for q in range(2):
                    ins = pe.transpose(psA[:, q * P:(q + 1) * P], agg[:, 4 * q:4 * q + 4, :].rearrange("p t f -> p (t f)"), g.ident[:, :])
                ins.then_inc(turned, 1)
                pe.wait_ge(flat, c + 1)
                if not (first and b == 0):
                    pe.wait_ge(leaky, c)
                pe.matmul(psD[:, 0:256], g.ones[0:1, :], over(g.bias[:, 7, :], 1, CH), start=True, stop=False, skip_group_check=True)
                for q in range(2):
                    ins = pe.matmul(psD[:, q * P:(q + 1) * P], aT[:, q * P:(q + 1) * P], g.w3[2][:, :], start=False, stop=False, skip_group_check=True)
                ins.then_inc(done, 1)
            chunks(g, pe, body)

        @block.vector
        def _(v):
            def body(k, b, first):
                c = 2 * k + b
                v.wait_ge(got[b], 32 * (k + 1))
                if not (first and b == 0):
                    v.wait_ge(turned, c)
                v.tensor_tensor(agg[:, :, :], M[:, bass.ts(c, CH), :], din[b][:, :, :], ALU.add).then_inc(zin, 1)
                if not first:
                    v.wait_ge(sent[b], 16 * CH * k)
                v.tensor_scalar(idxr[b][:, :], B.out[:, bass.ts(c, CH)], 1.0, None, ALU.mult).then_inc(made, 1)
                v.wait_ge(relu, c + 1)
                v.scalar_tensor_tensor(y[:, :, :], psD[:, 0:256].rearrange("p (t f) -> p t f", f=D), 0.01, r[:, :, :],
                                       ALU.mult, ALU.max).then_inc(leaky, 1)
                v.wait_ge(leaky, c + 1)
                v.tensor_tensor(rowr[b][:, :, :], y[:, :, :], xin[b][:, :, :], ALU.add).then_inc(made, 1)
            chunks(g, v, body)


def all_nodes(g, out):
    BN = 2 * CH
    q = g.NPART
    steps = g.NPER // BN
    NS = 4
    LAST = steps % NS
    ROUNDS = steps // NS
    PE_N, ACT_N, DVE_N = 11, 13, 13
    with Phase(g, "nodes") as ph:
        streams = []
        for i in range(NS):
            st = Names()
            st.got, st.stored, st.by_pe, st.by_act, st.by_dve = (
                ph.sem(f"{n}{i}") for n in ("got", "stored", "by_pe", "by_act", "by_dve"))
            st.x, st.o, st.xc = ph.sb(f"x{i}", [P, BN, D + 1]), ph.sb(f"o{i}", [P, 4 * P]), ph.sb(f"xc{i}", [P, BN, D])
            st.xT, st.hT, st.e, st.r, st.root, st.inv, st.x3 = (
                ph.sb(f"{n}{i}", [P, 4 * P]) for n in ("xT", "hT", "e", "r", "root", "inv", "x3"))
            st.ps, st.ps2 = ph.ps(f"ps{i}"), ph.ps(f"ps2{i}")
            streams.append(st)
        cleared = ph.sem("cleared")
        block = ph.block()
        n2 = g.nodes2.rearrange("(p n) f -> p n f", p=q)
        od = out.rearrange("(p n) f -> p n f", p=q)

        def rounds(eng, body):
            body(0, streams, True)
            with eng.Fori(1, ROUNDS) as k:
                body(k, streams, False)
            body(ROUNDS, streams[0:LAST], False)

        @block.sync
        def _(sp):
            sp.wait_ge(cleared, NS)

            def load(k, i):
                st = streams[i]
                sp.dma_start(st.x[0:q, :, :], n2[:, bass.ts(NS * k + i, BN), :]).then_inc(st.got, 16)

            def store(k, i):
                st = streams[i]
                sp.wait_ge(st.by_act, ACT_N * (k + 1))
                sp.dma_start(od[:, bass.ts(NS * k + i, BN), :],
                             st.o[0:q, :].rearrange("p (t f) -> p t f", f=D)).then_inc(st.stored, 16)

            for i in range(NS):
                load(0, i)
            with sp.Fori(0, ROUNDS - 1) as k:
                for i in range(NS):
                    sp.wait_ge(streams[i].by_dve, DVE_N * k + 1)
                    load(k + 1, i)
                for i in range(NS):
                    store(k, i)
            for i in range(LAST):
                sp.wait_ge(streams[i].by_dve, DVE_N * (ROUNDS - 1) + 1)
                load(ROUNDS, i)
            for i in range(NS):
                store(ROUNDS - 1, i)
            for i in range(LAST):
                store(ROUNDS, i)
            for i in range(NS):
                sp.wait_ge(streams[i].stored, 16 * (ROUNDS + (i < LAST)))

        @block.tensor
        def _(pe):
            def turn(dst, src):
                for j in range(4):
                    ins = pe.transpose(dst[:, j * P:(j + 1) * P], src[:, j * P:(j + 1) * P], g.ident[:, :])
                return ins

            def times(w, src, dst):
                return pe.matmul(dst[:, :], w[:, :], src[:, :], start=True, stop=True)

            def body(k, sts, first):
                A, V = ACT_N * k, DVE_N * k
                for st in sts:
                    pe.wait_ge(st.by_dve, V + 1)
                    turn(st.ps, st.xc[:, :, :].rearrange("p t f -> p (t f)")).then_inc(st.by_pe, 1)
                for st in sts:
                    pe.wait_ge(st.by_act, A + 1)
                    times(g.center, st.xT, st.ps2).then_inc(st.by_pe, 1)
                for st in sts:
                    pe.wait_ge(st.by_act, A + 2)
                    times(g.mean, st.e, st.ps).then_inc(st.by_pe, 1)
                for st in sts:
                    pe.wait_ge(st.by_dve, V + 3)
                    times(g.root[0], st.hT, st.ps).then_inc(st.by_pe, 1)
                for st in sts:
                    pe.wait_ge(st.by_dve, V + 5)
                    times(g.root[1], st.hT, st.ps).then_inc(st.by_pe, 1)
                for st in sts:
                    pe.wait_ge(st.by_dve, V + 7)
                    times(g.center, st.x3, st.ps2).then_inc(st.by_pe, 1)
                for st in sts:
                    pe.wait_ge(st.by_act, A + 8)
                    times(g.mean, st.e, st.ps).then_inc(st.by_pe, 1)
                for l in range(3):
                    for st in sts:
                        pe.wait_ge(st.by_dve, V + 9 + l)
                        times(g.w3[l], st.hT, st.ps).then_inc(st.by_pe, 1)
                for st in sts:
                    pe.wait_ge(st.by_dve, V + 13)
                    turn(st.ps2, st.hT).then_inc(st.by_pe, 1)
            rounds(pe, body)

        @block.scalar
        def _(act):
            def norm(st, pe_at):
                act.wait_ge(st.by_pe, pe_at)
                act.activation(st.e[:, :], st.ps2[:, :], ACT.Square).then_inc(st.by_act, 1)

            def root(st, pe_at):
                act.wait_ge(st.by_pe, pe_at)
                act.activation(st.root[:, :], st.ps[:, :], ACT.Sqrt, bias=g.eps[:, :]).then_inc(st.by_act, 1)

            def body(k, sts, first):
                T = PE_N * k
                for st in sts:
                    act.wait_ge(st.by_pe, T + 1)
                    act.copy(st.xT[:, :], st.ps[:, :]).then_inc(st.by_act, 1)
                for st in sts:
                    norm(st, T + 2)
                for st in sts:
                    root(st, T + 3)
                for i in range(2):
                    for st in sts:
                        act.wait_ge(st.by_pe, T + 4 + i)
                        act.activation(st.e[:, :], st.ps[:, :], ACT.Exp, bias=g.bcols[:, i:i + 1]).then_inc(st.by_act, 1)
                        act.activation(st.r[:, :], st.ps[:, :], ACT.Relu, bias=g.bcols[:, i:i + 1]).then_inc(st.by_act, 1)
                for st in sts:
                    norm(st, T + 6)
                for st in sts:
                    root(st, T + 7)
                for l in range(3):
                    for st in sts:
                        act.wait_ge(st.by_pe, T + 8 + l)
                        act.activation(st.r[:, :], st.ps[:, :], ACT.Identity, bias=g.bcols[:, 2 + l:3 + l]).then_inc(st.by_act, 1)
                for st in sts:
                    if not first:
                        act.wait_ge(st.stored, 16 * k)
                        act.sem_inc(g.hop, 1)
                    act.wait_ge(st.by_pe, T + 11)
                    act.copy(st.o[:, :], st.ps2[:, :]).then_inc(st.by_act, 1)
            rounds(act, body)

        @block.vector
        def _(v):
            def norm(sts, A, V):
                for st in sts:
                    v.wait_ge(st.by_act, A)
                    v.reciprocal(st.inv[:, :], st.root[:, :]).then_inc(st.by_dve, 1)
                for st in sts:
                    v.wait_ge(st.by_dve, V)
                    v.scalar_tensor_tensor(st.hT[:, :], st.ps2[:, :], 0.0, st.inv[:, :], ALU.max, ALU.mult).then_inc(st.by_dve, 1)

            for st in streams:
                v.memset(st.x[:, :, :], 0.0).then_inc(cleared, 1)

            def body(k, sts, first):
                A, V = ACT_N * k, DVE_N * k
                for st in sts:
                    v.wait_ge(st.got, 16 * (k + 1))
                    v.tensor_scalar(st.xc[:, :, :], st.x[:, :, 0:D], 1.0, None, ALU.mult).then_inc(st.by_dve, 1)
                norm(sts, A + 3, V + 2)
                for st in sts:
                    v.wait_ge(st.by_act, A + 5)
                    v.scalar_tensor_tensor(st.hT[:, :], st.e[:, :], 1.0, st.r[:, :], ALU.min, ALU.add).then_inc(st.by_dve, 1)
                    v.wait_ge(st.by_dve, V + 4)
                    v.tensor_scalar(st.hT[:, :], st.hT[:, :], -1.0, None, ALU.add).then_inc(st.by_dve, 1)
                for st in sts:
                    v.wait_ge(st.by_act, A + 7)
                    v.scalar_tensor_tensor(st.hT[:, :], st.e[:, :], 1.0, st.r[:, :], ALU.min, ALU.add).then_inc(st.by_dve, 1)
                    v.wait_ge(st.by_dve, V + 6)
                    v.scalar_tensor_tensor(st.x3[:, :], st.hT[:, :], -1.0, st.xT[:, :], ALU.add, ALU.add).then_inc(st.by_dve, 1)
                norm(sts, A + 9, V + 8)
                for l in range(3):
                    for st in sts:
                        v.wait_ge(st.by_act, A + 10 + l)
                        v.scalar_tensor_tensor(st.hT[:, :], st.r[:, :], 0.01, st.r[:, :], ALU.mult, ALU.max).then_inc(st.by_dve, 1)
                for st in sts:
                    v.wait_ge(st.by_dve, V + 12)
                    v.tensor_tensor(st.hT[:, :], st.hT[:, :], st.x3[:, :], ALU.add).then_inc(st.by_dve, 1)
            rounds(v, body)


def build(nc, a, out):
    E, N = a["src"].shape[0], a["x"].shape[0]
    g = Names()
    g.nc, g.E, g.N = nc, E, N
    g.W = -(-E // (P * CH)) * CH
    g.NP = P * g.W
    g.NCH = g.W // CH
    g.FULL, g.REST = E // g.W, E % g.W
    g.R0 = 256
    g.R1 = (N >> 8) + 2
    g.PADKEY = (g.R1 - 1) << 8
    g.CB, g.CA = 13, 2
    g.NPART = 125
    g.NPER = N // g.NPART
    assert g.NCH % 2 == 1 and g.NPER * g.NPART == N
    with ExitStack() as ctx:
        sb = lambda n, s, d=F32, c=ctx: c.enter_context(nc.sbuf_tensor(n, s, d))
        dram = lambda n, s, d=F32: nc.dram_tensor(n, s, d, kind="Internal").ap()
        g.hop = ctx.enter_context(nc.semaphore("hop"))
        g.b_mid, g.b_tab = dram("b_mid", [g.NP, g.CB]), dram("b_tab", [g.NP + 2, g.CB])
        g.a_mid, g.a_tab = dram("a_mid", [g.NP, g.CA]), dram("a_tab", [g.NP + 2, g.CA])
        g.nodes1, g.nodes2 = dram("nodes1", [N, D + 2]), dram("nodes2", [N, D + 1])
        g.xd_lin, g.xs_lin = dram("xd_lin", [g.NP, D + 2]), dram("xs_lin", [g.NP, D + 2])
        g.x1_lin = dram("x1_lin", [g.NP, D])
        g.x2s_lin, g.x2d_lin = dram("x2s_lin", [g.NP, D + 1]), dram("x2d_lin", [g.NP, D + 1])
        g.dst_lin, g.x3_lin = dram("dst_lin", [g.NP, D]), dram("x3_lin", [g.NP, D])
        g.tabs = [dram(f"tab{i}", [g.NP + 1, D]) for i in range(2)]
        g.agg_tab = dram("agg_tab", [g.NP + 1, D])

        g.iota16 = sb("iota16", [P, g.R1], F16)
        g.ident = sb("ident", [P, P])
        g.before, g.notbefore, g.ones16 = (sb(n, [P, P], F16) for n in ("before", "notbefore", "ones16"))
        g.ones = sb("ones", [P, P])
        g.zeros = sb("zeros", [P, g.R1])
        g.zerow = g.zeros[:, 0:g.W]
        assert g.R1 >= g.W
        g.starts = sb("starts", [P, g.R1 + 1])
        g.eps = sb("eps", [P, 1])
        g.beta = sb("beta", [P, 1])
        g.alone = sb("alone", [P, D])
        g.w0a, g.w0b = sb("w0a", [P, 2 * P]), sb("w0b", [P, 2 * D])
        g.w1s, g.w1d, g.w2 = (sb(n, [P, P]) for n in ("w1s", "w1d", "w2"))
        g.root = [sb(f"root{i}", [P, P]) for i in range(2)]
        g.w3 = [sb(f"w3_{i}", [P, P]) for i in range(3)]
        g.we = [sb(f"we{i}", [64, 256]) for i in range(3)]
        g.bias = sb("bias", [1, 11, D])
        g.bn = sb("bn", [P, 4, D])
        g.b0col = sb("b0col", [P, 1])
        g.bcols = sb("bcols", [P, 5])
        g.mean, g.center = sb("mean", [P, P]), sb("center", [P, P])
        g.spline = [sb(f"spline{i}", [3 * D, 9, D]) for i in range(2)]
        g.rows_b = sb("rows_b", [P, g.W, g.CB])

        def flags(n, column, c=ctx):
            f = Names()
            f.column = column
            f.same, f.last, f.pfx = (sb(f"{n}_{k}", [P, g.W], F32, c) for k in ("same", "last", "pfx"))
            f.other, f.own, f.out = (sb(f"{n}_{k}", [P, g.W], I32, c) for k in ("other", "own", "out"))
            return f
        B = flags("b", 1)
        with ExitStack() as c1:
            g.rows_a = sb("rows_a", [P, g.W, g.CA], F32, c1)
            A = flags("a", 0, c1)
            load_weights(g, a)
            first_rows(g, a)
            first_count(g, g.rows_b, node_table_filler(g, a))
            sort_pass(g, "sort_b0", g.rows_b, g.CB, 0, g.b_mid, g.rows_b, 1)
            sort_pass(g, "sort_b1", g.rows_b, g.CB, 1, g.b_tab, g.rows_a, 0)
            sort_pass(g, "sort_a0", g.rows_a, g.CA, 0, g.a_mid, g.rows_a, 1)
            sort_pass(g, "sort_a1", g.rows_a, g.CA, 1, g.a_tab, None, 0)
            places(g, "b", g.rows_b, g.b_tab, B)
            places(g, "a", g.rows_a, g.a_tab, A)
            QA = sb("QA", [P, g.W], I32, c1)
            PB = sb("PB", [P, g.W], F32, c1)
            H = sb("H", [P, g.W, D], F32, c1)
            layer0_edges(g, A, H, QA)
            fill_back(g, A, H)
            Z = sb("Z", [P, g.W, D], F32, c1)
            layer01_edges(g, A, H, QA, Z, PB)
            layer1_rest(g, A, H, Z, PB)
        all_nodes(g, out)
        WT = sb("WT", [P, g.W, 9])
        QB = sb("QB", [P, g.W], I32)
        spline_weights(g, WT)
        inv = sb("inv", [P, g.W, 1])
        M = sb("M", [P, g.W, D])
        S = sb("S", [P, g.W, D])
        conv1_edges(g, B, WT, M, S, QB)
        close_segments(g, B, M, g.tabs[0], "s1", count=inv, scale=inv)
        next_edges(g, B, WT, M, S, QB, g.tabs[0], "conv2", 0, "c2")
        close_segments(g, B, M, g.tabs[1], "s2", scale=inv)
        next_edges(g, B, WT, M, S, QB, g.tabs[1], "conv3", 0, "c3")
        close_segments(g, B, M, g.tabs[0], "s3")
        next_edges(g, B, WT, M, S, QB, g.tabs[0], "gin", 0, "g0")
        close_segments(g, B, M, g.tabs[1], "s4")
        next_edges(g, B, WT, M, S, QB, g.tabs[1], "gin", 1, "g1")
        close_segments(g, B, M, g.tabs[0], "s5")
        last_edges(g, B, M, out)


_INS = ['x', 'src', 'dst', 'edge_attr_3', 'edge_attr_8', 'L0_gnn_beta', 'L0_gnn_W1', 'L0_gnn_b1', 'L0_gnn_W2', 'L0_gnn_b2', 'L1_gnn_W1', 'L1_gnn_b1', 'L1_gnn_gamma1', 'L1_gnn_beta1', 'L1_gnn_W2', 'L1_gnn_b2', 'L1_gnn_gamma2', 'L1_gnn_beta2', 'L2_gnn_w1', 'L2_gnn_root1', 'L2_gnn_b1', 'L2_gnn_w2', 'L2_gnn_root2', 'L2_gnn_b2', 'L3_gnn_W', 'L3_gnn_b', 'L3_gnn_We', 'L3_gnn_be']
_OUTS = [((100000, 32), 'float32')]


def kernel(**inputs):
    import numpy as _np
    import concourse.bacc as _bacc
    from concourse import mybir as _mybir
    from concourse.bass_utils import run_bass_kernel_spmd as _run
    nc = _bacc.Bacc("TRN2", target_bir_lowering=False, num_devices=1)
    arrays, args = {}, {}
    for name in _INS:
        v = _np.ascontiguousarray(inputs[name])
        arrays[f"in_{name}_dram"] = v
        args[name] = nc.dram_tensor(f"in_{name}_dram", v.shape, _mybir.dt.from_np(v.dtype), kind="ExternalInput").ap()
    outs = []
    for i, (shape, dtype) in enumerate(_OUTS):
        dt = _mybir.dt.from_np(_np.dtype(dtype))
        outs.append(nc.dram_tensor(f"out_{i}_dram", shape, dt, kind="ExternalOutput").ap())
    build(nc, args, *outs)
    r = _run(nc, [arrays], core_ids=[0])
    return r.results[0]["out_0_dram"]
```
